# Optimizing a Trainium2 kernel written in Bass

```python
import numpy as np
import jax
import jax.numpy as jnp

def _softmax(x, axis=-1):
    return jax.nn.softmax(x, axis=axis)

def _gelu(x):
    return jax.nn.gelu(x, approximate=True)

def _silu(x):
    return jax.nn.silu(x)

def _sigmoid(x):
    return jax.nn.sigmoid(x)

def _layernorm(x, axis=-1, eps=1e-05):
    m = jnp.mean(x, axis=axis, keepdims=True)
    v = jnp.var(x, axis=axis, keepdims=True)
    return (x - m) / jnp.sqrt(v + eps)

def _scatter_add(tgt, idx, src, axis=0):
    return tgt.at[idx].add(src)

def _segment_sum(src, seg, n):
    return jax.ops.segment_sum(src, seg, n)
kernel_name = 'mk_flamingo_gated_d1_seqx_r4_484079'

def setup_inputs(seed: int=0):
    np.random.seed(seed)
    _w = jnp.asarray

    def _rec_inputs():
        import jax
        import jax.numpy as jnp
        _rk = jax.random.key(seed)
        x = -0.0002928 + 1 * jax.random.normal(jax.random.fold_in(_rk, 1), (16, 112, 256), jnp.float32)
        _lenS = 112 - jax.random.randint(jax.random.fold_in(_rk, 7), (16,), 0, max(1, 112 // 4) + 1, jnp.int32)
        _lenS2 = 375 - jax.random.randint(jax.random.fold_in(_rk, 8), (16,), 0, max(1, 375 // 4) + 1, jnp.int32)
        _ctx_1024P = jax.random.normal(jax.random.fold_in(_rk, 11), (16, 16, 256), jnp.float32)
        _ctx_1024c = jax.random.dirichlet(jax.random.fold_in(_rk, 511), 0.3 * jnp.ones((16,), jnp.float32), (16, 375))
        _ctx_1024t = jnp.einsum('bsk,bkd->bsd', _ctx_1024c, _ctx_1024P)
        _ctx_1024t = _ctx_1024t * jax.lax.rsqrt(jnp.mean(jnp.square(_ctx_1024t)) + 1e-12) * 0.953939
        ctx_1024 = -1.39393e-06 + 0.999914 * (_ctx_1024t + 0.3 * jax.random.normal(jax.random.fold_in(_rk, 611), (16, 375, 256), jnp.float32))
        fside_BxSxS2_0 = jax.random.uniform(jax.random.fold_in(_rk, 12), (16, 112, 375), jnp.float32, 0.0, 1)
        _validS = jnp.arange(112)[None, :] < _lenS[:, None]
        _validS2 = jnp.arange(375)[None, :] < _lenS2[:, None]
        _causal = jnp.tril(jnp.ones((112, 112), dtype=bool))
        mask_BxSxS2_ik1 = jnp.where(jnp.broadcast_to(_validS2[:, None, :], (16, 112, 375)), 1, 0).astype(jnp.int32)
        _g = jax.random.normal(jax.random.fold_in(_rk, 9001), (2, 1), jnp.float32)
        _g = jnp.sign(_g) * jnp.maximum(jnp.abs(_g), 1.0) + (_g == 0) * 1.0
        g_xattn = _g[0]
        g_ffn = _g[1]
        return (x, ctx_1024, fside_BxSxS2_0, mask_BxSxS2_ik1, g_xattn, g_ffn)
    x, ctx_1024, fside_BxSxS2_0, mask_BxSxS2_ik1, g_xattn, g_ffn = _rec_inputs()

    def _L0_xattn_setup():
        import jax, jax.numpy as jnp
        import numpy as np
        NUM_HEADS = 16
        HIDDEN = 256
        B, S = (2, 512)

        def _split_heads(x, H):
            b, s, d = x.shape
            return x.reshape(b, s, H, d // H).transpose(0, 2, 1, 3)
        key = jax.random.key(seed)
        ks = jax.random.split(key, 14)
        D = HIDDEN
        scale = 1.0 / np.sqrt(D)
        inp = {'query': jax.random.normal(ks[0], (B, S, D), jnp.float32), 'key_in': jax.random.normal(ks[1], (B, S, D), jnp.float32), 'value': jax.random.normal(ks[2], (B, S, D), jnp.float32), 'group_prob': jax.random.uniform(ks[3], (B, S, S), jnp.float32), 'mask': jax.random.randint(ks[4], (B, S, S), 0, 2, jnp.int32), 'wq_k': jax.random.normal(ks[5], (D, D), jnp.float32) * scale, 'wq_b': jnp.zeros((D,), jnp.float32), 'wk_k': jax.random.normal(ks[6], (D, D), jnp.float32) * scale, 'wk_b': jnp.zeros((D,), jnp.float32), 'wv_k': jax.random.normal(ks[7], (D, D), jnp.float32) * scale, 'wv_b': jnp.zeros((D,), jnp.float32), 'wo_k': jax.random.normal(ks[8], (D, D), jnp.float32) * scale, 'wo_b': jnp.zeros((D,), jnp.float32)}
        return inp
    _L0_xattn_all = _L0_xattn_setup()
    _L0_xattn_in = {k: v for k, v in _L0_xattn_all.items() if k in ('wq_k', 'wq_b', 'wk_k', 'wk_b', 'wv_k', 'wv_b', 'wo_k', 'wo_b')}
    del _L0_xattn_all

    def _L0_ffn_setup():
        import jax, jax.numpy as jnp
        import numpy as np
        D, H, O, E, TOPK = (256, 1024, 256, 8, 2)
        B, S = (4, 256)
        key = jax.random.key(seed)
        ks = jax.random.split(key, 12)
        std = 0.02
        return {'hidden_states': jax.random.normal(ks[0], (B, S, D), dtype=jnp.float32), 'norm_weight': jnp.ones((D,), dtype=jnp.float32), 'router_w': jax.random.normal(ks[1], (E, D), dtype=jnp.float32) * std, 'sw1': jax.random.normal(ks[2], (D, H), dtype=jnp.float32) * (1.0 / np.sqrt(D)), 'sb1': jnp.zeros((H,), dtype=jnp.float32), 'sw2': jax.random.normal(ks[3], (H, O), dtype=jnp.float32) * (1.0 / np.sqrt(H)), 'sb2': jnp.zeros((O,), dtype=jnp.float32), 'ew1': jax.random.normal(ks[4], (E, D, H), dtype=jnp.float32) * (1.0 / np.sqrt(D)), 'eb1': jnp.zeros((E, H), dtype=jnp.float32), 'ew2': jax.random.normal(ks[5], (E, H, O), dtype=jnp.float32) * (1.0 / np.sqrt(H)), 'eb2': jnp.zeros((E, O), dtype=jnp.float32)}
    _L0_ffn_all = _L0_ffn_setup()
    _L0_ffn_in = {k: v for k, v in _L0_ffn_all.items() if k in ('norm_weight', 'router_w', 'sw1', 'sb1', 'sw2', 'sb2', 'ew1', 'eb1', 'ew2', 'eb2')}
    del _L0_ffn_all
    return {'x': x, 'ctx_1024': ctx_1024, 'fside_BxSxS2_0': fside_BxSxS2_0, 'mask_BxSxS2_ik1': mask_BxSxS2_ik1, 'g_xattn': g_xattn, 'g_ffn': g_ffn, 'L0_xattn_wq_k': _L0_xattn_in['wq_k'], 'L0_xattn_wq_b': _L0_xattn_in['wq_b'], 'L0_xattn_wk_k': _L0_xattn_in['wk_k'], 'L0_xattn_wk_b': _L0_xattn_in['wk_b'], 'L0_xattn_wv_k': _L0_xattn_in['wv_k'], 'L0_xattn_wv_b': _L0_xattn_in['wv_b'], 'L0_xattn_wo_k': _L0_xattn_in['wo_k'], 'L0_xattn_wo_b': _L0_xattn_in['wo_b'], 'L0_ffn_norm_weight': _L0_ffn_in['norm_weight'], 'L0_ffn_router_w': _L0_ffn_in['router_w'], 'L0_ffn_sw1': _L0_ffn_in['sw1'], 'L0_ffn_sb1': _L0_ffn_in['sb1'], 'L0_ffn_sw2': _L0_ffn_in['sw2'], 'L0_ffn_sb2': _L0_ffn_in['sb2'], 'L0_ffn_ew1': _L0_ffn_in['ew1'], 'L0_ffn_eb1': _L0_ffn_in['eb1'], 'L0_ffn_ew2': _L0_ffn_in['ew2'], 'L0_ffn_eb2': _L0_ffn_in['eb2']}

def reference(x, ctx_1024, fside_BxSxS2_0, mask_BxSxS2_ik1, g_xattn, g_ffn, L0_xattn_wq_k, L0_xattn_wq_b, L0_xattn_wk_k, L0_xattn_wk_b, L0_xattn_wv_k, L0_xattn_wv_b, L0_xattn_wo_k, L0_xattn_wo_b, L0_ffn_norm_weight, L0_ffn_router_w, L0_ffn_sw1, L0_ffn_sb1, L0_ffn_sw2, L0_ffn_sb2, L0_ffn_ew1, L0_ffn_eb1, L0_ffn_ew2, L0_ffn_eb2):
    import jax
    import jax.numpy as jnp

    def _L0_xattn_ref(query, key_in, value, group_prob, mask, wq_k, wq_b, wk_k, wk_b, wv_k, wv_b, wo_k, wo_b):
        import jax, jax.numpy as jnp
        import numpy as np
        NUM_HEADS = 16
        HIDDEN = 256
        B, S = (2, 512)

        def _split_heads(x, H):
            b, s, d = x.shape
            return x.reshape(b, s, H, d // H).transpose(0, 2, 1, 3)
        H = NUM_HEADS
        dh = query.shape[-1] // H
        q = _split_heads(query @ wq_k + wq_b, H)
        k = _split_heads(key_in @ wk_k + wk_b, H)
        v = _split_heads(value @ wv_k + wv_b, H)
        logits = jnp.einsum('bhqd,bhkd->bhqk', q, k) / jnp.sqrt(jnp.asarray(dh, q.dtype))
        neg = (1.0 - mask.astype(q.dtype)) * -1000000000.0
        logits = logits + neg[:, None, :, :]
        attn = jax.nn.softmax(logits, axis=-1)
        attn = attn * group_prob[:, None, :, :]
        out = jnp.einsum('bhqk,bhkd->bhqd', attn, v)
        out = out.transpose(0, 2, 1, 3).reshape(query.shape[0], -1, H * dh)
        return out @ wo_k + wo_b

    def _L0_ffn_ref(hidden_states, norm_weight, router_w, sw1, sb1, sw2, sb2, ew1, eb1, ew2, eb2):
        import jax, jax.numpy as jnp
        import numpy as np
        D, H, O, E, TOPK = (256, 1024, 256, 8, 2)
        B, S = (4, 256)
        b, s, d = hidden_states.shape
        var = jnp.mean(jnp.square(hidden_states), axis=-1, keepdims=True)
        normed = hidden_states * jax.lax.rsqrt(var + 1e-08) * norm_weight
        shared = jnp.maximum(normed @ sw1 + sb1, 0.0) @ sw2 + sb2
        flat = normed.reshape(-1, d)
        T = flat.shape[0]
        probs = jax.nn.sigmoid(flat @ router_w.T)
        scores, idx = jax.lax.top_k(probs, TOPK)
        w = scores / (jnp.sum(scores, axis=-1, keepdims=True) + 1e-06)
        comb = jnp.zeros((T, E), dtype=flat.dtype)
        comb = comb.at[jnp.arange(T)[:, None], idx].add(w)
        h = jnp.maximum(jnp.einsum('td,edh->teh', flat, ew1) + eb1[None, :, :], 0.0)
        eo = jnp.einsum('teh,eho->teo', h, ew2) + eb2[None, :, :]
        routed = jnp.einsum('teo,te->to', eo, comb)
        return shared + routed.reshape(b, s, -1)
    x = x + jnp.tanh(g_xattn[0]) * _L0_xattn_ref(_layernorm(x, axis=-1), ctx_1024, ctx_1024, fside_BxSxS2_0, mask_BxSxS2_ik1, L0_xattn_wq_k, L0_xattn_wq_b, L0_xattn_wk_k, L0_xattn_wk_b, L0_xattn_wv_k, L0_xattn_wv_b, L0_xattn_wo_k, L0_xattn_wo_b)
    x = x + jnp.tanh(g_ffn[0]) * _L0_ffn_ref(_layernorm(x, axis=-1), L0_ffn_norm_weight, L0_ffn_router_w, L0_ffn_sw1, L0_ffn_sb1, L0_ffn_sw2, L0_ffn_sb2, L0_ffn_ew1, L0_ffn_eb1, L0_ffn_ew2, L0_ffn_eb2)
    return x

_drawn_inputs = setup_inputs


def setup_inputs(seed=0):
    import zlib

    import numpy as np

    out = dict(_drawn_inputs(seed))
    spreads = {'L0_xattn_wq_b': (0.0, 0.1),
     'L0_xattn_wk_b': (0.0, 0.1),
     'L0_xattn_wv_b': (0.0, 0.1),
     'L0_xattn_wo_b': (0.0, 0.1),
     'L0_ffn_norm_weight': (1.0, 0.2),
     'L0_ffn_sb1': (0.0, 0.1),
     'L0_ffn_sb2': (0.0, 0.1),
     'L0_ffn_eb1': (0.0, 0.1),
     'L0_ffn_eb2': (0.0, 0.1)}
    factors = {}
    for name, (base, spread) in spreads.items():
        noise = np.random.default_rng([zlib.crc32(name.encode()), seed]).standard_normal(out[name].shape)
        drawn = base * np.exp(spread * noise) if base else spread * noise
        out[name] = jnp.asarray(drawn.astype(out[name].dtype))
    for name, factor in factors.items():
        out[name] = (out[name] * factor).astype(out[name].dtype)
    return out
```

```python
from contextlib import ExitStack

import concourse.bass as bass
from concourse import mybir

F32, F16, I32 = mybir.dt.float32, mybir.dt.float16, mybir.dt.int32
ALU = mybir.AluOpType
ACT = mybir.ActivationFunctionType
AX = mybir.AxisListType

P = 128
B, S, D = 16, 112, 256
S2, H = 375, 16
DH = D // H
T = B * S
NT = T // P
KC = 3
KP = S2 // KC
ND = D // P
E, F = 8, 1024
NF = F // P
TILE = 256
ST = T // TILE
RT = (2 * T + E * (TILE - 1)) // TILE
ROWS = (ST + RT + 2) * TILE
ZEROS = RT + 2 + RT - E
HI, LO = 0, 1
PASSES = ((HI, HI), (HI, LO), (LO, HI))
SLOT = 64
STACK = 3 * DH
Q_PARTS, K_PARTS = (HI, LO, HI), (HI, HI, LO)
LN_EPS, RMS_EPS = 1e-5, 1e-8
BIG = 3.0e38


def flamingo_block(nc, x, ctx, gp, mask, g_xattn, g_ffn, wq, bq, wk, bk, wv, bv, wo, bo, nw, router,
                   sw1, sb1, sw2, sb2, ew1, eb1, ew2, eb2, out):
    x_rows = x.rearrange("b s d -> (b s) d")
    out_rows = out.rearrange("b s d -> (b s) d")
    k_scratch = nc.dram_tensor("k_scratch", (B, 2, D, S2), F16, kind="Internal").ap()
    q_scratch = nc.dram_tensor("q_scratch", (2, D, T), F16, kind="Internal").ap()
    x_sent = nc.dram_tensor("x_sent", (ROWS, 2 * D), F16, kind="Internal").ap()
    y_sent = nc.dram_tensor("y_sent", ((ST + RT) * TILE, D), F32, kind="Internal").ap()

    with ExitStack() as st:
        def sb(name, shape, dt):
            return st.enter_context(nc.sbuf_tensor(name, shape, dt))

        def sem(name):
            return st.enter_context(nc.semaphore(name))

        x_sb = sb("x_sb", [P, NT, D], F32)
        xnT = sb("xnT", [P, 2, ND, T], F16)
        oT = xnT
        qT = sb("qT", [P, 2, ND, T], F16)
        xpair = qT[:, :, :, :].rearrange("p a b t -> p (a b t)").rearrange("p (i c) -> p i c", i=NT)
        arena = sb("arena", [P, H // 2 * T // 2], F32)
        q_stack = arena[:, :].bitcast(F16).rearrange("p (j t) -> p j t", j=H // 2)
        hid32 = arena[:, 0:NF * TILE].rearrange("p (f n) -> p f n", f=NF)
        hid = arena[:, NF * TILE:2 * NF * TILE].bitcast(F16).rearrange("p (a f n) -> p a f n", a=2, f=NF)
        back = arena[:, 2 * NF * TILE:2 * NF * TILE + 6 * D].rearrange("p (a c d) -> p a c d", a=2, c=3)
        qb = sb("qb", [P, 2, H // 2, S], F16)
        kst = sb("kst", [P, 2, H // 2, S2], F16)
        kT = sb("kT", [P, 2, ND, S2], F16)
        ctx_in = sb("ctx_in", [KP, 2, KC, D], F32)
        ctxT = sb("ctxT", [P, 2, ND, S2], F16)
        mask_in = sb("mask_in", [S, 2, S2], I32)
        neg = sb("neg", [S, 2, S2], F32)
        gp_in = sb("gp_in", [S, 2, S2], F32)
        gpT = sb("gpT", [KP, 2, KC, S], F32)
        v_sb = sb("v_sb", [KP, 2, KC, D], F32)
        probs = sb("probs", [S, 4, S2], F32)
        probsT = sb("probsT", [KP, 2, KC, S], F32)
        negmax = sb("negmax", [S, 2, H], F32)
        rowsum = sb("rowsum", [S, 2, H], F32)
        rrow = sb("rrow", [S, H], F32)
        o_n = sb("o_n", [S, D], F32)
        wpair = sb("wpair", [P, 4, 2, ND, D], F16)
        bcol_in = sb("bcol_in", [4, P], F32)
        bcol = sb("bcol", [P, 4], F32)
        bv_in = sb("bv_in", [1, D], F32)
        bv_pair = sb("bv_pair", [1, 2, D], F16)
        bo_bc = sb("bo_bc", [P, D], F32)
        nw_bc = sb("nw_bc", [P, D], F32)
        b1 = sb("b1", [P, NF, E + 1], F32)
        b2_bc = sb("b2_bc", [P, 2, D], F32)
        r_in = sb("r_in", [E, D], F32)
        rT = sb("rT", [P, 2, ND, E], F16)
        gates = sb("gates", [P, 2], F32)
        ident = sb("ident", [P, P], F32)
        ident16 = sb("ident16", [P, P], F16)
        tri = sb("tri", [P, P], F16)
        ones16 = sb("ones16", [P, P], F16)
        stats = sb("stats", [P, NT, 6], F32)
        mv = sb("mv", [P, NT, 2], F32)
        nrm = sb("nrm", [P, 8, NT], F32)
        xn = sb("xn", [P, 2, D], F32)
        xrT = sb("xrT", [P, 2, 2 * ND, P], F16)
        logit = sb("logit", [P, NT, E], F32)
        rt = sb("rt", [P, 6, NT, E], F32)
        top = sb("top", [P, 10, NT], F32)
        count16 = sb("count16", [P, 3, NT, E], F16)
        est = sb("est", [P, 6, E + 2], F32)
        est_i = sb("est_i", [P, 2, E + 2], I32)
        tile_of = sb("tile_of", [P, E + 2], I32)
        slots = sb("slots", [P, 2, NT], I32)
        w1s = sb("w1s", [P, ND, F], F32)
        w2s = sb("w2s", [P, NF, D], F32)
        wstage = w2s[:, :, :].rearrange("p (n c) d -> p n c d", n=4)
        b1_in = w1s[0:E + 1, 0]
        w1 = sb("w1", [P, 2, 2, ND, F], F16)
        w2 = sb("w2", [P, 2, 2, NF, D], F16)
        xin = sb("xin", [P, TILE // P, 2 * D], F16)
        xT = sb("xT", [P, 2 * ND, TILE], F16)
        y_sb = sb("y_sb", [P, TILE // P, D], F32)
        zero = y_sb[:, :, :].rearrange("p a d -> p (a d)").bitcast(F16)

        ps = st.enter_context(nc.psum_tensor("ps", [P, 8, 512], F32))
        SC, PT, OB, PR = (0, 1), (2, 3), (4, 5), (6, 7)

        in_x, in_w, in_small = sem("in_x"), sem("in_w"), sem("in_small")
        in_ctx = [sem(f"in_ctx{p}") for p in range(2)]
        in_mask = [sem(f"in_mask{p}") for p in range(2)]
        in_gp = [sem(f"in_gp{p}") for p in range(2)]
        consts = sem("consts")
        dve_step, act_step = sem("dve_step"), sem("act_step")
        dve_ask, act_ask, act_gave = sem("dve_ask"), sem("act_ask"), sem("act_gave")
        w_hi, w_lo = sem("w_hi"), sem("w_lo")
        small_T, small_out = sem("small_T"), sem("small_out")
        xn_made, xn_T, xn_hi, xn_lo = sem("xn_made"), sem("xn_T"), sem("xn_hi"), sem("xn_lo")
        q_mm, q_hi, q_lo, q_out, q_in = sem("q_mm"), sem("q_hi"), sem("q_lo"), sem("q_out"), sem("q_in")
        resid = sem("resid")
        neg_made, qb_made = sem("neg_made"), sem("qb_made")
        prep_mm, prep_act, prep_lo = sem("prep_mm"), sem("prep_act"), sem("prep_lo")
        k_out = sem("k_out")
        k_in = [sem(f"k_in{p}") for p in range(2)]
        sc_made, sc_read, exp_made = sem("sc_made"), sem("sc_read"), sem("exp_made")
        pt_made, pt_read, av_made = sem("pt_made"), sem("pt_read"), sem("av_made")
        o_read, rr_made, oT_mm, oT_hi, oT_lo = sem("o_read"), sem("rr_made"), sem("oT_mm"), sem("oT_hi"), sem("oT_lo")
        pj_mm, x2_made = sem("pj_mm"), sem("x2_made")
        n2a, n2_made, n2_hi, n2_lo = sem("n2a"), sem("n2_made"), sem("n2_hi"), sem("n2_lo")
        n2_T, n2_Ts, rl_mm = sem("n2_T"), sem("n2_Ts"), sem("rl_mm")
        sent, zeroed, z_done = sem("sent"), sem("zeroed"), sem("z_done")
        cnt_made, rank_mm, slot_made, tiles_made, scattered = (
            sem("cnt_made"), sem("rank_mm"), sem("slot_made"), sem("tiles_made"), sem("scattered"))
        in_w1, in_w2 = sem("in_w1"), sem("in_w2")
        in_b2 = [sem(f"in_b2{p}") for p in range(2)]
        split_made = sem("split_made")
        x_in = sem("x_in")
        xT_mm, xT_made = sem("xT_mm"), sem("xT_made")
        h_mm, h_relu, h_hi, h_split = sem("h_mm"), sem("h_relu"), sem("h_hi"), sem("h_split")
        y_mm, y_made, y_out = sem("y_mm"), sem("y_made"), sem("y_out")
        back_in = [sem(f"back_in{p}") for p in range(2)]
        mixed, out_done = sem("mixed"), sem("out_done")

        block = st.enter_context(nc.Block())

        SC_FREE, PROBS_FREE, PT_FREE, AT_FREE, O_FREE, OT_FREE, Y_FREE = 2, 4, 2, 2, 2, 1, 16

        def bank(n, rows, cols):
            return ps[0:rows, n, 0:cols]

        @block.sync
        def _(sp):
            sp.dma_start(x_sb[:, :, :], x_rows.rearrange("(i p) d -> p i d", p=P)).then_inc(in_x, 16)
            for n, w in enumerate((wq, wk, wv, wo)):
                sp.dma_start(wstage[:, n], w.rearrange("(c p) n -> p c n", p=P)).then_inc(in_w, 16)
            smalls = [(bcol_in[0:2, :], bq.rearrange("(c p) -> c p", p=P)),
                      (bcol_in[2:4, :], bk.rearrange("(c p) -> c p", p=P)),
                      (bv_in[:, :], bv.rearrange("(a n) -> a n", a=1)),
                      (bo_bc[:, :], bo.partition_broadcast(P)),
                      (nw_bc[:, :], nw.partition_broadcast(P)),
                      (b1_in[0:E], eb1), (b1_in[E:E + 1], sb1.rearrange("(a n) -> a n", a=1)),
                      (r_in[:, :], router),
                      (gates[:, 0:1], g_xattn.partition_broadcast(P)),
                      (gates[:, 1:2], g_ffn.partition_broadcast(P))]
            for to, of in smalls:
                sp.dma_start(to, of).then_inc(in_small, 16)

            def load_batch(b, p):
                sp.dma_start(ctx_in[:, p], ctx[bass.ds(b, 1)].rearrange("a (c p) d -> p (a c) d", p=KP)).then_inc(in_ctx[p], 16)
                sp.dma_start(mask_in[:, p], mask[bass.ds(b, 1)].rearrange("a q k -> q (a k)")).then_inc(in_mask[p], 16)
                sp.dma_start(gp_in[:, p], gp[bass.ds(b, 1)].rearrange("a q k -> q (a k)")).then_inc(in_gp[p], 16)

            def restack_keys(b, p):
                sp.wait_ge(prep_act, 7 * b + 4)
                sp.wait_ge(prep_lo, 4 * b + 4)
                for c in range(2):
                    sp.dma_start(k_scratch[bass.ds(b, 1), c].rearrange("a (m p) k -> p (a m) k", p=P),
                                 kT[:, c]).then_inc(k_out, 16)
                sp.wait_ge(k_out, 32 * b + 32)
                for par in range(2):
                    for n, c in enumerate(K_PARTS):
                        lo = par * SLOT + n * DH
                        sp.dma_start(kst[lo:lo + DH, p],
                                     k_scratch[bass.ds(b, 1), c].rearrange("a (j e r) k -> r e (a j) k", e=2, r=DH)[:, par]
                                     ).then_inc(k_in[p], 16)

            load_batch(0, 0)
            load_batch(1, 1)
            sp.wait_ge(q_hi, 8)
            sp.wait_ge(q_lo, 8)
            for c in range(2):
                sp.dma_start(q_scratch[c].rearrange("(m p) t -> p m t", p=P), qT[:, c]).then_inc(q_out, 16)
            sp.wait_ge(q_out, 32)
            sp.wait_ge(zeroed, 2)
            for par in range(2):
                for n, c in enumerate(Q_PARTS):
                    lo = par * SLOT + n * DH
                    sp.dma_start(q_stack[lo:lo + DH], q_scratch[c].rearrange("(j e r) t -> r e j t", e=2, r=DH)[:, par]
                                 ).then_inc(q_in, 16)
            restack_keys(0, 0)
            sp.wait_ge(zeroed, 1)
            for n in range(RT + 2):
                sp.dma_start(x_sent[(ST + n) * TILE:(ST + n + 1) * TILE].rearrange("(a p) c -> p a c", p=P),
                             zero.rearrange("p (a c) -> p a c", a=2)).then_inc(z_done, 16)
            for n in range(ST + E, ST + RT):
                sp.dma_start(y_sent[n * TILE:(n + 1) * TILE].rearrange("(a p) d -> p a d", p=P), y_sb[:, :, :]).then_inc(z_done, 16)

            def step(t, p, more):
                restack_keys(t + 1, 1 - p)
                if more:
                    sp.wait_ge(prep_mm, 7 * t + 5)
                    sp.wait_ge(neg_made, t + 1)
                    load_batch(t + 2, p)

            step(0, 0, True)
            with sp.Fori(0, B // 2 - 2) as i:
                step(2 * i + 1, 1, True)
                step(2 * i + 2, 0, True)
            step(B - 3, 1, True)
            step(B - 2, 0, False)

            for i in range(NT):
                sp.wait_ge(n2_lo, i + 1)
                sp.wait_ge(n2_hi, i + 1)
                sp.dma_start(x_sent[i * P:(i + 1) * P], xpair[:, i]).then_inc(sent, 16)

            def load_tile(i):
                sp.dma_start(xin[:, :, :], x_sent[bass.ds(i * TILE, TILE)].rearrange("(a p) c -> p a c", p=P)).then_inc(x_in, 16)

            def store_tile(i):
                sp.wait_ge(xT_mm, i + 2)
                load_tile(i + 2)
                sp.wait_ge(y_made, 2 * i + 4)
                sp.dma_start(y_sent[bass.ds(i * TILE, TILE)].rearrange("(a p) c -> p a c", p=P), y_sb[:, :, :]).then_inc(y_out, 16)

            sp.wait_ge(sent, 16 * NT)
            load_tile(0)
            sp.wait_ge(xT_mm, 1)
            load_tile(1)
            with sp.Fori(0, ST - 2) as i:
                store_tile(i)
            sp.wait_ge(scattered, 16 * 2 * NT)
            store_tile(ST - 2)
            store_tile(ST - 1)
            sp.wait_ge(tiles_made, 1)
            last = sp.value_load(tile_of[0:1, E:E + 1], min_val=ST + E, max_val=ST + RT)
            with sp.Fori(ST, last) as i:
                store_tile(i)
            for i in range(NT):
                sp.wait_ge(mixed, i + 1)
                sp.dma_start(out_rows[i * P:(i + 1) * P], x_sb[:, i]).then_inc(out_done, 16)
            sp.wait_ge(out_done, 16 * NT)

        @block.gpsimd
        def _(pool):
            pool.memset(ident[:, :], 0.0).then_inc(consts, 1)
            pool.memset(tri[:, :], 0.0).then_inc(consts, 1)
            pool.memset(ones16[:, :], 1.0).then_inc(consts, 1)
            pool.wait_ge(consts, 3)
            pool.affine_select(out=ident[:, :], in_=ident[:, :], compare_op=ALU.not_equal, fill=1.0,
                               base=0, pattern=[[-1, P]], channel_multiplier=1).then_inc(consts, 1)
            pool.affine_select(out=tri[:, :], in_=tri[:, :], compare_op=ALU.is_ge, fill=1.0,
                               base=0, pattern=[[-1, P]], channel_multiplier=1).then_inc(consts, 1)
            pool.wait_ge(consts, 5)
            pool.tensor_copy(ident16[:, :], ident[:, :]).then_inc(consts, 1)
            pool.memset(zero, 0.0).then_inc(zeroed, 1)
            pool.wait_ge(zeroed, 1)
            pool.memset(arena[32:64, :], 0.0).then_inc(zeroed, 1)
            pool.wait_ge(zeroed, 2)

            def make_neg(b, p, n):
                loaded = pool.compute_val(16 * n)
                pool.wait_ge(consts, 6)
                pool.wait_ge(in_mask[p], loaded)
                pool.tensor_scalar(neg[:, p], mask_in[:, p], 1.0e9, -1.0e9, ALU.mult, ALU.add).then_inc(neg_made, 1)

            def take_queries(b, p):
                rows = slice(0, SLOT + STACK)
                pool.tensor_copy(qb[rows, p], q_stack[rows, :, bass.ds(b * S, S)]).then_inc(qb_made, 1)

            make_neg(0, 0, 1)
            pool.wait_ge(q_in, 96)
            take_queries(0, 0)
            make_neg(1, 1, 1)
            take_queries(1, 1)

            def step(t, p, n):
                done = pool.compute_val(16 * t + 16 + SC_FREE)
                pool.wait_ge(consts, 6)
                pool.wait_ge(sc_read, done)
                make_neg(t + 2, p, n)
                take_queries(t + 2, p)

            with pool.Fori(0, B // 2 - 1) as i:
                step(2 * i, 0, i + 2)
                step(2 * i + 1, 1, i + 2)

            def load_weights(e):
                w1_of = sw1 if e is None else ew1[bass.ds(e, 1)].rearrange("a d f -> (a d) f")
                w2_of = sw2 if e is None else ew2[bass.ds(e, 1)].rearrange("a f d -> (a f) d")
                pool.dma_start(w1s[:, :, :], w1_of.rearrange("(c p) f -> p c f", p=P)).then_inc(in_w1, 16)
                pool.dma_start(w2s[:, :, :], w2_of.rearrange("(c p) d -> p c d", p=P)).then_inc(in_w2, 16)

            def load_b2(e, p):
                b2_of = sb2 if e is None else eb2[bass.ds(e, 1)].rearrange("a d -> (a d)")
                pool.dma_start(b2_bc[:, p], b2_of.partition_broadcast(P)).then_inc(in_b2[p], 16)

            def split_weights(n, p):
                pool.wait_ge(in_w1, 16 * n + 16)
                pool.tensor_copy(w1[:, p, HI], w1s[:, :, :]).then_inc(split_made, 1)
                pool.wait_ge(in_w2, 16 * n + 16)
                pool.tensor_copy(w2[:, p, HI], w2s[:, :, :]).then_inc(split_made, 1)
                pool.wait_ge(split_made, 4 * n + 2)
                pool.tensor_tensor(w1[:, p, LO], w1s[:, :, :], w1[:, p, HI], ALU.subtract).then_inc(split_made, 1)
                pool.tensor_tensor(w2[:, p, LO], w2s[:, :, :], w2[:, p, HI], ALU.subtract).then_inc(split_made, 1)
                pool.wait_ge(split_made, 4 * n + 4)

            load_weights(None)
            load_b2(None, 0)
            split_weights(0, 0)
            load_weights(0)
            load_b2(0, 1)

            for i in range(NT):
                pool.wait_ge(n2_made, i + 1)
                pool.wait_ge(n2_hi, i + 1)
                pool.tensor_tensor(xpair[:, i, D:2 * D], xn[:, i % 2], xpair[:, i, 0:D], ALU.subtract).then_inc(n2_lo, 1)
            split_weights(1, 1)
            load_weights(1)
            pool.wait_ge(slot_made, 2)
            pool.wait_ge(z_done, 16 * ZEROS)
            for i in range(NT):
                for j in range(2):
                    pool.indirect_dma_start(x_sent[:, :], bass.IndirectOffsetOnAxis(ap=slots[:, j, i:i + 1], axis=0),
                                            xpair[:, i], None).then_inc(scattered, 16)

            def next_expert(n, p, more):
                end = pool.value_load(tile_of[0:1, n - 2:n - 1], min_val=ST, max_val=ST + RT)
                done = pool.compute_val(end * 2 + 2)
                pool.wait_ge(in_w1, 16 * n + 16)
                pool.wait_ge(y_made, done)
                split_weights(n, p)
                load_b2(n - 1, p)
                if more:
                    load_weights(n)

            for n in range(2, E + 1):
                next_expert(n, n % 2, n < E)

            pool.wait_ge(tiles_made, 1)
            last = pool.value_load(tile_of[0:1, E:E + 1], min_val=ST + E, max_val=ST + RT)
            stored = pool.compute_val(last * 16 + Y_FREE)
            pool.wait_ge(slot_made, 2)
            pool.wait_ge(y_out, stored)
            for i in range(NT):
                if i >= 2:
                    pool.wait_ge(mixed, i - 1)
                pool.dma_start(back[:, i % 2, 2], y_sent[i * P:(i + 1) * P]).then_inc(back_in[i % 2], 16)
                for j in range(2):
                    pool.indirect_dma_start(back[:, i % 2, j], None, y_sent[:, :],
                                            bass.IndirectOffsetOnAxis(ap=slots[:, j, i:i + 1], axis=0)
                                            ).then_inc(back_in[i % 2], 16)

        @block.scalar
        def _(act):
            act.wait_ge(in_w, 64)
            for n in range(4):
                act.activation(wpair[:, n, HI], wstage[:, n], ACT.Copy, scale=0.25 if n == 0 else 1.0).then_inc(w_hi, 1)
            act.wait_ge(in_small, 16 * 10)
            act.activation(bv_pair[:, HI], bv_in[:, :], ACT.Copy).then_inc(w_hi, 1)
            act.wait_ge(dve_ask, 1)
            act.activation(nrm[:, 1], nrm[:, 0], ACT.Sqrt).then_inc(act_gave, 1)
            act.activation(gates[:, :], gates[:, :], ACT.Tanh).then_inc(act_gave, 1)
            act.wait_ge(small_T, 1)
            act.activation(bcol[:, 0:2], bank(PR[0], P, 4)[:, 0:2], ACT.Copy, scale=0.25).then_inc(small_out, 1)
            act.activation(bcol[:, 2:4], bank(PR[0], P, 4)[:, 2:4], ACT.Copy).then_inc(small_out, 1)
            act.wait_ge(small_T, 2)
            act.activation(b1[:, :, :], bank(PR[1], P, NF * (E + 1)).rearrange("p (f e) -> p f e", f=NF), ACT.Copy).then_inc(small_out, 1)
            act.wait_ge(small_T, 3)
            act.activation(rT[:, HI], bank(PT[0], P, ND * E).rearrange("p (c e) -> p c e", c=ND), ACT.Copy).then_inc(small_out, 1)
            for i in range(NT):
                act.wait_ge(xn_T, i + 1)
                act.activation(xnT[:, HI, :, i * P:(i + 1) * P], bank(SC[i % 2], P, D).rearrange("p (c t) -> p c t", c=ND),
                               ACT.Copy).then_inc(xn_hi, 1)
            for n in range(8):
                m, c = n % ND, n // ND
                act.wait_ge(q_mm, n + 1)
                act.activation(qT[:, HI, m, c * 4 * S:(c + 1) * 4 * S], bank(OB[n % 2], P, 4 * S), ACT.Identity,
                               bias=bcol[:, m:m + 1]).then_inc(q_hi, 1)

            def prep_piece(b, k, p):
                act.wait_ge(prep_mm, 7 * b + k + 1)
                if k < 2:
                    act.activation(ctxT[:, HI, k], bank(PR[k], P, S2), ACT.Copy).then_inc(prep_act, 1)
                elif k < 4:
                    if not (isinstance(b, int) and b == 0):
                        act.wait_ge(k_out, 32 * b)
                    act.activation(kT[:, HI, k - 2], bank(PR[k - 2], P, S2), ACT.Identity,
                                   bias=bcol[:, k:k + 1]).then_inc(prep_act, 1)
                elif k == 4:
                    act.activation(gpT[:, p], bank(PR[0], KP, KC * S).rearrange("p (c q) -> p c q", c=KC), ACT.Copy).then_inc(prep_act, 1)
                elif k == 5:
                    act.activation(v_sb[:, p, 0:2], bank(PR[1], KP, 2 * D).rearrange("p (c d) -> p c d", c=2), ACT.Copy).then_inc(prep_act, 1)
                else:
                    act.activation(v_sb[:, p, 2], bank(PR[0], KP, D), ACT.Copy).then_inc(prep_act, 1)

            def turn_out(t):
                act.wait_ge(oT_mm, t + 1)
                act.activation(oT[:, HI, :, bass.ds(t * S, S)], bank(PR[1], P, ND * S).rearrange("p (c q) -> p c q", c=ND),
                               ACT.Copy).then_inc(oT_hi, 1)

            for k in range(7):
                prep_piece(0, k, 0)

            def step(t, p, first=False, prep=True):
                act.wait_ge(o_read, t + 1)
                for h in range(H):
                    act.wait_ge(sc_read, 16 * t + h + 1 + SC_FREE)
                    n = h % 4
                    act.activation(probs[:, n], probs[:, n], ACT.Exp, bias=negmax[:, p, h:h + 1], scale=-1.0,
                                   accum_out=rowsum[:, p, h:h + 1]).then_inc(exp_made, 1)
                    if prep and h in (1, 2, 5, 6, 8, 9, 10):
                        prep_piece(t + 1, (1, 2, 5, 6, 8, 9, 10).index(h), 1 - p)
                    if h == 11 and not first:
                        turn_out(t - 1)

            step(0, 0, first=True)
            with act.Fori(0, B // 2 - 1) as i:
                step(2 * i + 1, 1)
                step(2 * i + 2, 0)
            step(B - 1, 1, prep=False)
            turn_out(B - 1)

            act.wait_ge(dve_ask, 2)
            act.activation(nrm[:, 1], nrm[:, 0], ACT.Sqrt).then_inc(act_gave, 1)
            act.wait_ge(dve_ask, 3)
            act.activation(nrm[:, 1], nrm[:, 0], ACT.Sqrt).then_inc(act_gave, 1)
            for i in range(NT):
                act.wait_ge(n2_made, i + 1)
                act.activation(xpair[:, i, 0:D], xn[:, i % 2], ACT.Copy).then_inc(n2_hi, 1)
                act.wait_ge(n2_T, i + 1)
                act.activation(xrT[:, i % 2], ps[:, SC[i % 2], 0:D].bitcast(F16).rearrange("p (c t) -> p c t", t=P),
                               ACT.Copy).then_inc(n2_Ts, 1)
            act.wait_ge(dve_ask, 4)
            act.activation(top[:, 6:8], top[:, 6:8], ACT.Exp, scale=-1.0).then_inc(act_gave, 1)

            def feed_tile(i, e):
                for f in range(NF):
                    act.wait_ge(h_mm, NF * i + (f | 1) + 1)
                    act.activation(hid32[:, f], ps[:, f // 2 % 4, f % 2 * TILE:(f % 2 + 1) * TILE], ACT.Relu,
                                   bias=b1[:, f, e:e + 1]).then_inc(h_relu, 1)
                act.wait_ge(xT_mm, i + 2)
                act.activation(xT[:, :, :], ps[:, 6, 0:2 * TILE].bitcast(F16).rearrange("p (c t) -> p c t", c=2 * ND),
                               ACT.Copy).then_inc(xT_made, 1)

            act.wait_ge(xT_mm, 1)
            act.activation(xT[:, :, :], ps[:, 6, 0:2 * TILE].bitcast(F16).rearrange("p (c t) -> p c t", c=2 * ND),
                           ACT.Copy).then_inc(xT_made, 1)
            with act.Fori(0, ST) as i:
                feed_tile(i, E)
            act.wait_ge(tiles_made, 1)
            for e in range(E):
                first = act.value_load(tile_of[0:1, e:e + 1], min_val=ST + e, max_val=ST + RT)
                end = act.value_load(tile_of[0:1, e + 1:e + 2], min_val=ST + e + 1, max_val=ST + RT)
                with act.Fori(first, end) as i:
                    feed_tile(i, e)

        @block.tensor
        def _(pe):
            pe.wait_ge(consts, 6)
            pe.wait_ge(in_small, 16 * 10)
            pe.transpose(bank(PR[0], P, 4), bcol_in[:, :], ident[0:4, 0:4]).then_inc(small_T, 1)
            for f in range(NF):
                mm = pe.transpose(ps[:, PR[1], f * (E + 1):(f + 1) * (E + 1)], b1_in[:, f * P:(f + 1) * P], ident[0:E + 1, 0:E + 1])
            mm.then_inc(small_T, 1)
            for c in range(ND):
                mm = pe.transpose(ps[:, PT[0], c * E:(c + 1) * E], r_in[:, c * P:(c + 1) * P], ident[0:E, 0:E])
            mm.then_inc(small_T, 1)

            for i in range(NT):
                pe.wait_ge(xn_made, i + 1)
                if i >= 2:
                    pe.wait_ge(xn_lo, i - 1)
                for c in range(ND):
                    mm = pe.transpose(ps[:, SC[i % 2], c * P:(c + 1) * P], xn[:, i % 2, c * P:(c + 1) * P], ident[:, :])
                mm.then_inc(xn_T, 1)
            pe.wait_ge(w_hi, 5)
            pe.wait_ge(w_lo, 5)
            pe.wait_ge(xn_hi, NT)
            pe.wait_ge(xn_lo, NT)
            for n in range(8):
                m, c = n % ND, n // ND
                if n >= 2:
                    pe.wait_ge(q_lo, n - 1)
                parts = [(w, a, k) for k in range(ND) for w, a in PASSES]
                for j, (w, a, k) in enumerate(parts):
                    mm = pe.matmul(bank(OB[n % 2], P, 4 * S), wpair[:, 0, w, k, m * P:(m + 1) * P],
                                   xnT[:, a, k, c * 4 * S:(c + 1) * 4 * S], start=(j == 0), stop=(j == len(parts) - 1))
                mm.then_inc(q_mm, 1)

            def prep_piece(b, k, p, n):
                first = isinstance(b, int) and b == 0
                if k == 0:
                    pe.wait_ge(in_ctx[p], 16 * n)
                    if not first:
                        pe.wait_ge(prep_act, 7 * b)
                    else:
                        pe.wait_ge(small_out, 4)
                if k == 1 and not (isinstance(b, int) and b < 2):
                    pe.wait_ge(oT_lo, b - 2 + OT_FREE)
                if k < 2:
                    for c in range(KC):
                        mm = pe.transpose(ps[:, PR[k], c * KP:(c + 1) * KP], ctx_in[:, p, c, k * P:(k + 1) * P], ident[0:KP, 0:KP])
                elif k < 4:
                    pe.wait_ge(prep_lo, 4 * b + 2)
                    parts = [(w, a, kk) for kk in range(ND) for w, a in PASSES]
                    for j, (w, a, kk) in enumerate(parts):
                        mm = pe.matmul(bank(PR[k - 2], P, S2), wpair[:, 1, w, kk, (k - 2) * P:(k - 1) * P], ctxT[:, a, kk],
                                       start=(j == 0), stop=(j == len(parts) - 1))
                elif k == 4:
                    pe.wait_ge(in_gp[p], 16 * n)
                    pe.wait_ge(prep_lo, 4 * b + 3)
                    for c in range(KC):
                        mm = pe.transpose(ps[0:KP, PR[0], c * S:(c + 1) * S], gp_in[:, p, c * KP:(c + 1) * KP], ident[0:S, 0:S])
                else:
                    if k == 5:
                        pe.wait_ge(prep_lo, 4 * b + 4)
                    else:
                        pe.wait_ge(prep_act, 7 * b + 5)
                    for c in (0, 1) if k == 5 else (2,):
                        to = ps[0:KP, PR[6 - k], c % 2 * D:c % 2 * D + D]
                        for a in range(2):
                            pe.matmul(to, ones16[0:1, 0:KP], bv_pair[0:1, a], start=(a == 0), stop=False)
                        parts = [(a, w, kk) for kk in range(ND) for a, w in PASSES]
                        for j, (a, w, kk) in enumerate(parts):
                            mm = pe.matmul(to, ctxT[:, a, kk, c * KP:(c + 1) * KP], wpair[:, 2, w, kk],
                                           start=False, stop=(j == len(parts) - 1))
                mm.then_inc(prep_mm, 1)

            def turn_out(t):
                pe.wait_ge(o_read, t + 1 + O_FREE)
                pe.wait_ge(prep_act, 7 * t + 20 if not (isinstance(t, int) and t >= B - 2) else 7 * B)
                for c in range(ND):
                    mm = pe.transpose(ps[:, PR[1], c * S:(c + 1) * S], o_n[:, c * P:(c + 1) * P], ident[0:S, 0:S])
                mm.then_inc(oT_mm, 1)

            def scores(t, h, p):
                if h == 0:
                    pe.wait_ge(k_in[p], kcount(t))
                    pe.wait_ge(qb_made, t + 1)
                pe.wait_ge(sc_read, 16 * t + h + 1)
                rows = slice(h % 2 * SLOT, h % 2 * SLOT + STACK)
                pe.matmul(bank(SC[h % 2], S, S2), qb[rows, p, h // 2], kst[rows, p, h // 2], start=True, stop=True).then_inc(sc_made, 1)

            def kcount(t):
                return (t // 2 + 1) * 96 if isinstance(t, int) else t * 48 + 0

            def turn_probs(t, h):
                pe.wait_ge(exp_made, 16 * t + h + 1)
                pe.wait_ge(pt_read, 16 * t + h + 1)
                for c in range(KC):
                    mm = pe.transpose(ps[0:KP, PT[h % 2], c * S:(c + 1) * S], probs[:, h % 4, c * KP:(c + 1) * KP], ident[0:S, 0:S])
                mm.then_inc(pt_made, 1)

            def values(t, h, p):
                if h == 0:
                    pe.wait_ge(o_read, t + 1)
                    pe.wait_ge(prep_act, 7 * t + 7)
                pe.wait_ge(pt_read, 16 * t + h + 1 + PT_FREE)
                for c in range(KC):
                    mm = pe.matmul(ps[0:S, OB[p], h * DH:(h + 1) * DH], probsT[:, h % 2, c], v_sb[:, p, c, h * DH:(h + 1) * DH],
                                   start=(c == 0), stop=(c == KC - 1))
                mm.then_inc(av_made, 1)

            pe.sem_inc(pt_made, PROBS_FREE)
            pe.sem_inc(av_made, AT_FREE)
            for k in range(7):
                prep_piece(0, k, 0, 1)
            for h in range(3):
                scores(0, h, 0)

            def step(t, p, n, tk, first=False, prep=True):
                for h in range(H):
                    turn_probs(t, h)
                    if h + 3 < H:
                        scores(t, h + 3, p)
                    elif prep:
                        if h + 3 == H:
                            pe.wait_ge(k_in[1 - p], tk)
                        scores_next(t + 1, h + 3 - H, 1 - p)
                    if h > 0:
                        values(t, h - 1, p)
                    elif not first:
                        values(t - 1, H - 1, 1 - p)
                    if prep and h in (0, 1, 4, 5, 7, 8, 9):
                        prep_piece(t + 1, (0, 1, 4, 5, 7, 8, 9).index(h), 1 - p, n)
                    if h == 10 and not first:
                        turn_out(t - 1)

            def scores_next(t, h, p):
                if h == 0:
                    pe.wait_ge(qb_made, t + 1)
                pe.wait_ge(sc_read, 16 * t + h + 1)
                rows = slice(h % 2 * SLOT, h % 2 * SLOT + STACK)
                pe.matmul(bank(SC[h % 2], S, S2), qb[rows, p, h // 2], kst[rows, p, h // 2], start=True, stop=True).then_inc(sc_made, 1)

            step(0, 0, 1, 96, first=True)
            with pe.Fori(0, B // 2 - 1) as i:
                step(2 * i + 1, 1, i + 2, i * 96 + 192)
                step(2 * i + 2, 0, i + 2, i * 96 + 192)
            step(B - 1, 1, None, None, prep=False)
            values(B - 1, H - 1, 1)
            pe.wait_ge(oT_lo, B - 1 + OT_FREE)
            turn_out(B - 1)

            pe.wait_ge(oT_hi, B)
            pe.wait_ge(oT_lo, B + OT_FREE)
            for i in range(NT):
                if i >= 2:
                    pe.wait_ge(x2_made, i - 1)
                parts = [(a, w, k) for k in range(ND) for a, w in PASSES]
                for j, (a, w, k) in enumerate(parts):
                    mm = pe.matmul(bank(OB[i % 2], P, D), oT[:, a, k, i * P:(i + 1) * P], wpair[:, 3, w, k],
                                   start=(j == 0), stop=(j == len(parts) - 1))
                mm.then_inc(pj_mm, 1)

            def route(i):
                pe.wait_ge(n2_Ts, i + 1)
                parts = [(a, w, k) for k in range(ND) for a in range(2) for w in range(2)]
                for j, (a, w, k) in enumerate(parts):
                    mm = pe.matmul(ps[:, PR[1], P + i * E:P + (i + 1) * E], xrT[:, i % 2, a * ND + k], rT[:, w, k],
                                   start=(j == 0), stop=(j == len(parts) - 1))
                mm.then_inc(rl_mm, 1)

            for i in range(NT):
                pe.wait_ge(n2_hi, i + 1)
                pe.wait_ge(n2_lo, i + 1)
                if i >= 2:
                    pe.wait_ge(n2_Ts, i - 1)
                for c in range(2 * ND):
                    mm = pe.transpose(ps[:, SC[i % 2], 0:D].bitcast(F16)[:, c * P:(c + 1) * P], xpair[:, i, c * P:(c + 1) * P], ident16[:, :])
                mm.then_inc(n2_T, 1)
                if i >= 1:
                    route(i - 1)
            route(NT - 1)

            def turn_tile(i):
                pe.wait_ge(x_in, 16 * i + 16)
                for a in range(TILE // P):
                    for c in range(2 * ND):
                        mm = pe.transpose(ps[:, 6, 0:2 * TILE].bitcast(F16)[:, c * TILE + a * P:c * TILE + (a + 1) * P],
                                          xin[:, a, c * P:(c + 1) * P], ident16[:, :])
                mm.then_inc(xT_mm, 1)

            def feed_tile(i, p, between=None):
                pe.wait_ge(xT_made, i + 1)
                for f in range(NF):
                    parts = [(w, a, k) for k in range(ND) for w, a in PASSES]
                    for j, (w, a, k) in enumerate(parts):
                        mm = pe.matmul(ps[:, f // 2 % 4, f % 2 * TILE:(f % 2 + 1) * TILE], w1[:, p, w, k, f * P:(f + 1) * P],
                                       xT[:, a * ND + k], start=(j == 0), stop=(j == len(parts) - 1))
                    mm.then_inc(h_mm, 1)
                turn_tile(i + 1)
                if between:
                    between()
                for a in range(TILE // P):
                    pe.wait_ge(y_made, 2 * i + a + 1)
                    for f in range(NF):
                        if a == 0 and f % 2 == 0:
                            pe.wait_ge(h_split, (NF // 2) * i + f // 2 + 1)
                        for j, (u, w) in enumerate(PASSES):
                            mm = pe.matmul(ps[:, 4 + a, 0:D], hid[:, u, f, a * P:(a + 1) * P], w2[:, p, w, f],
                                           start=(f == 0 and j == 0), stop=(f == NF - 1 and j == 2))
                    mm.then_inc(y_mm, 1)

            turn_tile(0)
            pe.wait_ge(split_made, 4)
            def rank_pairs():
                pe.wait_ge(cnt_made, 1)
                rk = bank(PR[1], P, NT * E)
                pe.matmul(rk, tri[:, :], count16[:, 0].rearrange("p i e -> p (i e)"), start=True, stop=False)
                pe.matmul(rk, ones16[:, :], count16[:, 1].rearrange("p i e -> p (i e)"), start=False, stop=True).then_inc(rank_mm, 1)
                pe.matmul(ps[:, PR[1], NT * E:(NT + 1) * E], ones16[:, :], count16[:, 2, 0], start=True, stop=True).then_inc(rank_mm, 1)

            feed_tile(0, 0, rank_pairs)
            with pe.Fori(1, ST) as i:
                feed_tile(i, 0)
            pe.wait_ge(tiles_made, 1)
            for e in range(E):
                first = pe.value_load(tile_of[0:1, e:e + 1], min_val=ST + e, max_val=ST + RT)
                end = pe.value_load(tile_of[0:1, e + 1:e + 2], min_val=ST + e + 1, max_val=ST + RT)
                pe.wait_ge(split_made, 4 * (e + 2))
                with pe.Fori(first, end) as i:
                    feed_tile(i, (e + 1) % 2)
    
        @block.vector
        def _(dve):
            steps = [0]

            def then(ins):
                steps[0] += 1
                ins.then_inc(dve_step, 1)
                dve.wait_ge(dve_step, steps[0])

            def inverse_root(gave):
                dve.wait_ge(act_gave, gave)
                then(dve.reciprocal(nrm[:, 3], nrm[:, 1]))
                then(dve.tensor_tensor(nrm[:, 3], nrm[:, 3], nrm[:, 0], ALU.mult))
                then(dve.tensor_tensor(nrm[:, 3], nrm[:, 3], nrm[:, 1], ALU.add))
                then(dve.tensor_scalar(nrm[:, 3], nrm[:, 3], 0.5, None, ALU.mult))
                then(dve.reciprocal(nrm[:, 2], nrm[:, 3]))

            dve.wait_ge(in_x, 16)
            for i in range(NT):
                last = dve.bn_stats(stats[:, i], x_sb[:, i])
            then(last)
            for i in range(NT):
                last = dve.bn_aggr(mv[:, i], stats[:, i])
            then(last)
            dve.tensor_scalar(nrm[:, 0], mv[:, :, 1], LN_EPS, None, ALU.add).then_inc(dve_ask, 1)
            dve.wait_ge(w_hi, 4)
            dve.scalar_tensor_tensor(wpair[:, 0, LO], wstage[:, 0], 0.25, wpair[:, 0, HI], ALU.mult, ALU.subtract).then_inc(w_lo, 1)
            for n in range(1, 4):
                dve.tensor_tensor(wpair[:, n, LO], wstage[:, n], wpair[:, n, HI], ALU.subtract).then_inc(w_lo, 1)
            dve.wait_ge(w_hi, 5)
            dve.tensor_tensor(bv_pair[:, LO], bv_in[:, :], bv_pair[:, HI], ALU.subtract).then_inc(w_lo, 1)
            inverse_root(1)

            def lo_part(i):
                dve.wait_ge(xn_hi, i + 1)
                cols = slice(i * P, (i + 1) * P)
                dve.tensor_tensor(xnT[:, LO, :, cols], bank(SC[i % 2], P, D).rearrange("p (c t) -> p c t", c=ND),
                                  xnT[:, HI, :, cols], ALU.subtract).then_inc(xn_lo, 1)

            for i in range(NT):
                if i >= 2:
                    dve.wait_ge(xn_T, i - 1)
                dve.tensor_scalar(xn[:, i % 2], x_sb[:, i], mv[:, i, 0:1], nrm[:, 2, i:i + 1], ALU.subtract, ALU.mult).then_inc(xn_made, 1)
                if i >= 1:
                    lo_part(i - 1)
            lo_part(NT - 1)
            dve.wait_ge(small_out, 4)
            dve.tensor_tensor(rT[:, LO], bank(PT[0], P, ND * E).rearrange("p (c e) -> p c e", c=ND), rT[:, HI], ALU.subtract).then_inc(w_lo, 1)
            for n in range(8):
                m, c = n % ND, n // ND
                dve.wait_ge(q_hi, n + 1)
                cols = slice(c * 4 * S, (c + 1) * 4 * S)
                dve.scalar_tensor_tensor(qT[:, LO, m, cols], bank(OB[n % 2], P, 4 * S), bcol[:, m:m + 1], qT[:, HI, m, cols],
                                         ALU.add, ALU.subtract).then_inc(q_lo, 1)
            dve.wait_ge(act_gave, 2)
            then(dve.tensor_scalar(bo_bc[:, :], bo_bc[:, :], gates[:, 0:1], None, ALU.mult))
            dve.tensor_tensor(x_sb[:, :, :], x_sb[:, :, :], bo_bc[:, :].unsqueeze(1).to_broadcast([P, NT, D]), ALU.add).then_inc(resid, 1)

            dve.sem_inc(sc_read, SC_FREE)
            dve.sem_inc(pt_read, PT_FREE)
            dve.sem_inc(o_read, O_FREE)
            dve.sem_inc(oT_lo, OT_FREE)

            def prep_lo_part(b, k):
                dve.wait_ge(prep_act, 7 * b + k + 1)
                if k < 2:
                    dve.tensor_tensor(ctxT[:, LO, k], bank(PR[k], P, S2), ctxT[:, HI, k], ALU.subtract).then_inc(prep_lo, 1)
                else:
                    dve.scalar_tensor_tensor(kT[:, LO, k - 2], bank(PR[k - 2], P, S2), bcol[:, k:k + 1], kT[:, HI, k - 2],
                                             ALU.add, ALU.subtract).then_inc(prep_lo, 1)

            def mask_scores(t, h, p):
                if h == 0:
                    dve.wait_ge(neg_made, t + 1)
                head = dve.compute_val(16 * t + h + 1)
                dve.wait_ge(neg_made, 1)
                dve.wait_ge(sc_made, head)
                dve.wait_ge(pt_made, head)
                dve.tensor_tensor_reduce(probs[:, h % 4], bank(SC[h % 2], S, S2), neg[:, p], -1.0, BIG, ALU.add, ALU.min,
                                         negmax[:, p, h:h + 1]).then_inc(sc_read, 1)

            def weigh(t, h, p):
                dve.wait_ge(pt_made, 16 * t + h + 1 + PROBS_FREE)
                dve.wait_ge(av_made, 16 * t + h + 1)
                dve.tensor_tensor(probsT[:, h % 2], bank(PT[h % 2], KP, KC * S).rearrange("p (c q) -> p c q", c=KC),
                                  gpT[:, p], ALU.mult).then_inc(pt_read, 1)

            def divide(t, p):
                dve.wait_ge(av_made, 16 * t + 16 + AT_FREE)
                dve.reciprocal(rrow[:, :], rowsum[:, p]).then_inc(rr_made, 1)
                dve.wait_ge(rr_made, t + 1)
                if not (isinstance(t, int) and t == 0):
                    dve.wait_ge(oT_mm, t)
                dve.tensor_tensor(o_n[:, :].rearrange("q (h d) -> q h d", h=H),
                                  bank(OB[p], S, D).rearrange("q (h d) -> q h d", h=H),
                                  rrow[:, :].unsqueeze(2).to_broadcast([S, H, DH]), ALU.mult).then_inc(o_read, 1)

            def turn_out(t):
                dve.wait_ge(oT_hi, t + 1)
                cols = bass.ds(t * S, S)
                dve.tensor_tensor(oT[:, LO, :, cols], bank(PR[1], P, ND * S).rearrange("p (c q) -> p c q", c=ND),
                                  oT[:, HI, :, cols], ALU.subtract).then_inc(oT_lo, 1)

            for k in range(4):
                prep_lo_part(0, k)
            mask_scores(0, 0, 0)
            mask_scores(0, 1, 0)

            def step(t, p, first=False, prep=True):
                for h in range(H):
                    if h + 2 < H:
                        mask_scores(t, h + 2, p)
                    elif prep:
                        mask_scores(t + 1, h + 2 - H, 1 - p)
                    weigh(t, h, p)
                    if prep and h in (2, 3, 6, 7):
                        prep_lo_part(t + 1, (2, 3, 6, 7).index(h))
                    if h == 3 and not first:
                        divide(t - 1, 1 - p)
                    if h == 12 and not first:
                        turn_out(t - 1)

            step(0, 0, first=True)
            with dve.Fori(0, B // 2 - 1) as i:
                step(2 * i + 1, 1)
                step(2 * i + 2, 0)
            step(B - 1, 1, prep=False)
            divide(B - 1, 1)
            turn_out(B - 1)

            for i in range(NT):
                dve.wait_ge(pj_mm, i + 1)
                if i == 0:
                    dve.wait_ge(resid, 1)
                dve.scalar_tensor_tensor(x_sb[:, i], bank(OB[i % 2], P, D), gates[:, 0:1], x_sb[:, i], ALU.mult, ALU.add).then_inc(x2_made, 1)
                if i >= 1:
                    dve.wait_ge(x2_made, i)
                    dve.bn_stats(stats[:, i - 1], x_sb[:, i - 1])
            dve.wait_ge(x2_made, NT)
            then(dve.bn_stats(stats[:, NT - 1], x_sb[:, NT - 1]))
            for i in range(NT):
                last = dve.bn_aggr(mv[:, i], stats[:, i])
            then(last)
            dve.tensor_scalar(nrm[:, 0], mv[:, :, 1], LN_EPS, None, ALU.add).then_inc(dve_ask, 1)
            inverse_root(3)
            then(dve.tensor_copy(nrm[:, 4], nrm[:, 2]))
            then(dve.tensor_tensor(nrm[:, 5], nrm[:, 2], nrm[:, 2], ALU.mult))
            then(dve.tensor_tensor(nrm[:, 5], nrm[:, 5], mv[:, :, 1], ALU.mult))
            dve.tensor_scalar(nrm[:, 0], nrm[:, 5], RMS_EPS, None, ALU.add).then_inc(dve_ask, 1)
            inverse_root(4)
            then(dve.tensor_tensor(nrm[:, 4], nrm[:, 4], nrm[:, 2], ALU.mult))
            for i in range(NT):
                if i >= 2:
                    dve.wait_ge(n2_lo, i - 1)
                dve.tensor_scalar(xn[:, i % 2], x_sb[:, i], mv[:, i, 0:1], nrm[:, 4, i:i + 1], ALU.subtract, ALU.mult).then_inc(n2a, 1)
                dve.wait_ge(n2a, i + 1)
                dve.tensor_tensor(xn[:, i % 2], xn[:, i % 2], nw_bc[:, :], ALU.mult).then_inc(n2_made, 1)

            dve.wait_ge(rl_mm, NT)
            then(dve.tensor_copy(logit[:, :, :], ps[:, PR[1], P:P + NT * E].rearrange("p (i e) -> p i e", e=E)))

            def spread(col):
                return col.unsqueeze(2).to_broadcast([P, NT, E])

            def choose(src, n):
                then(dve.tensor_reduce(top[:, n], src, AX.X, ALU.max))
                then(dve.tensor_tensor(rt[:, n], src, spread(top[:, n]), ALU.is_equal))
                then(dve.tensor_copy(top[:, 2], rt[:, n, :, 0]))
                for e in range(1, E):
                    then(dve.tensor_scalar(top[:, 3], top[:, 2], -1.0, 1.0, ALU.mult, ALU.add))
                    then(dve.tensor_tensor(rt[:, n, :, e], rt[:, n, :, e], top[:, 3], ALU.mult))
                    then(dve.tensor_tensor(top[:, 2], top[:, 2], rt[:, n, :, e], ALU.add))

            choose(logit[:, :, :], 0)
            then(dve.scalar_tensor_tensor(rt[:, 2], rt[:, 0], -BIG, logit[:, :, :], ALU.mult, ALU.add))
            choose(rt[:, 2], 1)
            then(dve.tensor_copy(top[:, 6:8], top[:, 0:2]))
            then(dve.tensor_tensor(rt[:, 3], rt[:, 0], rt[:, 1], ALU.add))
            then(dve.tensor_copy(count16[:, 0], rt[:, 3]))
            then(dve.memset(rt[:, 4, 0], 0.0))
            for i in range(1, NT):
                then(dve.tensor_tensor(rt[:, 4, i], rt[:, 4, i - 1], rt[:, 3, i - 1], ALU.add))
            then(dve.tensor_copy(count16[:, 1], rt[:, 4]))
            then(dve.tensor_tensor(est[:, 0, 0:E], rt[:, 4, NT - 1], rt[:, 3, NT - 1], ALU.add))
            dve.tensor_copy(count16[:, 2, 0], est[:, 0, 0:E]).then_inc(cnt_made, 1)
            dve.sem_inc(dve_ask, 1)
            dve.wait_ge(rank_mm, 2)
            then(dve.tensor_scalar(est[:, 1, 0:E], ps[:, PR[1], NT * E:(NT + 1) * E], 1.0, float(TILE - 1), ALU.max, ALU.add))
            then(dve.tensor_copy(est_i[:, 0, 0:E], est[:, 1, 0:E]))
            then(dve.tensor_scalar(est_i[:, 1, 0:E], est_i[:, 0, 0:E], TILE.bit_length() - 1, None, ALU.arith_shift_right))
            then(dve.tensor_copy(est[:, 2, 0:E], est_i[:, 1, 0:E]))
            then(dve.memset(est[:, 3, 0:1], float(ST)))
            for e in range(E):
                then(dve.tensor_tensor(est[:, 3, e + 1:e + 2], est[:, 3, e:e + 1], est[:, 2, e:e + 1], ALU.add))
            dve.tensor_copy(tile_of[:, 0:E + 1], est[:, 3, 0:E + 1]).then_inc(tiles_made, 1)
            then(dve.tensor_scalar(est[:, 4, 0:E], est[:, 3, 0:E], float(TILE), None, ALU.mult))
            then(dve.tensor_tensor(rt[:, 4], bank(PR[1], P, NT * E).rearrange("p (i e) -> p i e", e=E),
                                   est[:, 4, 0:E].unsqueeze(1).to_broadcast([P, NT, E]), ALU.add))
            for j in range(2):
                then(dve.tensor_tensor(rt[:, 5], rt[:, 4], rt[:, j], ALU.mult))
                then(dve.tensor_reduce(top[:, 4 + j], rt[:, 5], AX.X, ALU.add))
                dve.tensor_copy(slots[:, j], top[:, 4 + j]).then_inc(slot_made, 1)
            dve.wait_ge(act_gave, 5)
            then(dve.tensor_scalar(top[:, 6:8], top[:, 6:8], 1.0, None, ALU.add))
            then(dve.reciprocal(top[:, 6:8], top[:, 6:8]))
            then(dve.tensor_tensor(top[:, 8], top[:, 6], top[:, 7], ALU.add))
            then(dve.tensor_scalar(top[:, 8], top[:, 8], 1e-6, None, ALU.add))
            then(dve.reciprocal(top[:, 9], top[:, 8]))
            then(dve.tensor_tensor(top[:, 6], top[:, 6], top[:, 9], ALU.mult))
            then(dve.tensor_tensor(top[:, 7], top[:, 7], top[:, 9], ALU.mult))

            dve.sem_inc(y_made, 2)
            dve.sem_inc(y_out, Y_FREE)

            def feed_tile(i, p, nb2):
                for g in range(NF // 2):
                    two = slice(2 * g, 2 * g + 2)
                    dve.wait_ge(h_relu, NF * i + 2 * g + 2)
                    dve.tensor_copy(hid[:, HI, two], hid32[:, two]).then_inc(h_hi, 1)
                    dve.wait_ge(h_hi, (NF // 2) * i + g + 1)
                    dve.tensor_tensor(hid[:, LO, two], hid32[:, two], hid[:, HI, two], ALU.subtract).then_inc(h_split, 1)
                dve.wait_ge(y_out, 16 * i + Y_FREE)
                for a in range(TILE // P):
                    dve.wait_ge(y_mm, 2 * i + a + 1)
                    dve.tensor_tensor(y_sb[:, a], ps[:, 4 + a, 0:D], b2_bc[:, p], ALU.add).then_inc(y_made, 1)

            dve.wait_ge(z_done, 16 * ZEROS)
            dve.wait_ge(in_b2[0], 16)
            with dve.Fori(0, ST) as i:
                feed_tile(i, 0, 1)
            dve.wait_ge(tiles_made, 1)
            for e in range(E):
                first = dve.value_load(tile_of[0:1, e:e + 1], min_val=ST + e, max_val=ST + RT)
                end = dve.value_load(tile_of[0:1, e + 1:e + 2], min_val=ST + e + 1, max_val=ST + RT)
                dve.wait_ge(in_b2[(e + 1) % 2], 16 * ((e + 1) // 2 + 1))
                with dve.Fori(first, end) as i:
                    feed_tile(i, (e + 1) % 2, None)
    
            for i in range(NT):
                p = i % 2
                dve.wait_ge(back_in[p], 48 * (i // 2 + 1))
                then(dve.scalar_tensor_tensor(back[:, p, 2], back[:, p, 0], top[:, 6, i:i + 1], back[:, p, 2], ALU.mult, ALU.add))
                then(dve.scalar_tensor_tensor(back[:, p, 2], back[:, p, 1], top[:, 7, i:i + 1], back[:, p, 2], ALU.mult, ALU.add))
                dve.scalar_tensor_tensor(x_sb[:, i], back[:, p, 2], gates[:, 1:2], x_sb[:, i], ALU.mult, ALU.add).then_inc(mixed, 1)


_INS = ['x', 'ctx_1024', 'fside_BxSxS2_0', 'mask_BxSxS2_ik1', 'g_xattn', 'g_ffn', 'L0_xattn_wq_k', 'L0_xattn_wq_b',
        'L0_xattn_wk_k', 'L0_xattn_wk_b', 'L0_xattn_wv_k', 'L0_xattn_wv_b', 'L0_xattn_wo_k', 'L0_xattn_wo_b',
        'L0_ffn_norm_weight', 'L0_ffn_router_w', 'L0_ffn_sw1', 'L0_ffn_sb1', 'L0_ffn_sw2', 'L0_ffn_sb2',
        'L0_ffn_ew1', 'L0_ffn_eb1', 'L0_ffn_ew2', 'L0_ffn_eb2']
_OUTS = [((B, S, D), 'float32')]


def kernel(**inputs):
    import numpy as _np
    import concourse.bacc as _bacc
    from concourse import mybir as _mybir
    from concourse.bass_utils import run_bass_kernel_spmd as _run

    nc = _bacc.Bacc("TRN2", target_bir_lowering=False, num_devices=1)
    arrays, args = {}, []
    for name in _INS:
        a = _np.ascontiguousarray(inputs[name])
        arrays[f"in_{name}_dram"] = a
        args.append(nc.dram_tensor(f"in_{name}_dram", a.shape, _mybir.dt.from_np(a.dtype), kind="ExternalInput").ap())
    for i, (shape, dtype) in enumerate(_OUTS):
        dt = _mybir.dt.from_np(_np.dtype(dtype))
        args.append(nc.dram_tensor(f"out_{i}_dram", shape, dt, kind="ExternalOutput").ap())
    flamingo_block(nc, *args)
    r = _run(nc, [arrays], core_ids=[0])
    got = tuple(r.results[0][f"out_{i}_dram"] for i in range(len(_OUTS)))
    return got[0]
```

```python
from contextlib import ExitStack

import concourse.bass as bass
from concourse import mybir

F32, F16, I32 = mybir.dt.float32, mybir.dt.float16, mybir.dt.int32
ALU = mybir.AluOpType
ACT = mybir.ActivationFunctionType
AX = mybir.AxisListType

P = 128
B, S, D = 16, 112, 256
S2, H = 375, 16
DH = D // H
T = B * S
NT = T // P
NTP = 8
KC = 3
KP = S2 // KC
ND = D // P
E, F = 8, 1024
NF = F // P
TILE = 256
ST = T // TILE
RT = (2 * T + E * (TILE - 1)) // TILE
ROWS = (RT + 2) * TILE
SMALLS = 11
ZEROS = RT + 2 + RT - E
HI, LO = 0, 1
PASSES = ((HI, HI), (HI, LO), (LO, HI))
SLOT = 64
STACK = 3 * DH
Q_PARTS, K_PARTS = (HI, LO, HI), (HI, HI, LO)
BACK = 4
LN_EPS, RMS_EPS = 1e-5, 1e-8
BIG = 3.0e38


def flamingo_block(nc, x, ctx, gp, mask, g_xattn, g_ffn, wq, bq, wk, bk, wv, bv, wo, bo, nw, router,
                   sw1, sb1, sw2, sb2, ew1, eb1, ew2, eb2, out):
    x_rows = x.rearrange("b s d -> (b s) d")
    out_rows = out.rearrange("b s d -> (b s) d")
    k_scratch = nc.dram_tensor("k_scratch", (B, 2, D, S2), F16, kind="Internal").ap()
    q_scratch = nc.dram_tensor("q_scratch", (2, D, T), F16, kind="Internal").ap()
    x_sent = nc.dram_tensor("x_sent", (ROWS, 2 * D), F16, kind="Internal").ap()
    y_sent = nc.dram_tensor("y_sent", (RT * TILE, D), F32, kind="Internal").ap()

    with ExitStack() as st:
        def sb(name, shape, dt):
            return st.enter_context(nc.sbuf_tensor(name, shape, dt))

        def sem(name):
            return st.enter_context(nc.semaphore(name))

        x_sb = sb("x_sb", [P, NT, D], F32)
        xnT = sb("xnT", [P, 2, ND, T], F16)
        oT = xnT
        x2T = xnT
        qT = sb("qT", [P, 2, ND, T], F16)
        xpair = qT[:, :, :, :].rearrange("p a b t -> p (a b t)").rearrange("p (i c) -> p i c", i=NT)
        arena = sb("arena", [P, H // 2 * T // 2], F32)
        q_stack = arena[:, :].bitcast(F16).rearrange("p (j t) -> p j t", j=H // 2)
        hid32 = arena[:, 0:NF * TILE].rearrange("p (f n) -> p f n", f=NF)
        hid = arena[:, NF * TILE:2 * NF * TILE].bitcast(F16).rearrange("p (a f n) -> p a f n", a=2, f=NF)
        back = arena[:, 0:BACK * 2 * D].rearrange("p (a c d) -> p a c d", a=BACK, c=2)
        xn2 = arena[:, 0:NT * D].rearrange("p (i d) -> p i d", i=NT)
        qb = sb("qb", [P, 2, H // 2, S], F16)
        kst_all = sb("kst", [P, H * S2], F16)
        kst = kst_all[:, :].rearrange("p (a j k) -> p a j k", a=2, j=H // 2)
        kT = sb("kT", [P, 2, ND, S2], F16)
        ctx_in = sb("ctx_in", [KP, 2, KC, D], F32)
        ctxT = sb("ctxT", [P, 2, ND, S2], F16)
        mask_in = sb("mask_in", [S, 2, S2], I32)
        neg = sb("neg", [S, 2, S2], F32)
        gp_in = sb("gp_in", [S, 2, S2], F32)
        gpT = sb("gpT", [KP, 2, KC, S], F32)
        probs = sb("probs", [S, 4, S2], F32)
        probsT = sb("probsT", [KP, 2, KC, S], F32)
        negmax = sb("negmax", [S, 2, H], F32)
        rowsum = sb("rowsum", [S, 2, H], F32)
        rinv = sb("rinv", [S, H], F32)
        rrow = sb("rrow", [S, H, DH], F32)
        rT = sb("rT", [P, ND, S], F32)
        o32 = sb("o32", [P, ND, S], F32)
        wpair = sb("wpair", [P, 4, 2, ND, D], F16)
        bcol_in = sb("bcol_in", [4, P], F32)
        bcol = sb("bcol", [P, 4], F32)
        bv_in = sb("bv_in", [1, D], F32)
        bv_pair = sb("bv_pair", [1, 2, D], F16)
        bo_bc = sb("bo_bc", [P, D], F32)
        nw_bc = sb("nw_bc", [P, D], F32)
        b1 = sb("b1", [P, NF, E + 1], F32)
        sb2_bc = sb("sb2_bc", [P, D], F32)
        b2_bc = kst_all[:, :].bitcast(F32)[:, 0:E * D].rearrange("p (e d) -> p e d", e=E)
        r_in = sb("r_in", [E, D], F32)
        routerT = sb("routerT", [P, 2, ND, E], F16)
        gates = sb("gates", [P, 2], F32)
        ident = sb("ident", [P, P], F32)
        ident16 = sb("ident16", [P, P], F16)
        tri = sb("tri", [P, P], F16)
        ones16 = sb("ones16", [P, P], F16)
        stats = sb("stats", [P, NT, 6], F32)
        mv = sb("mv", [P, NT, 2], F32)
        nrm = sb("nrm", [P, 8, NT], F32)
        xn = sb("xn", [P, 2, D], F32)
        rt = sb("rt", [P, 6, NT, E], F32)
        order = sb("order", [P, E], F32)
        before = sb("before", [P, 2, NTP + NT, E], F32)
        top = sb("top", [P, 10, NT], F32)
        count16 = sb("count16", [P, 3, NT, E], F16)
        est = sb("est", [P, 6, E + E], F32)
        est_i = sb("est_i", [P, 2, E], I32)
        tile_of = sb("tile_of", [P, E + 2], I32)
        slots = sb("slots", [P, 2, NT], I32)
        w1s = sb("w1s", [P, ND, F], F32)
        w2s = sb("w2s", [P, NF, D], F32)
        wstage = w2s[:, :, :].rearrange("p (n c) d -> p n c d", n=4)
        b1_in = w1s[0:E + 1, 0]
        w1 = sb("w1", [P, 2, 2, ND, F], F16)
        w2 = sb("w2", [P, 2, 2, NF, D], F16)
        PAD = 2 * DH
        values_pad = [w[0:KP, 1].rearrange("p a n c -> p (a n c)").bitcast(F32)[:, 0:KC * (H + 1) * PAD].rearrange(
            "p (c n) -> p c n", c=KC) for w in (w1, w2)]
        xin = sb("xin", [P, TILE // P, 2 * D], F16)
        xT = sb("xT", [P, 2 * ND, TILE], F16)
        y_sb = sb("y_sb", [P, TILE // P, D], F32)
        zero = y_sb[:, :, :].rearrange("p a d -> p (a d)").bitcast(F16)

        ps = st.enter_context(nc.psum_tensor("ps", [P, 8, 512], F32))
        SC, PT, OB, PR = (0, 1), (2, 3), (4, 5), (6, 7)

        in_x, in_w, in_small = sem("in_x"), sem("in_w"), sem("in_small")
        in_ctx = [sem(f"in_ctx{p}") for p in range(2)]
        in_mask = [sem(f"in_mask{p}") for p in range(2)]
        in_gp = [sem(f"in_gp{p}") for p in range(2)]
        consts = sem("consts")
        dve_step, act_step = sem("dve_step"), sem("act_step")
        dve_ask, act_ask, act_gave = sem("dve_ask"), sem("act_ask"), sem("act_gave")
        w_hi, w_lo = sem("w_hi"), sem("w_lo")
        small_T, small_out = sem("small_T"), sem("small_out")
        xn_made, xn_T, xn_hi, xn_lo = sem("xn_made"), sem("xn_T"), sem("xn_hi"), sem("xn_lo")
        q_mm, q_hi, q_lo, q_out, q_in = sem("q_mm"), sem("q_hi"), sem("q_lo"), sem("q_out"), sem("q_in")
        resid = sem("resid")
        neg_made, qb_made = sem("neg_made"), sem("qb_made")
        prep_mm, prep_act, prep_lo = sem("prep_mm"), sem("prep_act"), sem("prep_lo")
        k_out = sem("k_out")
        k_in = [sem(f"k_in{p}") for p in range(2)]
        sc_made, sc_read, exp_made = sem("sc_made"), sem("sc_read"), sem("exp_made")
        pt_made, pt_read, av_made = sem("pt_made"), sem("pt_read"), sem("av_made")
        o_read, rr_made, rT_mm, rT_made = sem("o_read"), sem("rr_made"), sem("rT_mm"), sem("rT_made")
        ri_made, oT_hi, oT_lo = sem("ri_made"), sem("oT_hi"), sem("oT_lo")
        pj_mm, x2_made = sem("pj_mm"), sem("x2_made")
        n2a, n2_made, n2_hi, n2_lo = sem("n2a"), sem("n2_made"), sem("n2_hi"), sem("n2_lo")
        n2_T, n2_Ts, rl_mm = sem("n2_T"), sem("n2_Ts"), sem("rl_mm")
        zeroed, z_done = sem("zeroed"), sem("z_done")
        cnt_made, rank_mm, slot_made, tiles_made, scattered = (
            sem("cnt_made"), sem("rank_mm"), sem("slot_made"), sem("tiles_made"), sem("scattered"))
        in_w1, in_w2 = sem("in_w1"), sem("in_w2")
        in_b2 = sem("in_b2")
        w1_hi, w1_lo, w2_hi, w2_lo = sem("w1_hi"), sem("w1_lo"), sem("w2_hi"), sem("w2_lo")
        x_in = sem("x_in")
        xT_mm, xT_made = sem("xT_mm"), sem("xT_made")
        h_mm, h_relu, h_hi, h_split = sem("h_mm"), sem("h_relu"), sem("h_hi"), sem("h_split")
        y_mm, y_made, y_out = sem("y_mm"), sem("y_made"), sem("y_out")
        back_in = [sem(f"back_in{p}") for p in range(BACK)]
        mixed, out_done = sem("mixed"), sem("out_done")

        block = st.enter_context(nc.Block())

        SC_FREE, PROBS_FREE, PT_FREE, AT_FREE, O_FREE, RT_FREE, Y_FREE = 2, 4, 2, 2, 2, 1, 16

        def bank(n, rows, cols):
            return ps[0:rows, n, 0:cols]

        @block.sync
        def _(sp):
            sp.dma_start(x_sb[:, :, :], x_rows.rearrange("(i p) d -> p i d", p=P)).then_inc(in_x, 16)
            for n, w in enumerate((wq, wk, wv, wo)):
                sp.dma_start(wstage[:, n], w.rearrange("(c p) n -> p c n", p=P)).then_inc(in_w, 16)
            smalls = [(bcol_in[0:2, :], bq.rearrange("(c p) -> c p", p=P)),
                      (bcol_in[2:4, :], bk.rearrange("(c p) -> c p", p=P)),
                      (bv_in[:, :], bv.rearrange("(a n) -> a n", a=1)),
                      (bo_bc[:, :], bo.partition_broadcast(P)),
                      (nw_bc[:, :], nw.partition_broadcast(P)),
                      (b1_in[0:E], eb1), (b1_in[E:E + 1], sb1.rearrange("(a n) -> a n", a=1)),
                      (r_in[:, :], router),
                      (gates[:, 0:1], g_xattn.partition_broadcast(P)),
                      (gates[:, 1:2], g_ffn.partition_broadcast(P)),
                      (sb2_bc[:, :], sb2.partition_broadcast(P))]
            for to, of in smalls:
                sp.dma_start(to, of).then_inc(in_small, 16)

            def load_batch(b, p):
                sp.dma_start(ctx_in[:, p], ctx[bass.ds(b, 1)].rearrange("a (c p) d -> p (a c) d", p=KP)).then_inc(in_ctx[p], 16)
                sp.dma_start(mask_in[:, p], mask[bass.ds(b, 1)].rearrange("a q k -> q (a k)")).then_inc(in_mask[p], 16)
                sp.dma_start(gp_in[:, p], gp[bass.ds(b, 1)].rearrange("a q k -> q (a k)")).then_inc(in_gp[p], 16)

            def restack_keys(b, p):
                sp.wait_ge(prep_act, 7 * b + 4)
                sp.wait_ge(prep_lo, 4 * b + 4)
                for c in range(2):
                    sp.dma_start(k_scratch[bass.ds(b, 1), c].rearrange("a (m p) k -> p (a m) k", p=P),
                                 kT[:, c]).then_inc(k_out, 16)
                sp.wait_ge(k_out, 32 * b + 32)
                for par in range(2):
                    for n, c in enumerate(K_PARTS):
                        lo = par * SLOT + n * DH
                        sp.dma_start(kst[lo:lo + DH, p],
                                     k_scratch[bass.ds(b, 1), c].rearrange("a (j e r) k -> r e (a j) k", e=2, r=DH)[:, par]
                                     ).then_inc(k_in[p], 16)

            def load_weights(e):
                if e > 0:
                    sp.wait_ge(w1_lo, e + 1)
                sp.dma_start(w1s[:, :, :], ew1[e].rearrange("(c p) f -> p c f", p=P)).then_inc(in_w1, 16)
                if e > 0:
                    sp.wait_ge(w2_lo, e + 1)
                sp.dma_start(w2s[:, :, :], ew2[e].rearrange("(c p) d -> p c d", p=P)).then_inc(in_w2, 16)

            load_batch(0, 0)
            load_batch(1, 1)
            sp.wait_ge(q_hi, 8)
            sp.wait_ge(q_lo, 8)
            for c in range(2):
                sp.dma_start(q_scratch[c].rearrange("(m p) t -> p m t", p=P), qT[:, c]).then_inc(q_out, 16)
            sp.wait_ge(q_out, 32)
            sp.wait_ge(zeroed, E + 4)
            for par in range(2):
                for n, c in enumerate(Q_PARTS):
                    lo = par * SLOT + n * DH
                    sp.dma_start(q_stack[lo:lo + DH], q_scratch[c].rearrange("(j e r) t -> r e j t", e=2, r=DH)[:, par]
                                 ).then_inc(q_in, 16)
            restack_keys(0, 0)
            sp.wait_ge(small_T, 2)
            sp.dma_start(w1s[:, :, :], sw1.rearrange("(c p) f -> p c f", p=P)).then_inc(in_w1, 16)
            sp.wait_ge(w_lo, 4)
            sp.dma_start(w2s[:, :, :], sw2.rearrange("(c p) d -> p c d", p=P)).then_inc(in_w2, 16)
            sp.wait_ge(zeroed, E + 3)
            for n in range(RT + 2):
                sp.dma_start(x_sent[n * TILE:(n + 1) * TILE].rearrange("(a p) c -> p a c", p=P),
                             zero.rearrange("p (a c) -> p a c", a=2)).then_inc(z_done, 16)
            for n in range(E, RT):
                sp.dma_start(y_sent[n * TILE:(n + 1) * TILE].rearrange("(a p) d -> p a d", p=P), y_sb[:, :, :]).then_inc(z_done, 16)

            def step(t, p, more):
                restack_keys(t + 1, 1 - p)
                if more:
                    sp.wait_ge(prep_mm, 7 * t + 5)
                    sp.wait_ge(neg_made, t + 1)
                    load_batch(t + 2, p)

            step(0, 0, True)
            with sp.Fori(0, B // 2 - 2) as i:
                step(2 * i + 1, 1, True)
                step(2 * i + 2, 0, True)
            step(B - 3, 1, True)
            step(B - 2, 0, False)

            sp.wait_ge(w1_lo, 1)
            sp.wait_ge(w2_lo, 1)
            load_weights(0)
            sp.wait_ge(av_made, 16 * B + AT_FREE)
            sp.dma_start(b2_bc, eb2.partition_broadcast(P)).then_inc(in_b2, 16)

            def load_tile(r):
                sp.dma_start(xin[:, :, :], x_sent[bass.ds(r * TILE, TILE)].rearrange("(a p) c -> p a c", p=P)).then_inc(x_in, 16)

            def store_tile(r):
                sp.wait_ge(xT_mm, r + 2)
                load_tile(r + 2)
                sp.wait_ge(y_made, 2 * r + 2 * ST + 4)
                sp.dma_start(y_sent[bass.ds(r * TILE, TILE)].rearrange("(a p) c -> p a c", p=P), y_sb[:, :, :]).then_inc(y_out, 16)

            load_weights(1)
            sp.wait_ge(scattered, 16 * 2 * NT)
            load_tile(0)
            sp.wait_ge(xT_mm, 1)
            load_tile(1)
            sp.wait_ge(tiles_made, 1)
            for e in range(E):
                first = sp.value_load(tile_of[0:1, e:e + 1], min_val=e, max_val=RT)
                end = sp.value_load(tile_of[0:1, e + 1:e + 2], min_val=e + 1, max_val=RT)
                if e + 2 < E:
                    load_weights(e + 2)
                with sp.Fori(first, end) as r:
                    store_tile(r)
            for i in range(NT):
                sp.wait_ge(mixed, i + 1)
                sp.dma_start(out_rows[i * P:(i + 1) * P], x_sb[:, i]).then_inc(out_done, 16)
            sp.wait_ge(out_done, 16 * NT)

        @block.gpsimd
        def _(pool):
            pool.memset(ident[:, :], 0.0).then_inc(consts, 1)
            pool.memset(tri[:, :], 0.0).then_inc(consts, 1)
            pool.memset(ones16[:, :], 1.0).then_inc(consts, 1)
            pool.wait_ge(consts, 3)
            pool.affine_select(out=ident[:, :], in_=ident[:, :], compare_op=ALU.not_equal, fill=1.0,
                               base=0, pattern=[[-1, P]], channel_multiplier=1).then_inc(consts, 1)
            pool.affine_select(out=tri[:, :], in_=tri[:, :], compare_op=ALU.is_ge, fill=1.0,
                               base=0, pattern=[[-1, P]], channel_multiplier=1).then_inc(consts, 1)
            for e in range(E):
                pool.memset(order[:, e:e + 1], float(E - e)).then_inc(zeroed, 1)
            pool.memset(before[:, :, :, :], 0.0).then_inc(zeroed, 1)
            pool.memset(est[:, :, :], 0.0).then_inc(zeroed, 1)
            pool.wait_ge(zeroed, E + 2)
            pool.wait_ge(consts, 5)
            pool.tensor_copy(ident16[:, :], ident[:, :]).then_inc(consts, 1)
            pool.memset(zero, 0.0).then_inc(zeroed, 1)
            pool.wait_ge(zeroed, E + 3)
            pool.memset(arena[32:64, :], 0.0).then_inc(zeroed, 1)
            pool.wait_ge(zeroed, E + 4)
            for w in (w1, w2):
                pool.memset(w[:, 1].rearrange("p a n c -> p (a n c)").bitcast(F32), 0.0).then_inc(zeroed, 1)

            def make_neg(b, p, n):
                loaded = pool.compute_val(16 * n)
                pool.wait_ge(consts, 6)
                pool.wait_ge(in_mask[p], loaded)
                pool.tensor_scalar(neg[:, p], mask_in[:, p], 1.0e9, -1.0e9, ALU.mult, ALU.add).then_inc(neg_made, 1)

            def take_queries(b, p):
                rows = slice(0, SLOT + STACK)
                pool.tensor_copy(qb[rows, p], q_stack[rows, :, bass.ds(b * S, S)]).then_inc(qb_made, 1)

            make_neg(0, 0, 1)
            pool.wait_ge(q_in, 96)
            take_queries(0, 0)
            make_neg(1, 1, 1)
            take_queries(1, 1)

            def step(t, p, n):
                done = pool.compute_val(16 * t + 16 + SC_FREE)
                pool.wait_ge(consts, 6)
                pool.wait_ge(sc_read, done)
                make_neg(t + 2, p, n)
                take_queries(t + 2, p)

            with pool.Fori(0, B // 2 - 1) as i:
                step(2 * i, 0, i + 2)
                step(2 * i + 1, 1, i + 2)

            pool.wait_ge(in_w1, 16)
            pool.tensor_copy(w1[:, 0, HI], w1s[:, :, :]).then_inc(w1_hi, 1)
            pool.wait_ge(in_w2, 16)
            pool.tensor_copy(w2[:, 0, HI], w2s[:, :, :]).then_inc(w2_hi, 1)

            def split_low(n, p):
                pool.wait_ge(w1_hi, n + 1)
                pool.tensor_tensor(w1[:, p, LO], w1s[:, :, :], w1[:, p, HI], ALU.subtract).then_inc(w1_lo, 1)
                pool.wait_ge(w2_hi, n + 1)
                pool.tensor_tensor(w2[:, p, LO], w2s[:, :, :], w2[:, p, HI], ALU.subtract).then_inc(w2_lo, 1)

            split_low(0, 0)
            for i in range(NT):
                pool.wait_ge(n2_made, i + 1)
                pool.wait_ge(n2_hi, i + 1)
                pool.tensor_tensor(xpair[:, i, D:2 * D], xn2[:, i], xpair[:, i, 0:D], ALU.subtract).then_inc(n2_lo, 1)
            split_low(1, 1)
            pool.wait_ge(n2_lo, NT)
            pool.wait_ge(slot_made, 1)
            pool.wait_ge(z_done, 16 * ZEROS)
            for i in range(NT):
                for j in range(2):
                    pool.indirect_dma_start(x_sent[:, :], bass.IndirectOffsetOnAxis(ap=slots[:, j, i:i + 1], axis=0),
                                            xpair[:, i], None).then_inc(scattered, 16)
            for n in range(2, E + 1):
                split_low(n, n % 2)

            pool.wait_ge(tiles_made, 1)
            last = pool.value_load(tile_of[0:1, E:E + 1], min_val=E, max_val=RT)
            stored = pool.compute_val(last * 16 + Y_FREE)
            pool.wait_ge(slot_made, 1)
            pool.wait_ge(y_out, stored)
            for i in range(NT):
                if i >= BACK:
                    pool.wait_ge(mixed, i - BACK + 1)
                for j in range(2):
                    pool.indirect_dma_start(back[:, i % BACK, j], None, y_sent[:, :],
                                            bass.IndirectOffsetOnAxis(ap=slots[:, j, i:i + 1], axis=0)
                                            ).then_inc(back_in[i % BACK], 16)

        @block.scalar
        def _(act):
            act.wait_ge(in_w, 64)
            for n in range(4):
                act.activation(wpair[:, n, HI], wstage[:, n], ACT.Copy, scale=0.25 if n == 0 else 1.0).then_inc(w_hi, 1)
            act.wait_ge(in_small, 16 * SMALLS)
            act.activation(bv_pair[:, HI], bv_in[:, :], ACT.Copy).then_inc(w_hi, 1)
            act.wait_ge(dve_ask, 1)
            act.activation(nrm[:, 1], nrm[:, 0], ACT.Sqrt).then_inc(act_gave, 1)
            act.activation(gates[:, :], gates[:, :], ACT.Tanh).then_inc(act_gave, 1)
            act.wait_ge(small_T, 1)
            act.activation(bcol[:, 0:2], bank(PR[0], P, 4)[:, 0:2], ACT.Copy, scale=0.25).then_inc(small_out, 1)
            act.activation(bcol[:, 2:4], bank(PR[0], P, 4)[:, 2:4], ACT.Copy).then_inc(small_out, 1)
            act.wait_ge(small_T, 2)
            act.activation(b1[:, :, :], bank(PR[1], P, NF * (E + 1)).rearrange("p (f e) -> p f e", f=NF), ACT.Copy).then_inc(small_out, 1)
            act.wait_ge(small_T, 3)
            act.activation(routerT[:, HI], bank(PT[0], P, ND * E).rearrange("p (c e) -> p c e", c=ND), ACT.Copy).then_inc(small_out, 1)
            for i in range(NT):
                act.wait_ge(xn_T, i + 1)
                act.activation(xnT[:, HI, :, i * P:(i + 1) * P], bank(SC[i % 2], P, D).rearrange("p (c t) -> p c t", c=ND),
                               ACT.Copy).then_inc(xn_hi, 1)
            for n in range(8):
                m, c = n % ND, n // ND
                act.wait_ge(q_mm, n + 1)
                act.activation(qT[:, HI, m, c * 4 * S:(c + 1) * 4 * S], bank(OB[n % 2], P, 4 * S), ACT.Identity,
                               bias=bcol[:, m:m + 1]).then_inc(q_hi, 1)

            def prep_piece(b, k, p):
                act.wait_ge(prep_mm, 7 * b + k + 1)
                if k < 2:
                    act.activation(ctxT[:, HI, k], bank(PR[k], P, S2), ACT.Copy).then_inc(prep_act, 1)
                elif k < 4:
                    if not (isinstance(b, int) and b == 0):
                        act.wait_ge(k_out, 32 * b)
                    act.activation(kT[:, HI, k - 2], bank(PR[k - 2], P, S2), ACT.Identity,
                                   bias=bcol[:, k:k + 1]).then_inc(prep_act, 1)
                elif k == 4:
                    act.activation(gpT[:, p], bank(PR[0], KP, KC * S).rearrange("p (c q) -> p c q", c=KC), ACT.Copy).then_inc(prep_act, 1)
                elif k == 5:
                    if isinstance(b, int) and b == 0:
                        act.wait_ge(zeroed, E + 6)
                    act.activation(head_columns(p, 0, 2), bank(PR[1], KP, 2 * D).rearrange("p (c h d) -> p c h d", c=2, h=H),
                                   ACT.Copy).then_inc(prep_act, 1)
                else:
                    act.activation(head_columns(p, 2, 3), bank(PR[0], KP, D).rearrange("p (c h d) -> p c h d", c=1, h=H),
                                   ACT.Copy).then_inc(prep_act, 1)

            def head_columns(p, first, end):
                return values_pad[p][:, first:end, 0:H * PAD].rearrange("p c (h e) -> p c h e", h=H)[:, :, :, DH:PAD]

            def turn_sums(t):
                act.wait_ge(rT_mm, t + 1)
                act.wait_ge(o_read, t + O_FREE)
                act.activation(rT[:, :, :], bank(PR[1], P, ND * S).rearrange("p (c q) -> p c q", c=ND), ACT.Copy).then_inc(rT_made, 1)

            def split_out(t):
                act.wait_ge(o_read, t + 1 + O_FREE)
                act.activation(oT[:, HI, :, bass.ds(t * S, S)], o32[:, :, :], ACT.Copy).then_inc(oT_hi, 1)

            for k in range(7):
                prep_piece(0, k, 0)

            def step(t, p, first=False, prep=True):
                act.wait_ge(rr_made, t + 1)
                for h in range(H):
                    act.wait_ge(sc_read, 16 * t + h + 1 + SC_FREE)
                    n = h % 4
                    act.activation(probs[:, n], probs[:, n], ACT.Exp, bias=negmax[:, p, h:h + 1], scale=-1.0,
                                   accum_out=rowsum[:, p, h:h + 1]).then_inc(exp_made, 1)
                    if prep and h in (1, 2, 5, 6, 8, 9, 10):
                        prep_piece(t + 1, (1, 2, 5, 6, 8, 9, 10).index(h), 1 - p)
                    if h == 11 and not first:
                        turn_sums(t - 1)
                    if h == 13 and not first:
                        split_out(t - 1)

            step(0, 0, first=True)
            with act.Fori(0, B // 2 - 1) as i:
                step(2 * i + 1, 1)
                step(2 * i + 2, 0)
            step(B - 1, 1, prep=False)
            turn_sums(B - 1)
            split_out(B - 1)

            act.wait_ge(dve_ask, 2)
            act.activation(nrm[:, 1], nrm[:, 0], ACT.Sqrt).then_inc(act_gave, 1)
            def turned(i):
                act.wait_ge(n2_T, i + 1)
                act.activation(x2T[:, :, :, i * P:(i + 1) * P].rearrange("p a c t -> p (a c) t"),
                               ps[:, i % 4, 0:D].bitcast(F16).rearrange("p (c t) -> p c t", t=P), ACT.Copy).then_inc(n2_Ts, 1)

            for i in range(NT):
                act.wait_ge(n2_made, i + 1)
                act.activation(xpair[:, i, 0:D], xn2[:, i], ACT.Copy).then_inc(n2_hi, 1)
                if i >= 2:
                    turned(i - 2)
            turned(NT - 2)
            turned(NT - 1)

            def split_high(n, p):
                act.wait_ge(in_w1, 16 * n + 16)
                act.activation(w1[:, p, HI], w1s[:, :, :], ACT.Copy).then_inc(w1_hi, 1)

            def activate(i, e):
                for f in range(NF):
                    act.wait_ge(h_mm, NF * i + (f | 1) + 1)
                    act.activation(hid32[:, f], ps[:, f // 2 % 4, f % 2 * TILE:(f % 2 + 1) * TILE], ACT.Relu,
                                   bias=b1[:, f, e:e + 1]).then_inc(h_relu, 1)

            def take_tile(r):
                act.wait_ge(xT_mm, r + 1)
                act.activation(xT[:, :, :], ps[:, 6, 0:2 * TILE].bitcast(F16).rearrange("p (c t) -> p c t", c=2 * ND),
                               ACT.Copy).then_inc(xT_made, 1)

            activate(0, E)
            split_high(1, 1)
            with act.Fori(1, ST) as i:
                activate(i, E)
            take_tile(0)
            act.wait_ge(dve_ask, 3)
            act.activation(top[:, 6:8], top[:, 6:8], ACT.Exp, scale=-1.0).then_inc(act_gave, 1)
            act.wait_ge(tiles_made, 1)
            for e in range(E):
                first = act.value_load(tile_of[0:1, e:e + 1], min_val=e, max_val=RT)
                end = act.value_load(tile_of[0:1, e + 1:e + 2], min_val=e + 1, max_val=RT)
                if e + 1 < E:
                    split_high(e + 2, e % 2)
                with act.Fori(first, end) as r:
                    activate(r + ST, e)
                    take_tile(r + 1)

        @block.tensor
        def _(pe):
            pe.wait_ge(consts, 6)
            pe.wait_ge(in_small, 16 * SMALLS)
            pe.transpose(bank(PR[0], P, 4), bcol_in[:, :], ident[0:4, 0:4]).then_inc(small_T, 1)
            for f in range(NF):
                mm = pe.transpose(ps[:, PR[1], f * (E + 1):(f + 1) * (E + 1)], b1_in[:, f * P:(f + 1) * P], ident[0:E + 1, 0:E + 1])
            mm.then_inc(small_T, 1)
            for c in range(ND):
                mm = pe.transpose(ps[:, PT[0], c * E:(c + 1) * E], r_in[:, c * P:(c + 1) * P], ident[0:E, 0:E])
            mm.then_inc(small_T, 1)

            for i in range(NT):
                pe.wait_ge(xn_made, i + 1)
                if i >= 2:
                    pe.wait_ge(xn_lo, i - 1)
                for c in range(ND):
                    mm = pe.transpose(ps[:, SC[i % 2], c * P:(c + 1) * P], xn[:, i % 2, c * P:(c + 1) * P], ident[:, :])
                mm.then_inc(xn_T, 1)
            pe.wait_ge(w_hi, 5)
            pe.wait_ge(w_lo, 5)
            pe.wait_ge(xn_hi, NT)
            pe.wait_ge(xn_lo, NT)
            for n in range(8):
                m, c = n % ND, n // ND
                if n >= 2:
                    pe.wait_ge(q_lo, n - 1)
                parts = [(w, a, k) for k in range(ND) for w, a in PASSES]
                for j, (w, a, k) in enumerate(parts):
                    mm = pe.matmul(bank(OB[n % 2], P, 4 * S), wpair[:, 0, w, k, m * P:(m + 1) * P],
                                   xnT[:, a, k, c * 4 * S:(c + 1) * 4 * S], start=(j == 0), stop=(j == len(parts) - 1))
                mm.then_inc(q_mm, 1)

            def prep_piece(b, k, p, n):
                first = isinstance(b, int) and b == 0
                if k == 0:
                    pe.wait_ge(in_ctx[p], 16 * n)
                    if not first:
                        pe.wait_ge(prep_act, 7 * b)
                    else:
                        pe.wait_ge(small_out, 4)
                if k == 1 and not (isinstance(b, int) and b < 2):
                    pe.wait_ge(rT_made, b - 2 + RT_FREE)
                if k < 2:
                    for c in range(KC):
                        mm = pe.transpose(ps[:, PR[k], c * KP:(c + 1) * KP], ctx_in[:, p, c, k * P:(k + 1) * P], ident[0:KP, 0:KP])
                elif k < 4:
                    pe.wait_ge(prep_lo, 4 * b + 2)
                    parts = [(w, a, kk) for kk in range(ND) for w, a in PASSES]
                    for j, (w, a, kk) in enumerate(parts):
                        mm = pe.matmul(bank(PR[k - 2], P, S2), wpair[:, 1, w, kk, (k - 2) * P:(k - 1) * P], ctxT[:, a, kk],
                                       start=(j == 0), stop=(j == len(parts) - 1))
                elif k == 4:
                    pe.wait_ge(in_gp[p], 16 * n)
                    pe.wait_ge(prep_lo, 4 * b + 3)
                    for c in range(KC):
                        mm = pe.transpose(ps[0:KP, PR[0], c * S:(c + 1) * S], gp_in[:, p, c * KP:(c + 1) * KP], ident[0:S, 0:S])
                else:
                    if k == 5:
                        pe.wait_ge(prep_lo, 4 * b + 4)
                    else:
                        pe.wait_ge(prep_act, 7 * b + 5)
                    for c in (0, 1) if k == 5 else (2,):
                        to = ps[0:KP, PR[6 - k], c % 2 * D:c % 2 * D + D]
                        for a in range(2):
                            pe.matmul(to, ones16[0:1, 0:KP], bv_pair[0:1, a], start=(a == 0), stop=False)
                        parts = [(a, w, kk) for kk in range(ND) for a, w in PASSES]
                        for j, (a, w, kk) in enumerate(parts):
                            mm = pe.matmul(to, ctxT[:, a, kk, c * KP:(c + 1) * KP], wpair[:, 2, w, kk],
                                           start=False, stop=(j == len(parts) - 1))
                mm.then_inc(prep_mm, 1)

            def turn_sums(t):
                pe.wait_ge(rr_made, t + 1 + O_FREE)
                pe.wait_ge(prep_act, 7 * t + 20 if not (isinstance(t, int) and t >= B - 2) else 7 * B)
                for c in range(ND):
                    mm = pe.transpose(ps[:, PR[1], c * S:(c + 1) * S], rrow[:, c * H // ND:(c + 1) * H // ND].rearrange("q h d -> q (h d)"),
                                      ident[0:S, 0:S])
                mm.then_inc(rT_mm, 1)

            def scores(t, h, p):
                if h == 0:
                    pe.wait_ge(k_in[p], kcount(t))
                    pe.wait_ge(qb_made, t + 1)
                pe.wait_ge(sc_read, 16 * t + h + 1)
                rows = slice(h % 2 * SLOT, h % 2 * SLOT + STACK)
                pe.matmul(bank(SC[h % 2], S, S2), qb[rows, p, h // 2], kst[rows, p, h // 2], start=True, stop=True).then_inc(sc_made, 1)

            def kcount(t):
                return (t // 2 + 1) * 96 if isinstance(t, int) else t * 48 + 0

            def turn_probs(t, h):
                pe.wait_ge(exp_made, 16 * t + h + 1)
                pe.wait_ge(pt_read, 16 * t + h + 1)
                for c in range(KC):
                    mm = pe.transpose(ps[0:KP, PT[h % 2], c * S:(c + 1) * S], probs[:, h % 4, c * KP:(c + 1) * KP], ident[0:S, 0:S])
                mm.then_inc(pt_made, 1)

            def values(t, h, p):
                if h == 0:
                    pe.wait_ge(o_read, t + 1)
                    pe.wait_ge(prep_act, 7 * t + 7)
                pe.wait_ge(pt_read, 16 * t + h + 1 + PT_FREE)
                row, cols = h % (H // ND) // 2 * PAD, slice(h // (H // ND) * S, (h // (H // ND) + 1) * S)
                first = h * PAD + (DH if h % 2 == 0 else 0)
                for c in range(KC):
                    mm = pe.matmul(ps[row:row + PAD, OB[p], cols], values_pad[p][:, c, first:first + PAD], probsT[:, h % 2, c],
                                   start=(h % 2 == 0 and c == 0), stop=(h % 2 == 1 and c == KC - 1))
                mm.then_inc(av_made, 1)

            pe.sem_inc(pt_made, PROBS_FREE)
            pe.sem_inc(av_made, AT_FREE)
            for k in range(7):
                prep_piece(0, k, 0, 1)
            for h in range(3):
                scores(0, h, 0)

            def step(t, p, n, tk, first=False, prep=True):
                for h in range(H):
                    turn_probs(t, h)
                    if h + 3 < H:
                        scores(t, h + 3, p)
                    elif prep:
                        if h + 3 == H:
                            pe.wait_ge(k_in[1 - p], tk)
                        scores_next(t + 1, h + 3 - H, 1 - p)
                    if h > 0:
                        values(t, h - 1, p)
                    elif not first:
                        values(t - 1, H - 1, 1 - p)
                    if prep and h in (0, 1, 4, 5, 7, 8, 9):
                        prep_piece(t + 1, (0, 1, 4, 5, 7, 8, 9).index(h), 1 - p, n)
                    if h == 10 and not first:
                        turn_sums(t - 1)

            def scores_next(t, h, p):
                if h == 0:
                    pe.wait_ge(qb_made, t + 1)
                pe.wait_ge(sc_read, 16 * t + h + 1)
                rows = slice(h % 2 * SLOT, h % 2 * SLOT + STACK)
                pe.matmul(bank(SC[h % 2], S, S2), qb[rows, p, h // 2], kst[rows, p, h // 2], start=True, stop=True).then_inc(sc_made, 1)

            step(0, 0, 1, 96, first=True)
            with pe.Fori(0, B // 2 - 1) as i:
                step(2 * i + 1, 1, i + 2, i * 96 + 192)
                step(2 * i + 2, 0, i + 2, i * 96 + 192)
            step(B - 1, 1, None, None, prep=False)
            values(B - 1, H - 1, 1)
            pe.wait_ge(rT_made, B - 1 + RT_FREE)
            turn_sums(B - 1)

            pe.wait_ge(oT_hi, B)
            pe.wait_ge(oT_lo, B)
            for i in range(NT):
                if i >= 2:
                    pe.wait_ge(x2_made, i - 1)
                parts = [(a, w, k) for k in range(ND) for a, w in PASSES]
                for j, (a, w, k) in enumerate(parts):
                    mm = pe.matmul(bank(OB[i % 2], P, D), oT[:, a, k, i * P:(i + 1) * P], wpair[:, 3, w, k],
                                   start=(j == 0), stop=(j == len(parts) - 1))
                mm.then_inc(pj_mm, 1)

            def route(i):
                pe.wait_ge(n2_Ts, i + 1)
                parts = [(a, w, k) for k in range(ND) for a in range(2) for w in range(2)]
                for j, (a, w, k) in enumerate(parts):
                    mm = pe.matmul(ps[:, PR[1], P + i * E:P + (i + 1) * E], x2T[:, a, k, i * P:(i + 1) * P], routerT[:, w, k],
                                   start=(j == 0), stop=(j == len(parts) - 1))
                mm.then_inc(rl_mm, 1)

            for i in range(NT):
                pe.wait_ge(n2_hi, i + 1)
                pe.wait_ge(n2_lo, i + 1)
                if i >= 4:
                    pe.wait_ge(n2_Ts, i - 3)
                for c in range(2 * ND):
                    mm = pe.transpose(ps[:, i % 4, 0:D].bitcast(F16)[:, c * P:(c + 1) * P], xpair[:, i, c * P:(c + 1) * P], ident16[:, :])
                mm.then_inc(n2_T, 1)
                if i >= 3:
                    route(i - 3)
            for i in range(NT - 3, NT):
                route(i)

            def turn_tile(r):
                pe.wait_ge(x_in, 16 * r + 16)
                for a in range(TILE // P):
                    for c in range(2 * ND):
                        mm = pe.transpose(ps[:, 6, 0:2 * TILE].bitcast(F16)[:, c * TILE + a * P:c * TILE + (a + 1) * P],
                                          xin[:, a, c * P:(c + 1) * P], ident16[:, :])
                mm.then_inc(xT_mm, 1)

            def hidden(p, rows):
                for f in range(NF):
                    parts = [(w, a, k) for k in range(ND) for w, a in PASSES]
                    for j, (w, a, k) in enumerate(parts):
                        mm = pe.matmul(ps[:, f // 2 % 4, f % 2 * TILE:(f % 2 + 1) * TILE], w1[:, p, w, k, f * P:(f + 1) * P],
                                       rows(a, k), start=(j == 0), stop=(j == len(parts) - 1))
                    mm.then_inc(h_mm, 1)

            def results(i, p):
                for a in range(TILE // P):
                    pe.wait_ge(y_made, 2 * i + a + 1)
                    for f in range(NF):
                        if a == 0 and f % 2 == 0:
                            pe.wait_ge(h_split, (NF // 2) * i + f // 2 + 1)
                        for j, (u, w) in enumerate(PASSES):
                            mm = pe.matmul(ps[:, 4 + a, 0:D], hid[:, u, f, a * P:(a + 1) * P], w2[:, p, w, f],
                                           start=(f == 0 and j == 0), stop=(f == NF - 1 and j == 2))
                    mm.then_inc(y_mm, 1)

            def shared_tile(i):
                hidden(0, lambda a, k: x2T[:, a, k, bass.ds(i * TILE, TILE)])
                if isinstance(i, int) and i == 0:
                    rank_pairs()
                if isinstance(i, int) and i == ST - 1:
                    turn_tile(0)
                results(i, 0)

            def rank_pairs():
                pe.wait_ge(cnt_made, 1)
                rk = bank(PR[1], P, NT * E)
                pe.matmul(rk, tri[:, :], count16[:, 0].rearrange("p i e -> p (i e)"), start=True, stop=False)
                pe.matmul(rk, ones16[:, :], count16[:, 1].rearrange("p i e -> p (i e)"), start=False, stop=True).then_inc(rank_mm, 1)
                pe.matmul(ps[:, PR[1], NT * E:(NT + 1) * E], ones16[:, :], count16[:, 2, 0], start=True, stop=True).then_inc(rank_mm, 1)

            pe.wait_ge(w1_lo, 1)
            pe.wait_ge(w2_lo, 1)
            shared_tile(0)
            with pe.Fori(1, ST - 1) as i:
                shared_tile(i)
            shared_tile(ST - 1)
            pe.wait_ge(tiles_made, 1)
            for e in range(E):
                first = pe.value_load(tile_of[0:1, e:e + 1], min_val=e, max_val=RT)
                end = pe.value_load(tile_of[0:1, e + 1:e + 2], min_val=e + 1, max_val=RT)
                p = (e + 1) % 2
                pe.wait_ge(w1_lo, e + 2)
                pe.wait_ge(w2_lo, e + 2)
                with pe.Fori(first, end) as r:
                    pe.wait_ge(xT_made, r + 1)
                    hidden(p, lambda a, k: xT[:, a * ND + k])
                    turn_tile(r + 1)
                    results(r + ST, p)

        @block.vector
        def _(dve):
            steps = [0]

            def then(ins):
                steps[0] += 1
                ins.then_inc(dve_step, 1)
                dve.wait_ge(dve_step, steps[0])

            def inverse_root(gave):
                dve.wait_ge(act_gave, gave)
                then(dve.reciprocal(nrm[:, 3], nrm[:, 1]))
                then(dve.tensor_tensor(nrm[:, 3], nrm[:, 3], nrm[:, 0], ALU.mult))
                then(dve.tensor_tensor(nrm[:, 3], nrm[:, 3], nrm[:, 1], ALU.add))
                then(dve.tensor_scalar(nrm[:, 3], nrm[:, 3], 0.5, None, ALU.mult))
                then(dve.reciprocal(nrm[:, 2], nrm[:, 3]))

            dve.wait_ge(in_x, 16)
            for i in range(NT):
                last = dve.bn_stats(stats[:, i], x_sb[:, i])
            then(last)
            for i in range(NT):
                last = dve.bn_aggr(mv[:, i], stats[:, i])
            then(last)
            dve.tensor_scalar(nrm[:, 0], mv[:, :, 1], LN_EPS, None, ALU.add).then_inc(dve_ask, 1)
            dve.wait_ge(w_hi, 4)
            dve.scalar_tensor_tensor(wpair[:, 0, LO], wstage[:, 0], 0.25, wpair[:, 0, HI], ALU.mult, ALU.subtract).then_inc(w_lo, 1)
            for n in range(1, 4):
                dve.tensor_tensor(wpair[:, n, LO], wstage[:, n], wpair[:, n, HI], ALU.subtract).then_inc(w_lo, 1)
            dve.wait_ge(w_hi, 5)
            dve.tensor_tensor(bv_pair[:, LO], bv_in[:, :], bv_pair[:, HI], ALU.subtract).then_inc(w_lo, 1)
            inverse_root(1)

            def lo_part(i):
                dve.wait_ge(xn_hi, i + 1)
                cols = slice(i * P, (i + 1) * P)
                dve.tensor_tensor(xnT[:, LO, :, cols], bank(SC[i % 2], P, D).rearrange("p (c t) -> p c t", c=ND),
                                  xnT[:, HI, :, cols], ALU.subtract).then_inc(xn_lo, 1)

            for i in range(NT):
                if i >= 2:
                    dve.wait_ge(xn_T, i - 1)
                dve.tensor_scalar(xn[:, i % 2], x_sb[:, i], mv[:, i, 0:1], nrm[:, 2, i:i + 1], ALU.subtract, ALU.mult).then_inc(xn_made, 1)
                if i >= 1:
                    lo_part(i - 1)
            lo_part(NT - 1)
            dve.wait_ge(small_out, 4)
            dve.tensor_tensor(routerT[:, LO], bank(PT[0], P, ND * E).rearrange("p (c e) -> p c e", c=ND), routerT[:, HI], ALU.subtract).then_inc(w_lo, 1)
            for n in range(8):
                m, c = n % ND, n // ND
                dve.wait_ge(q_hi, n + 1)
                cols = slice(c * 4 * S, (c + 1) * 4 * S)
                dve.scalar_tensor_tensor(qT[:, LO, m, cols], bank(OB[n % 2], P, 4 * S), bcol[:, m:m + 1], qT[:, HI, m, cols],
                                         ALU.add, ALU.subtract).then_inc(q_lo, 1)
            dve.wait_ge(act_gave, 2)
            then(dve.tensor_scalar(bo_bc[:, :], bo_bc[:, :], gates[:, 0:1], None, ALU.mult))
            dve.tensor_tensor(x_sb[:, :, :], x_sb[:, :, :], bo_bc[:, :].unsqueeze(1).to_broadcast([P, NT, D]), ALU.add).then_inc(resid, 1)

            dve.sem_inc(sc_read, SC_FREE)
            dve.sem_inc(pt_read, PT_FREE)
            dve.sem_inc(o_read, O_FREE)
            dve.sem_inc(rr_made, O_FREE)
            dve.sem_inc(rT_made, RT_FREE)

            def prep_lo_part(b, k):
                dve.wait_ge(prep_act, 7 * b + k + 1)
                if k < 2:
                    dve.tensor_tensor(ctxT[:, LO, k], bank(PR[k], P, S2), ctxT[:, HI, k], ALU.subtract).then_inc(prep_lo, 1)
                else:
                    dve.scalar_tensor_tensor(kT[:, LO, k - 2], bank(PR[k - 2], P, S2), bcol[:, k:k + 1], kT[:, HI, k - 2],
                                             ALU.add, ALU.subtract).then_inc(prep_lo, 1)

            def mask_scores(t, h, p):
                if h == 0:
                    dve.wait_ge(neg_made, t + 1)
                head = dve.compute_val(16 * t + h + 1)
                dve.wait_ge(neg_made, 1)
                dve.wait_ge(sc_made, head)
                dve.wait_ge(pt_made, head)
                dve.tensor_tensor_reduce(probs[:, h % 4], bank(SC[h % 2], S, S2), neg[:, p], -1.0, BIG, ALU.add, ALU.min,
                                         negmax[:, p, h:h + 1]).then_inc(sc_read, 1)

            def weigh(t, h, p):
                dve.wait_ge(pt_made, 16 * t + h + 1 + PROBS_FREE)
                dve.wait_ge(av_made, 16 * t + h + 1)
                dve.tensor_tensor(probsT[:, h % 2], bank(PT[h % 2], KP, KC * S).rearrange("p (c q) -> p c q", c=KC),
                                  gpT[:, p], ALU.mult).then_inc(pt_read, 1)

            def invert_sums(t, p):
                dve.wait_ge(exp_made, 16 * t + 16)
                if not (isinstance(t, int) and t == 0):
                    dve.wait_ge(rT_mm, t)
                dve.reciprocal(rinv[:, :], rowsum[:, p]).then_inc(ri_made, 1)
                dve.wait_ge(ri_made, t + 1)
                dve.tensor_copy(rrow[:, :, :], rinv[:, :].unsqueeze(2).to_broadcast([S, H, DH])).then_inc(rr_made, 1)

            def divide(t, p):
                dve.wait_ge(av_made, 16 * t + 16 + AT_FREE)
                dve.wait_ge(rT_made, t + 1 + RT_FREE)
                dve.tensor_tensor(o32[:, :, :], bank(OB[p], P, ND * S).rearrange("p (c q) -> p c q", c=ND), rT[:, :, :],
                                  ALU.mult).then_inc(o_read, 1)

            def split_out(t):
                dve.wait_ge(oT_hi, t + 1)
                cols = bass.ds(t * S, S)
                dve.tensor_tensor(oT[:, LO, :, cols], o32[:, :, :], oT[:, HI, :, cols], ALU.subtract).then_inc(oT_lo, 1)

            for k in range(4):
                prep_lo_part(0, k)
            mask_scores(0, 0, 0)
            mask_scores(0, 1, 0)

            def step(t, p, first=False, prep=True):
                for h in range(H):
                    if h + 2 < H:
                        mask_scores(t, h + 2, p)
                    elif prep:
                        mask_scores(t + 1, h + 2 - H, 1 - p)
                    weigh(t, h, p)
                    if prep and h in (2, 3, 6, 7):
                        prep_lo_part(t + 1, (2, 3, 6, 7).index(h))
                    if h == 4 and not first:
                        invert_sums(t - 1, 1 - p)
                    if h == 12 and not first:
                        divide(t - 1, 1 - p)
                    if h == 14 and not first:
                        split_out(t - 1)

            step(0, 0, first=True)
            with dve.Fori(0, B // 2 - 1) as i:
                step(2 * i + 1, 1)
                step(2 * i + 2, 0)
            step(B - 1, 1, prep=False)
            invert_sums(B - 1, 1)
            divide(B - 1, 1)
            split_out(B - 1)

            for i in range(NT):
                dve.wait_ge(pj_mm, i + 1)
                if i == 0:
                    dve.wait_ge(resid, 1)
                dve.scalar_tensor_tensor(x_sb[:, i], bank(OB[i % 2], P, D), gates[:, 0:1], x_sb[:, i], ALU.mult, ALU.add).then_inc(x2_made, 1)
                if i >= 1:
                    dve.wait_ge(x2_made, i)
                    dve.bn_stats(stats[:, i - 1], x_sb[:, i - 1])
            dve.wait_ge(x2_made, NT)
            then(dve.bn_stats(stats[:, NT - 1], x_sb[:, NT - 1]))
            for i in range(NT):
                last = dve.bn_aggr(mv[:, i], stats[:, i])
            then(last)
            then(dve.tensor_scalar(nrm[:, 4], mv[:, :, 1], LN_EPS, RMS_EPS, ALU.add, ALU.mult))
            dve.tensor_tensor(nrm[:, 0], nrm[:, 4], mv[:, :, 1], ALU.add).then_inc(dve_ask, 1)
            inverse_root(3)
            for i in range(NT):
                dve.tensor_scalar(xn2[:, i], x_sb[:, i], mv[:, i, 0:1], nrm[:, 2, i:i + 1], ALU.subtract, ALU.mult).then_inc(n2a, 1)
                dve.wait_ge(n2a, i + 1)
                dve.tensor_tensor(xn2[:, i], xn2[:, i], nw_bc[:, :], ALU.mult).then_inc(n2_made, 1)

            dve.wait_ge(rl_mm, NT)
            dve.wait_ge(zeroed, E + 2)
            logit = ps[:, PR[1], P:P + NT * E].rearrange("p (i e) -> p i e", e=E)

            def spread(col):
                return col.unsqueeze(2).to_broadcast([P, NT, E])

            def choose(src, n):
                then(dve.tensor_reduce(top[:, n], src, AX.X, ALU.max))
                then(dve.tensor_tensor(rt[:, 3], src, spread(top[:, n]), ALU.is_equal))
                then(dve.tensor_tensor(rt[:, 3], rt[:, 3], order[:, :].unsqueeze(1).to_broadcast([P, NT, E]), ALU.mult))
                then(dve.tensor_reduce(top[:, 2], rt[:, 3], AX.X, ALU.max))
                then(dve.tensor_tensor(rt[:, n], rt[:, 3], spread(top[:, 2]), ALU.is_equal))

            def running(buf, n, pad, steps):
                for k in range(steps):
                    src, to = buf(k % 2), buf((k + 1) % 2)
                    then(dve.tensor_tensor(to[:, pad:pad + n], src[:, pad:pad + n], src[:, pad - 2 ** k:pad - 2 ** k + n], ALU.add))

            choose(logit, 0)
            then(dve.scalar_tensor_tensor(rt[:, 2], rt[:, 0], -BIG, logit, ALU.mult, ALU.add))
            choose(rt[:, 2], 1)
            then(dve.tensor_tensor(before[:, 0, NTP:NTP + NT], rt[:, 0], rt[:, 1], ALU.add))
            then(dve.tensor_copy(count16[:, 0], before[:, 0, NTP:NTP + NT]))
            running(lambda k: before[:, k], NT, NTP, 4)
            then(dve.tensor_copy(count16[:, 1], before[:, 0, NTP - 1:NTP - 1 + NT]))
            dve.tensor_copy(count16[:, 2, 0], before[:, 0, NTP + NT - 1]).then_inc(cnt_made, 1)

            def place_pairs():
                dve.wait_ge(rank_mm, 2)
                then(dve.tensor_scalar(est_i[:, 0, :], ps[:, PR[1], NT * E:(NT + 1) * E], 1.0, float(TILE - 1), ALU.max, ALU.add))
                then(dve.tensor_scalar(est_i[:, 1, :], est_i[:, 0, :], TILE.bit_length() - 1, None, ALU.arith_shift_right))
                then(dve.tensor_copy(est[:, 0, E:2 * E], est_i[:, 1, :]))
                running(lambda k: est[:, k], E, E, 3)
                dve.tensor_copy(tile_of[:, 0:E + 1], est[:, 1, E - 1:2 * E]).then_inc(tiles_made, 1)
                then(dve.tensor_scalar(est[:, 4, 0:E], est[:, 1, E - 1:2 * E - 1], float(TILE), None, ALU.mult))
                then(dve.tensor_tensor(rt[:, 4], bank(PR[1], P, NT * E).rearrange("p (i e) -> p i e", e=E),
                                       est[:, 4, 0:E].unsqueeze(1).to_broadcast([P, NT, E]), ALU.add))
                then(dve.tensor_tensor(rt[:, 2:4], rt[:, 0:2], rt[:, 4].unsqueeze(1).to_broadcast([P, 2, NT, E]), ALU.mult))
                then(dve.tensor_reduce(top[:, 4:6], rt[:, 2:4], AX.X, ALU.add))
                dve.tensor_copy(slots[:, :, :], top[:, 4:6]).then_inc(slot_made, 1)
                dve.tensor_copy(top[:, 6:8], top[:, 0:2]).then_inc(dve_ask, 1)

            dve.sem_inc(y_made, 2)
            dve.sem_inc(y_out, Y_FREE)

            def split_hidden(i):
                for g in range(NF // 2):
                    two = slice(2 * g, 2 * g + 2)
                    dve.wait_ge(h_relu, NF * i + 2 * g + 2)
                    dve.tensor_copy(hid[:, HI, two], hid32[:, two]).then_inc(h_hi, 1)
                    dve.wait_ge(h_hi, (NF // 2) * i + g + 1)
                    dve.tensor_tensor(hid[:, LO, two], hid32[:, two], hid[:, HI, two], ALU.subtract).then_inc(h_split, 1)

            def split_high(n, p):
                dve.wait_ge(in_w2, 16 * n + 16)
                dve.tensor_copy(w2[:, p, HI], w2s[:, :, :]).then_inc(w2_hi, 1)

            def shared_tile(i):
                split_hidden(i)
                for a in range(TILE // P):
                    dve.wait_ge(y_mm, 2 * i + a + 1)
                    row = bass.ds(2 * i + a, 1)
                    dve.scalar_tensor_tensor(x_sb[:, row].rearrange("p a d -> p (a d)"), ps[:, 4 + a, 0:D], gates[:, 1:2],
                                             x_sb[:, row].rearrange("p a d -> p (a d)"), ALU.mult, ALU.add).then_inc(y_made, 1)

            then(dve.tensor_scalar(sb2_bc[:, :], sb2_bc[:, :], gates[:, 1:2], None, ALU.mult))
            shared_tile(0)
            place_pairs()
            split_high(1, 1)
            then(dve.tensor_tensor(x_sb[:, :, :], x_sb[:, :, :], sb2_bc[:, :].unsqueeze(1).to_broadcast([P, NT, D]), ALU.add))
            with dve.Fori(1, ST) as i:
                shared_tile(i)
            dve.wait_ge(act_gave, 4)
            then(dve.tensor_scalar(top[:, 6:8], top[:, 6:8], 1.0, None, ALU.add))
            then(dve.reciprocal(top[:, 6:8], top[:, 6:8]))
            then(dve.tensor_tensor(top[:, 8], top[:, 6], top[:, 7], ALU.add))
            then(dve.tensor_scalar(top[:, 8], top[:, 8], 1e-6, None, ALU.add))
            then(dve.reciprocal(top[:, 9], top[:, 8]))
            then(dve.tensor_scalar(top[:, 9], top[:, 9], gates[:, 1:2], None, ALU.mult))
            then(dve.tensor_tensor(top[:, 6:8], top[:, 6:8], top[:, 9].unsqueeze(1).to_broadcast([P, 2, NT]), ALU.mult))

            dve.wait_ge(z_done, 16 * ZEROS)
            dve.wait_ge(in_b2, 16)
            dve.wait_ge(tiles_made, 1)
            for e in range(E):
                first = dve.value_load(tile_of[0:1, e:e + 1], min_val=e, max_val=RT)
                end = dve.value_load(tile_of[0:1, e + 1:e + 2], min_val=e + 1, max_val=RT)
                if e + 1 < E:
                    split_high(e + 2, e % 2)
                with dve.Fori(first, end) as r:
                    split_hidden(r + ST)
                    dve.wait_ge(y_out, 16 * r + Y_FREE)
                    for a in range(TILE // P):
                        dve.wait_ge(y_mm, 2 * r + 2 * ST + a + 1)
                        dve.tensor_tensor(y_sb[:, a], ps[:, 4 + a, 0:D], b2_bc[:, e], ALU.add).then_inc(y_made, 1)

            for i in range(NT):
                p = i % BACK
                dve.wait_ge(back_in[p], 32 * (i // BACK + 1))
                then(dve.scalar_tensor_tensor(x_sb[:, i], back[:, p, 0], top[:, 6, i:i + 1], x_sb[:, i], ALU.mult, ALU.add))
                dve.scalar_tensor_tensor(x_sb[:, i], back[:, p, 1], top[:, 7, i:i + 1], x_sb[:, i], ALU.mult, ALU.add).then_inc(mixed, 1)


_INS = ['x', 'ctx_1024', 'fside_BxSxS2_0', 'mask_BxSxS2_ik1', 'g_xattn', 'g_ffn', 'L0_xattn_wq_k', 'L0_xattn_wq_b',
        'L0_xattn_wk_k', 'L0_xattn_wk_b', 'L0_xattn_wv_k', 'L0_xattn_wv_b', 'L0_xattn_wo_k', 'L0_xattn_wo_b',
        'L0_ffn_norm_weight', 'L0_ffn_router_w', 'L0_ffn_sw1', 'L0_ffn_sb1', 'L0_ffn_sw2', 'L0_ffn_sb2',
        'L0_ffn_ew1', 'L0_ffn_eb1', 'L0_ffn_ew2', 'L0_ffn_eb2']
_OUTS = [((B, S, D), 'float32')]


def kernel(**inputs):
    import numpy as _np
    import concourse.bacc as _bacc
    from concourse import mybir as _mybir
    from concourse.bass_utils import run_bass_kernel_spmd as _run

    nc = _bacc.Bacc("TRN2", target_bir_lowering=False, num_devices=1)
    arrays, args = {}, []
    for name in _INS:
        a = _np.ascontiguousarray(inputs[name])
        arrays[f"in_{name}_dram"] = a
        args.append(nc.dram_tensor(f"in_{name}_dram", a.shape, _mybir.dt.from_np(a.dtype), kind="ExternalInput").ap())
    for i, (shape, dtype) in enumerate(_OUTS):
        dt = _mybir.dt.from_np(_np.dtype(dtype))
        args.append(nc.dram_tensor(f"out_{i}_dram", shape, dt, kind="ExternalOutput").ap())
    flamingo_block(nc, *args)
    r = _run(nc, [arrays], core_ids=[0])
    got = tuple(r.results[0][f"out_{i}_dram"] for i in range(len(_OUTS)))
    return got[0]
```

```python
from contextlib import ExitStack

import concourse.bass as bass
from concourse import mybir

F32, F16, I32 = mybir.dt.float32, mybir.dt.float16, mybir.dt.int32
ALU = mybir.AluOpType
ACT = mybir.ActivationFunctionType
AX = mybir.AxisListType

P = 128
B, S, D = 16, 112, 256
S2, H = 375, 16
DH = D // H
T = B * S
NT = T // P
NTP = 8
KC = 3
KP = S2 // KC
ND = D // P
E, F = 8, 1024
NF = F // P
TILE = 256
ST = T // TILE
RT = (2 * T + E * (TILE - 1)) // TILE
ZT = -(-(RT + 2) // (B - 2))
ROWS = ZT * (B - 2) * TILE
assert ROWS >= (RT + 2) * TILE
RW = 2 * D + 4
YPAD = 4
YROWS = YPAD + 2 * T
SMALLS = 9
PROBS = 8
PREP = 4
BIAS_TILES = 2
LEAD = 3
ZEROS = B - 2
QB = 4
QC = B // QB
Q_TILES = [range(-(-c * QB * S // P), -(-(c + 1) * QB * S // P)) for c in range(QC)]
W_ORDER = (1, 0, 2, 3)
HI, LO = 0, 1
PASSES = ((HI, HI), (HI, LO), (LO, HI))
ORDER = [h + d for h in range(0, H, 4) for d in (0, 2, 1, 3)]
SLOT = 64
STACK = 3 * DH
Q_PARTS, K_PARTS = (HI, LO, HI), (HI, HI, LO)
BACK = 2
LN_EPS, RMS_EPS = 1e-5, 1e-8
BIG = 3.0e38


def flamingo_block(nc, x, ctx, gp, mask, g_xattn, g_ffn, wq, bq, wk, bk, wv, bv, wo, bo, nw, router,
                   sw1, sb1, sw2, sb2, ew1, eb1, ew2, eb2, out):
    x_rows = x.rearrange("b s d -> (b s) d")
    out_rows = out.rearrange("b s d -> (b s) d")
    k_scratch = nc.dram_tensor("k_scratch", (B, H, STACK, S2), F16, kind="Internal").ap()
    q_scratch = nc.dram_tensor("q_scratch", (H, STACK, T), F16, kind="Internal").ap()
    x_sent = nc.dram_tensor("x_sent", (ROWS, RW), F16, kind="Internal").ap()
    y_back = nc.dram_tensor("y_back", (YROWS, D), F32, kind="Internal").ap()

    with ExitStack() as st:
        def sb(name, shape, dt):
            return st.enter_context(nc.sbuf_tensor(name, shape, dt))

        def sem(name):
            return st.enter_context(nc.semaphore(name))

        x_sb = sb("x_sb", [P, NT, D], F32)
        xnT = sb("xnT", [P, 2, ND, T], F16)
        oT = xnT
        x2T = xnT
        qT_all = sb("qT", [P, max(2 * ND * T, NT * RW)], F16)
        qT = qT_all[:, 0:2 * ND * T].rearrange("p (a b t) -> p a b t", a=2, b=ND)
        xpair = qT_all[:, 0:NT * RW].rearrange("p (i c) -> p i c", i=NT)
        xwords = qT_all[:, 0:NT * RW].bitcast(F32).rearrange("p (i c) -> p i c", i=NT)[:, :, D:D + 2]
        arena = sb("arena", [P, H // 2 * T // 2], F32)
        q_stack = arena[:, :].bitcast(F16).rearrange("p (j t) -> p j t", j=H // 2)
        hid32 = arena[:, 0:NF * TILE].rearrange("p (f n) -> p f n", f=NF)
        hid = arena[:, NF * TILE:2 * NF * TILE].bitcast(F16).rearrange("p (a f n) -> p a f n", a=2, f=NF)
        back = arena[:, 0:NT * 2 * D].rearrange("p (i c d) -> p i c d", i=NT, c=2)
        xn2 = arena[:, 0:NT * D].rearrange("p (i d) -> p i d", i=NT)
        qb = sb("qb", [P, 2, H // 2, S], F16)
        kst_all = sb("kst", [P, H * S2], F16)
        kst = kst_all[:, :].rearrange("p (a j k) -> p a j k", a=2, j=H // 2)
        kT = sb("kT", [P, 2, ND, S2], F16)
        ctx_in = sb("ctx_in", [KP, 2, KC, D], F32)
        ctx_pair = sb("ctx_pair", [KP, 2, KC, D], F16)
        ctxT = sb("ctxT", [P, 2, ND, S2], F16)
        mask_in = sb("mask_in", [S, 2, S2], I32)
        neg = sb("neg", [S, 2, S2], F32)
        gp_in = sb("gp_in", [S, 2, S2], F32)
        gpT = sb("gpT", [KP, 2, KC, S], F32)
        probs_all = sb("probs", [P, PROBS * S2], F32)
        probs = probs_all[0:S].rearrange("p (n k) -> p n k", n=PROBS)
        xin = probs_all[:, :].bitcast(F16)[:, 0:TILE // P * RW].rearrange("p (a c) -> p a c", c=RW)
        xT = probs_all[:, :].bitcast(F16)[:, TILE // P * RW:TILE // P * RW + 2 * ND * TILE].rearrange("p (k n) -> p k n", n=TILE)
        probsT = sb("probsT", [KP, 4, KC, S], F32)
        negmax = sb("negmax", [S, 2, H], F32)
        rowsum = sb("rowsum", [S, 2, H], F32)
        rinv = sb("rinv", [S, H], F32)
        rrow = sb("rrow", [S, H, DH], F32)
        rT = sb("rT", [P, ND, S], F32)
        o32 = sb("o32", [P, ND, S], F32)
        wpair = sb("wpair", [P, 4, 2, ND, D], F16)
        bcol_in = sb("bcol_in", [4, P], F32)
        bcol = sb("bcol", [P, 4], F32)
        bv_in = sb("bv_in", [1, D], F32)
        bv_pair = sb("bv_pair", [1, 2, D], F16)
        bo_bc = sb("bo_bc", [P, D], F32)
        nw_bc = sb("nw_bc", [P, D], F32)
        b1 = sb("b1", [P, NF, E + 1], F32)
        sb2_bc = sb("sb2_bc", [P, D], F32)
        b2_bc = kst_all[:, :].bitcast(F32)[:, 0:E * D].rearrange("p (e d) -> p e d", e=E)
        r_in = sb("r_in", [E, D], F32)
        routerT = sb("routerT", [P, 2, ND, E], F16)
        gates = sb("gates", [P, 2], F32)
        ident = sb("ident", [P, P], F32)
        ident16 = sb("ident16", [P, P], F16)
        tri = sb("tri", [P, P], F16)
        ones16 = sb("ones16", [P, P], F16)
        stats = sb("stats", [P, NT, 6], F32)
        mv = sb("mv", [P, NT, 2], F32)
        nrm = sb("nrm", [P, 8, NT], F32)
        rt = sb("rt", [P, 6, NT, E], F32)
        order = sb("order", [P, E], F32)
        before = sb("before", [P, 2, NTP + NT, E], F32)
        top = sb("top", [P, 10, NT], F32)
        count16 = sb("count16", [P, 3, NT, E], F16)
        est = sb("est", [P, 6, E + E], F32)
        est_i = sb("est_i", [P, 2, E], I32)
        tile_of = sb("tile_of", [P, E + 2], I32)
        token_row = sb("token_row", [P, NT], I32)
        words = sb("words", [P, TILE // P, 2], F32)
        dest = sb("dest", [P, TILE // P], I32)
        slots = sb("slots", [P, 2, NT], I32)
        w1s = sb("w1s", [P, ND, F], F32)
        w2s = sb("w2s", [P, NF, D], F32)
        wstage = w2s[:, :, :].rearrange("p (n c) d -> p n c d", n=4)
        b1_in = w1s[0:E + 1, 0]
        w1 = sb("w1", [P, 2, 2, ND, F], F16)
        w2 = sb("w2", [P, 2, 2, NF, D], F16)
        PAD = 2 * DH
        values_pad = [w[0:KP, 1].rearrange("p a n c -> p (a n c)").bitcast(F32)[:, 0:KC * (H + 1) * PAD].rearrange(
            "p (c n) -> p c n", c=KC) for w in (w1, w2)]
        xn = w1[:, 0].rearrange("p a c f -> p (a c f)").bitcast(F32).rearrange("p (i d) -> p i d", d=D)
        NX = 2 * ND * F // 2 // D
        y_sb = sb("y_sb", [P, TILE // P, D], F32)
        zero = y_sb[:, :, :].rearrange("p a d -> p (a d)").bitcast(F16)

        ps = st.enter_context(nc.psum_tensor("ps", [P, 8, 512], F32))
        SC, PT, OB, PR = (0, 1), (2, 3), (4, 5), (6, 7)

        in_x, in_w = [sem(f"in_x{n}") for n in range(2)], [sem(f"in_wa{n}") for n in range(4)]
        in_small, in_bias = sem("in_small"), sem("in_bias")
        in_ctx = [sem(f"in_ctx{p}") for p in range(2)]
        in_mask = [sem(f"in_mask{p}") for p in range(2)]
        in_gp = [sem(f"in_gp{p}") for p in range(2)]
        consts = sem("consts")
        dve_step, act_step = sem("dve_step"), sem("act_step")
        dve_ask, act_ask, act_gave = sem("dve_ask"), sem("act_ask"), sem("act_gave")
        w_hi, w_lo = sem("w_hi"), sem("w_lo")
        small_T, small_out = sem("small_T"), sem("small_out")
        xn_made, xn_T, xn_hi, xn_lo = sem("xn_made"), sem("xn_T"), sem("xn_hi"), sem("xn_lo")
        q_mm, q_hi, q_lo, q_out = sem("q_mm"), sem("q_hi"), sem("q_lo"), sem("q_out")
        q_in = [sem(f"q_in{c}") for c in range(QC)]
        bo_made, resid = sem("bo_made"), sem("resid")
        neg_made, qb_made = sem("neg_made"), sem("qb_made")
        ctx_hi, ctx_lo = sem("ctx_hi"), sem("ctx_lo")
        prep_mm, prep_act, prep_lo = sem("prep_mm"), sem("prep_act"), sem("prep_lo")
        k_out = sem("k_out")
        k_in = [[sem(f"k_in{p}_{m}") for m in range(ND)] for p in range(2)]
        sc_made, sc_read, exp_made = sem("sc_made"), sem("sc_read"), sem("exp_made")
        pt_made, pt_read, av_made = sem("pt_made"), sem("pt_read"), sem("av_made")
        gp_times, pt_copied = sem("gp_times"), sem("pt_copied")
        o_read, rr_made, rT_mm, rT_made = sem("o_read"), sem("rr_made"), sem("rT_mm"), sem("rT_made")
        ri_made, oT_hi, oT_lo = sem("ri_made"), sem("oT_hi"), sem("oT_lo")
        pj_mm, x2_made = sem("pj_mm"), sem("x2_made")
        root_made, n2_made, n2_hi, n2_lo = sem("root_made"), sem("n2_made"), sem("n2_hi"), sem("n2_lo")
        n2_T, n2_Ts, rl_mm = sem("n2_T"), sem("n2_Ts"), sem("rl_mm")
        z_done = sem("z_done")
        gap_zero, pad_zero, sent_zero, sum_zero = sem("gap_zero"), sem("pad_zero"), sem("sent_zero"), sem("sum_zero")
        cnt_made, rank_mm, slot_made, tiles_made, scattered = (
            sem("cnt_made"), sem("rank_mm"), sem("slot_made"), sem("tiles_made"), sem("scattered"))
        in_w1, in_w2 = sem("in_w1"), sem("in_w2")
        in_b2 = sem("in_b2")
        w1_hi, w1_lo, w2_hi, w2_lo = sem("w1_hi"), sem("w1_lo"), sem("w2_hi"), sem("w2_lo")
        x_in = sem("x_in")
        xT_mm, xT_made = sem("xT_mm"), sem("xT_made")
        h_mm, h_relu, h_hi, h_split = sem("h_mm"), sem("h_relu"), sem("h_hi"), sem("h_split")
        y_mm, y_made, y_out, y_free = sem("y_mm"), sem("y_made"), sem("y_out"), sem("y_free")
        words_taken, word_made, dest_cmp = sem("words_taken"), sem("word_made"), sem("dest_cmp")
        back_in = [sem(f"back_in{n}") for n in range(NT // BACK)]
        mixed, out_done = sem("mixed"), sem("out_done")

        block = st.enter_context(nc.Block())

        SC_FREE, PROBS_FREE, PT_FREE, AT_FREE, O_FREE, Y_FREE = 2, PROBS, 2, 2, 2, 1

        def bank(n, rows, cols):
            return ps[0:rows, n, 0:cols]

        POOL_HEADS = (2, 6, 8, 12)
        NPOOL, NDVE = len(POOL_HEADS), H - len(POOL_HEADS)

        def by_pool(n):
            return sum(m <= n for m in POOL_HEADS)

        def by_dve(n):
            return n + 1 - by_pool(n)

        def turned_ctx(k):
            return ps[:, PR[k], 0:KC * P].bitcast(F16).rearrange("p (a c n) -> p a c n", a=2, c=KC)

        def turned_sums(p):
            return ps[:, OB[p], 256:256 + ND * S].rearrange("p (c q) -> p c q", c=ND)

        @block.sync
        def _(sp):
            half = NT // 2
            w_of = (wq, wk, wv, wo)

            def load_x(n):
                rows = slice(n * half * P, (n + 1) * half * P)
                sp.dma_start(x_sb[:, n * half:(n + 1) * half], x_rows[rows].rearrange("(i p) d -> p i d", p=P)).then_inc(in_x[n], 16)

            def load_attention_weights(n):
                sp.dma_start(wstage[:, n], w_of[n].rearrange("(c p) n -> p c n", p=P)).then_inc(in_w[n], 16)

            def load_context(b, p):
                sp.dma_start(ctx_in[:, p], ctx[bass.ds(b, 1)].rearrange("a (c p) d -> p (a c) d", p=KP)).then_inc(in_ctx[p], 16)

            def load_mask(b, p):
                sp.dma_start(mask_in[:, p], mask[bass.ds(b, 1)].rearrange("a q k -> q (a k)")).then_inc(in_mask[p], 16)

            def load_group_prob(b, p):
                sp.dma_start(gp_in[:, p], gp[bass.ds(b, 1)].rearrange("a q k -> q (a k)")).then_inc(in_gp[p], 16)

            load_x(0)
            load_context(0, 0)
            load_attention_weights(W_ORDER[0])
            load_x(1)
            for to, of in ((bcol_in[0:2, :], bq), (bcol_in[2:4, :], bk)):
                sp.dma_start(to, of.rearrange("(c p) -> c p", p=P)).then_inc(in_bias, 16)
            load_attention_weights(W_ORDER[1])
            load_mask(0, 0)
            load_group_prob(0, 0)
            load_attention_weights(W_ORDER[2])
            load_attention_weights(W_ORDER[3])
            smalls = [(bv_in[:, :], bv.rearrange("(a n) -> a n", a=1)),
                      (bo_bc[:, :], bo.partition_broadcast(P)),
                      (nw_bc[:, :], nw.partition_broadcast(P)),
                      (b1_in[0:E], eb1), (b1_in[E:E + 1], sb1.rearrange("(a n) -> a n", a=1)),
                      (r_in[:, :], router),
                      (gates[:, 0:1], g_xattn.partition_broadcast(P)),
                      (gates[:, 1:2], g_ffn.partition_broadcast(P)),
                      (sb2_bc[:, :], sb2.partition_broadcast(P))]
            for to, of in smalls:
                sp.dma_start(to, of).then_inc(in_small, 16)
            load_context(1, 1)
            load_mask(1, 1)
            load_group_prob(1, 1)

            def restack_keys(b, p):
                for m in range(ND):
                    high, low = sp.compute_val(7 * b + 3 + m), sp.compute_val(2 * b + 1 + m)
                    sp.wait_ge(in_x[0], 16)
                    sp.wait_ge(prep_act, high)
                    sp.wait_ge(prep_lo, low)
                    heads = k_scratch[bass.ds(b, 1), m * H // ND:(m + 1) * H // ND].rearrange("a h r k -> (a h) r k")
                    for n, c in enumerate(K_PARTS):
                        sp.dma_start(heads[:, n * DH:(n + 1) * DH], kT[:, c, m]).then_inc(k_out, 16)
                    sp.wait_ge(k_out, 96 * b + 48 * m + 48)
                    for par in range(2):
                        lo, pairs = par * SLOT, slice(m * H // 2 // ND, (m + 1) * H // 2 // ND)
                        sp.dma_start(kst[lo:lo + STACK, p, pairs], heads.rearrange("(j e) r k -> e r j k", e=2)[par]
                                     ).then_inc(k_in[p][m], 16)

            def load_weights(e):
                if e > 0:
                    sp.wait_ge(w1_lo, e + 1)
                sp.dma_start(w1s[:, :, :], ew1[e].rearrange("(c p) f -> p c f", p=P)).then_inc(in_w1, 16)
                if e > 0:
                    sp.wait_ge(w2_lo, e + 1)
                sp.dma_start(w2s[:, :, :], ew2[e].rearrange("(c p) d -> p c d", p=P)).then_inc(in_w2, 16)

            restack_keys(0, 0)
            sp.wait_ge(gap_zero, 1)
            def store_queries(c):
                cols = slice(c * QB * S, (c + 1) * QB * S)
                sp.wait_ge(q_hi, ND * (c + 1))
                sp.wait_ge(q_lo, ND * (c + 1))
                for m in range(ND):
                    for n, a in enumerate(Q_PARTS):
                        sp.dma_start(q_scratch[m * H // ND:(m + 1) * H // ND, n * DH:(n + 1) * DH, cols], qT[:, a, m, cols]).then_inc(q_out, 16)

            def stack_queries(c):
                cols = slice(c * QB * S, (c + 1) * QB * S)
                sp.wait_ge(q_out, 96 * (c + 1))
                for par in range(2):
                    sp.dma_start(q_stack[par * SLOT:par * SLOT + STACK, :, cols],
                                 q_scratch[:, :, cols].rearrange("(j e) r t -> e r j t", e=2)[par]).then_inc(q_in[c], 16)

            store_queries(0)
            stack_queries(0)
            sp.wait_ge(sent_zero, 1)

            def send_zeros(t):
                sp.dma_start(x_sent[bass.ds(t * ZT * TILE, ZT * TILE)].rearrange("(a p) c -> p a c", p=P),
                             zero[:, 0:RW].unsqueeze(1).to_broadcast([P, ZT * TILE // P, RW])).then_inc(z_done, 16)

            def next_sides(t, p):
                next_t = sp.compute_val(t + 1)
                sp.wait_ge(in_x[0], 16)
                sp.wait_ge(ctx_lo, next_t)
                sp.wait_ge(neg_made, next_t)
                load_context(t + 2, p)
                load_mask(t + 2, p)

            def step(t, p, more=True):
                if not (isinstance(t, int) and t == 0):
                    turned, used = sp.compute_val(7 * t), sp.compute_val(NPOOL * t)
                    sp.wait_ge(in_x[0], 16)
                    sp.wait_ge(prep_mm, turned)
                    sp.wait_ge(gp_times, used)
                    load_group_prob(t + 1, 1 - p)
                restack_keys(t + 1, 1 - p)
                if more:
                    next_sides(t + 1, 1 - p)
                if isinstance(t, int) and 1 <= t < QC:
                    stack_queries(t)
                if isinstance(t, int) and t + 1 < QC:
                    store_queries(t + 1)
                if isinstance(t, int) and t + 1 == QC:
                    sp.wait_ge(small_T, 2)
                    sp.dma_start(w1s[:, :, :], sw1.rearrange("(c p) f -> p c f", p=P)).then_inc(in_w1, 16)
                if isinstance(t, int) and t == QC:
                    sp.wait_ge(w_lo, 4)
                    sp.dma_start(w2s[:, :, :], sw2.rearrange("(c p) d -> p c d", p=P)).then_inc(in_w2, 16)
                if more:
                    send_zeros(t)

            next_sides(0, 0)
            for t in range(QC + 1):
                step(t, t % 2)
            with sp.Fori(QC // 2, B // 2 - 2) as i:
                step(2 * i + 1, 1)
                step(2 * i + 2, 0)
            send_zeros(B - 3)
            step(B - 3, 1, False)
            step(B - 2, 0, False)

            sp.wait_ge(w1_lo, 1)
            sp.wait_ge(w2_lo, 1)
            load_weights(0)
            sp.wait_ge(av_made, H // 2 * B + AT_FREE)
            sp.dma_start(b2_bc, eb2.partition_broadcast(P)).then_inc(in_b2, 16)

            load_weights(1)
            sp.wait_ge(scattered, 16 * 2 * NT)
            sp.dma_start(xin[:, :, :], x_sent[0:TILE].rearrange("(a p) c -> p a c", p=P)).then_inc(x_in, 16)
            sp.wait_ge(tiles_made, 1)
            for e in range(2, E):
                load_weights(e)
            end = sp.value_load(tile_of[0:1, E:E + 1], min_val=E, max_val=RT)
            done = sp.compute_val(end + Y_FREE)
            sp.wait_ge(in_x[0], 16)
            sp.wait_ge(y_free, done)
            for n in range(NT // BACK):
                sp.dma_start(back[:, n * BACK:(n + 1) * BACK].rearrange("p i c d -> p i (c d)"),
                             y_back[YPAD + n * BACK * 2 * P:YPAD + (n + 1) * BACK * 2 * P].rearrange("(i p c) d -> p i (c d)", p=P, c=2)
                             ).then_inc(back_in[n], 16)
            for n in range(NT // BACK):
                sp.wait_ge(mixed, (n + 1) * BACK)
                rows, tiles = slice(n * BACK * P, (n + 1) * BACK * P), slice(n * BACK, (n + 1) * BACK)
                sp.dma_start(out_rows[rows].rearrange("(i p) d -> p i d", p=P), x_sb[:, tiles]).then_inc(out_done, 16)
            sp.wait_ge(out_done, 16 * NT // BACK)

        @block.gpsimd
        def _(pool):
            pool.memset(ident[:, :], 0.0).then_inc(consts, 1)
            pool.wait_ge(consts, 1)
            pool.affine_select(out=ident[:, :], in_=ident[:, :], compare_op=ALU.not_equal, fill=1.0,
                               base=0, pattern=[[-1, P]], channel_multiplier=1).then_inc(consts, 1)
            pool.wait_ge(consts, 2)
            pool.tensor_copy(ident16[:, :], ident[:, :]).then_inc(consts, 1)
            pool.memset(ones16[:, :], 1.0).then_inc(consts, 1)
            pool.wait_ge(consts, 4)
            pool.memset(arena[32:64, :], 0.0).then_inc(gap_zero, 1)
            pool.wait_ge(gap_zero, 1)

            def make_neg(b, p, n):
                loaded = pool.compute_val(16 * n)
                pool.wait_ge(consts, 4)
                pool.wait_ge(in_mask[p], loaded)
                pool.tensor_scalar(neg[:, p], mask_in[:, p], 1.0e9, -1.0e9, ALU.mult, ALU.add).then_inc(neg_made, 1)

            def take_queries(b, p, part):
                rows, pairs = slice(0, SLOT + STACK), slice(part * H // 4, (part + 1) * H // 4)
                pool.tensor_copy(qb[rows, p, pairs], q_stack[rows, pairs, bass.ds(b * S, S)]).then_inc(qb_made, 1)

            def context_high(b, p, n, turned, chunks):
                loaded = pool.compute_val(16 * n)
                pool.wait_ge(consts, 4)
                pool.wait_ge(in_ctx[p], loaded)
                if turned is not None:
                    pool.wait_ge(prep_mm, turned)
                pool.tensor_copy(ctx_pair[:, HI, chunks], ctx_in[:, p, chunks]).then_inc(ctx_hi, chunks.stop - chunks.start)

            def context_low(b, p):
                now = pool.compute_val(KC * b + KC)
                pool.wait_ge(consts, 4)
                pool.wait_ge(ctx_hi, now)
                pool.tensor_tensor(ctx_pair[:, LO], ctx_in[:, p], ctx_pair[:, HI], ALU.subtract).then_inc(ctx_lo, 1)

            context_high(0, 0, 1, None, slice(0, KC))
            context_low(0, 0)
            make_neg(0, 0, 1)
            for w in (w1, w2):
                pool.memset(w[:, 1].rearrange("p a n c -> p (a n c)").bitcast(F32), 0.0).then_inc(pad_zero, 1)
            context_high(1, 1, 1, ND, slice(0, KC))
            context_low(1, 1)
            pool.memset(zero, 0.0).then_inc(sent_zero, 1)
            pool.wait_ge(gap_zero, 1)
            pool.wait_ge(q_in[0], 32)
            for part in range(2):
                take_queries(0, 0, part)
            pool.memset(tri[:, :], 0.0).then_inc(consts, 1)
            pool.wait_ge(consts, 5)
            pool.affine_select(out=tri[:, :], in_=tri[:, :], compare_op=ALU.is_ge, fill=1.0,
                               base=0, pattern=[[-1, P]], channel_multiplier=1).then_inc(consts, 1)
            for e in range(E):
                pool.memset(order[:, e:e + 1], float(E - e)).then_inc(sum_zero, 1)
            pool.memset(before[:, :, :, :], 0.0).then_inc(sum_zero, 1)
            pool.memset(est[:, :, :], 0.0).then_inc(sum_zero, 1)
            pool.iota(token_row[:, :], [[2 * P, NT]], base=YPAD, channel_multiplier=2).then_inc(sum_zero, 1)
            pool.wait_ge(sum_zero, E + 3)

            def times_group_prob(t, n, p, loaded=None):
                now = pool.compute_val(H * t + n + 1)
                pool.wait_ge(consts, 4)
                if loaded is not None:
                    loaded = pool.compute_val(16 * loaded)
                    pool.wait_ge(in_gp[p], loaded)
                pool.wait_ge(exp_made, now)
                pool.tensor_tensor(probs[:, n % PROBS], probs[:, n % PROBS], gp_in[:, p], ALU.mult).then_inc(gp_times, 1)

            def step(t, p, own, ahead, more=True, last=False):
                if more:
                    turned = pool.compute_val(7 * t + 9)
                    context_high(t + 2, p, own + 1, turned, slice(0, 2))
                for k, n in enumerate(POOL_HEADS):
                    times_group_prob(t, n, p, own if k == 0 else None)
                    if k == 0 and more:
                        context_high(t + 2, p, own + 1, turned, slice(2, KC))
                    if k == 0 and not last:
                        done = pool.compute_val(H * t + SC_FREE)
                        pool.wait_ge(consts, 4)
                        pool.wait_ge(sc_read, done)
                        make_neg(t + 1, 1 - p, ahead)
                    if k == 2 and more:
                        context_low(t + 2, p)
                    if not more:
                        first = (k + (len(POOL_HEADS) if last else 0)) * BIAS_TILES
                        if first < NT:
                            tiles = slice(first, min(first + BIAS_TILES, NT))
                            pool.tensor_tensor(x_sb[:, tiles], x_sb[:, tiles],
                                               bo_bc[:, :].unsqueeze(1).to_broadcast([P, tiles.stop - first, D]), ALU.add).then_inc(resid, 1)
                    if k in (2, 3) and not last:
                        take_queries(t + 1, 1 - p, k - 2)

            for t in range(QC + 1):
                if t == QB - 1:
                    pool.wait_ge(q_in[1], 32)
                step(t, t % 2, t // 2 + 1, (t + 1) // 2 + 1)
            for c in range(2, QC):
                pool.wait_ge(q_in[c], 32)
            with pool.Fori(QC // 2, B // 2 - 2) as i:
                step(2 * i + 1, 1, i + 1, i + 2)
                step(2 * i + 2, 0, i + 2, i + 2)
            step(B - 3, 1, B // 2 - 1, B // 2)
            pool.wait_ge(bo_made, 1)
            pool.wait_ge(xn_made, NT)
            step(B - 2, 0, B // 2, B // 2, more=False)
            step(B - 1, 1, B // 2, None, more=False, last=True)

            def split_low(n, p):
                pool.wait_ge(w1_hi, n + 1)
                pool.tensor_tensor(w1[:, p, LO], w1s[:, :, :], w1[:, p, HI], ALU.subtract).then_inc(w1_lo, 1)
                pool.wait_ge(w2_hi, n + 1)
                pool.tensor_tensor(w2[:, p, LO], w2s[:, :, :], w2[:, p, HI], ALU.subtract).then_inc(w2_lo, 1)

            split_low(0, 0)
            split_low(1, 1)
            pool.tensor_copy(xwords[:, :, 0], token_row[:, :]).then_inc(word_made, 1)
            pool.wait_ge(word_made, 2)
            pool.wait_ge(n2_lo, NT)
            pool.wait_ge(slot_made, 1)
            pool.wait_ge(z_done, 16 * ZEROS)
            for i in range(NT):
                for j in range(2):
                    pool.indirect_dma_start(x_sent[:, :], bass.IndirectOffsetOnAxis(ap=slots[:, j, i:i + 1], axis=0),
                                            xpair[:, i], None).then_inc(scattered, 16)
            pool.wait_ge(tiles_made, 1)
            for e in range(E):
                first = pool.value_load(tile_of[0:1, e:e + 1], min_val=e, max_val=RT)
                end = pool.value_load(tile_of[0:1, e + 1:e + 2], min_val=e + 1, max_val=RT)
                if e + 1 < E:
                    split_low(e + 2, e % 2)
                with pool.Fori(first, end) as r:
                    made, gone = pool.compute_val(2 * r + 2 * ST + 4), pool.compute_val(32 * r + 32)
                    pool.wait_ge(consts, 4)
                    pool.wait_ge(y_made, made)
                    for a in range(TILE // P):
                        pool.indirect_dma_start(y_back[:, :], bass.IndirectOffsetOnAxis(ap=dest[:, a:a + 1], axis=0),
                                                y_sb[:, a], None).then_inc(y_out, 16)
                    pool.wait_ge(consts, 4)
                    pool.wait_ge(y_out, gone)
                    pool.sem_inc(y_free, 1)

        @block.scalar
        def _(act):
            def weights_high(n):
                act.wait_ge(in_w[n], 16)
                act.activation(wpair[:, n, HI], wstage[:, n], ACT.Copy, scale=0.25 if n == 0 else 1.0).then_inc(w_hi, 1)

            def turned_high(tiles):
                for i in tiles:
                    act.wait_ge(xn_T, i + 1)
                    act.activation(xnT[:, HI, :, i * P:(i + 1) * P], bank(i % 4, P, D).rearrange("p (c t) -> p c t", c=ND),
                                   ACT.Copy).then_inc(xn_hi, 1)

            def queries_high(c):
                for m in range(ND):
                    act.wait_ge(q_mm, ND * c + m + 1)
                    act.activation(qT[:, HI, m, c * QB * S:(c + 1) * QB * S], bank(OB[m], P, QB * S), ACT.Identity,
                                   bias=bcol[:, m:m + 1]).then_inc(q_hi, 1)

            def prep_piece(b, k, p):
                act.wait_ge(prep_mm, 7 * b + k + 1)
                if k < 2:
                    act.activation(ctxT[:, :, k].rearrange("p a (c n) -> p a c n", c=KC), turned_ctx(k)[:, :, :, 0:KP],
                                   ACT.Copy).then_inc(prep_act, 1)
                elif k < 4:
                    if not (isinstance(b, int) and b == 0):
                        act.wait_ge(k_out, 96 * b)
                    act.activation(kT[:, HI, k - 2], bank(PR[k - 2], P, S2), ACT.Identity,
                                   bias=bcol[:, k:k + 1]).then_inc(prep_act, 1)
                elif k == 6:
                    act.activation(gpT[:, p], bank(PR[1], KP, KC * S).rearrange("p (c q) -> p c q", c=KC), ACT.Copy).then_inc(prep_act, 1)
                elif k == 4:
                    if isinstance(b, int) and b == 0:
                        act.wait_ge(pad_zero, 2)
                    act.activation(head_columns(p, 0, 2), bank(PR[1], KP, 2 * D).rearrange("p (c h d) -> p c h d", c=2, h=H),
                                   ACT.Copy).then_inc(prep_act, 1)
                else:
                    act.activation(head_columns(p, 2, 3), bank(PR[0], KP, D).rearrange("p (c h d) -> p c h d", c=1, h=H),
                                   ACT.Copy).then_inc(prep_act, 1)

            def head_columns(p, first, end):
                return values_pad[p][:, first:end, 0:H * PAD].rearrange("p c (h e) -> p c h e", h=H)[:, :, :, DH:PAD]

            def take_sums(t, p):
                act.wait_ge(rT_mm, t + 1)
                act.wait_ge(o_read, t + O_FREE)
                act.activation(rT[:, :, :], turned_sums(p), ACT.Copy).then_inc(rT_made, 1)

            def split_out(t):
                act.wait_ge(o_read, t + 1 + O_FREE)
                act.activation(oT[:, HI, :, bass.ds(t * S, S)], o32[:, :, :], ACT.Copy).then_inc(oT_hi, 1)

            weights_high(W_ORDER[0])
            act.wait_ge(small_T, 1)
            act.activation(bcol[:, 0:2], bank(PR[0], P, 4)[:, 0:2], ACT.Copy, scale=0.25).then_inc(small_out, 1)
            act.activation(bcol[:, 2:4], bank(PR[0], P, 4)[:, 2:4], ACT.Copy).then_inc(small_out, 1)
            weights_high(W_ORDER[1])
            act.wait_ge(dve_ask, 1)
            act.activation(nrm[:, 1], nrm[:, 0], ACT.Sqrt).then_inc(act_gave, 1)
            for k in range(4):
                prep_piece(0, k, 0)
            turned_high(Q_TILES[0])
            turned_high(Q_TILES[1])
            queries_high(0)
            weights_high(W_ORDER[2])
            weights_high(W_ORDER[3])
            act.wait_ge(in_small, 16 * SMALLS)
            act.activation(bv_pair[:, HI], bv_in[:, :], ACT.Copy).then_inc(w_hi, 1)
            for c in range(1, QC):
                if c + 1 < QC:
                    turned_high(Q_TILES[c + 1])
                queries_high(c)
            for k in range(4, 7):
                prep_piece(0, k, 0)
            act.wait_ge(small_T, 3)
            act.activation(b1[:, :, :], bank(PT[0], P, NF * (E + 1)).rearrange("p (f e) -> p f e", f=NF), ACT.Copy).then_inc(small_out, 1)
            act.activation(routerT[:, HI], bank(PT[1], P, ND * E).rearrange("p (c e) -> p c e", c=ND), ACT.Copy).then_inc(small_out, 1)
            act.activation(gates[:, :], gates[:, :], ACT.Tanh).then_inc(act_gave, 1)

            def copy_probs(t, n):
                act.wait_ge(pt_made, 16 * t + n + 1 + PROBS_FREE)
                act.wait_ge(av_made, 8 * t + n // 2 - 1 + AT_FREE)
                act.activation(probsT[:, n % 4], bank(PT[n % 2], KP, KC * S).rearrange("p (c q) -> p c q", c=KC), ACT.Copy).then_inc(pt_copied, 1)

            pieces = {0: 1, 3: 2, 5: 3, 11: 4, 13: 5, 14: 6}

            def step(t, p, first=False, t_next=True, t_after=True):
                act.wait_ge(rr_made, t + 1)
                for n in range(H):
                    act.wait_ge(sc_read, 16 * t + n + 1 + SC_FREE)
                    act.activation(probs[:, n % PROBS], probs[:, n % PROBS], ACT.Exp, bias=negmax[:, p, n:n + 1], scale=-1.0,
                                   accum_out=rowsum[:, p, ORDER[n]:ORDER[n] + 1]).then_inc(exp_made, 1)
                    if n - LEAD + 1 in POOL_HEADS:
                        copy_probs(t, n - LEAD + 1)
                    if t_next and n in pieces:
                        prep_piece(t + 1, pieces[n], 1 - p)
                    if t_after and n == H - 1:
                        prep_piece(t + 2, 0, p)
                    if n == 6 and not first:
                        take_sums(t - 1, 1 - p)
                    if n == 10 and not first:
                        split_out(t - 1)

            prep_piece(1, 0, 1)
            step(0, 0, first=True)
            with act.Fori(0, B // 2 - 2) as i:
                step(2 * i + 1, 1)
                step(2 * i + 2, 0)
            step(B - 3, 1)
            step(B - 2, 0, t_after=False)
            step(B - 1, 1, t_next=False, t_after=False)
            take_sums(B - 1, 1)
            split_out(B - 1)

            act.wait_ge(in_w1, 16)
            act.activation(w1[:, 0, HI], w1s[:, :, :], ACT.Copy).then_inc(w1_hi, 1)
            act.wait_ge(in_w2, 16)
            act.activation(w2[:, 0, HI], w2s[:, :, :], ACT.Copy).then_inc(w2_hi, 1)
            act.wait_ge(dve_ask, 2)
            act.activation(nrm[:, 1], nrm[:, 0], ACT.Sqrt).then_inc(act_gave, 1)
            def turned(i):
                act.wait_ge(n2_T, i + 1)
                act.activation(x2T[:, :, :, i * P:(i + 1) * P].rearrange("p a c t -> p (a c) t"),
                               ps[:, i % 4, 0:D].bitcast(F16).rearrange("p (c t) -> p c t", t=P), ACT.Copy).then_inc(n2_Ts, 1)

            act.wait_ge(root_made, 1)
            for i in range(NT):
                act.wait_ge(n2_made, i + 1)
                act.activation(xpair[:, i, 0:D], xn2[:, i], ACT.Copy, scale=nrm[:, 2, i:i + 1]).then_inc(n2_hi, 1)
                if i >= 2:
                    turned(i - 2)
            turned(NT - 2)
            turned(NT - 1)

            def split_high(n, p):
                act.wait_ge(in_w1, 16 * n + 16)
                act.activation(w1[:, p, HI], w1s[:, :, :], ACT.Copy).then_inc(w1_hi, 1)

            def activate(i, e):
                for f in range(NF):
                    act.wait_ge(h_mm, NF * i + (f | 1) + 1)
                    act.activation(hid32[:, f], ps[:, f // 2 % 4, f % 2 * TILE:(f % 2 + 1) * TILE], ACT.Relu,
                                   bias=b1[:, f, e:e + 1]).then_inc(h_relu, 1)

            def take_tile(r):
                act.wait_ge(xT_mm, r + 1)
                act.activation(xT[:, :, :], ps[:, 6, 0:2 * TILE].bitcast(F16).rearrange("p (c t) -> p c t", c=2 * ND),
                               ACT.Copy).then_inc(xT_made, 1)

            def load_tile(r):
                act.dma_start(xin[:, :, :], x_sent[bass.ds(r * TILE, TILE)].rearrange("(a p) c -> p a c", p=P)).then_inc(x_in, 16)

            activate(0, E)
            split_high(1, 1)
            with act.Fori(1, ST) as i:
                activate(i, E)
            act.wait_ge(dve_ask, 3)
            act.activation(top[:, 6:8], top[:, 6:8], ACT.Exp, scale=-1.0).then_inc(act_gave, 1)
            take_tile(0)
            act.wait_ge(words_taken, 1)
            load_tile(1)
            act.wait_ge(tiles_made, 1)
            for e in range(E):
                first = act.value_load(tile_of[0:1, e:e + 1], min_val=e, max_val=RT)
                end = act.value_load(tile_of[0:1, e + 1:e + 2], min_val=e + 1, max_val=RT)
                if e + 1 < E:
                    split_high(e + 2, e % 2)
                with act.Fori(first, end) as r:
                    activate(r + ST, e)
                    take_tile(r + 1)
                    taken = act.compute_val(r + 2)
                    act.wait_ge(consts, 3)
                    act.wait_ge(words_taken, taken)
                    load_tile(r + 2)
            loaded = act.compute_val(end * 16 + 32)
            act.wait_ge(consts, 3)
            act.wait_ge(x_in, loaded)

        @block.tensor
        def _(pe):
            pe.wait_ge(consts, 3)
            pe.wait_ge(in_bias, 32)
            pe.transpose(bank(PR[0], P, 4), bcol_in[:, :], ident[0:4, 0:4]).then_inc(small_T, 1)

            def turn_x(tiles):
                for i in tiles:
                    pe.wait_ge(xn_made, i + 1)
                    if i >= 4:
                        pe.wait_ge(xn_lo, i - 3)
                    for c in range(ND):
                        mm = pe.transpose(ps[:, i % 4, c * P:(c + 1) * P], xn[:, i % NX, c * P:(c + 1) * P], ident[:, :])
                    mm.then_inc(xn_T, 1)

            def queries(c):
                pe.wait_ge(w_lo, 2)
                pe.wait_ge(xn_hi, Q_TILES[c].stop)
                pe.wait_ge(xn_lo, Q_TILES[c].stop)
                for m in range(ND):
                    if c > 0:
                        pe.wait_ge(q_lo, ND * (c - 1) + m + 1)
                    parts = [(w, a, k) for k in range(ND) for w, a in PASSES]
                    for j, (w, a, k) in enumerate(parts):
                        mm = pe.matmul(bank(OB[m], P, QB * S), wpair[:, 0, w, k, m * P:(m + 1) * P],
                                       xnT[:, a, k, c * QB * S:(c + 1) * QB * S], start=(j == 0), stop=(j == len(parts) - 1))
                    mm.then_inc(q_mm, 1)

            def turn_ctx(b, k):
                if k == 0:
                    pe.wait_ge(ctx_lo, b + 1)
                    if isinstance(b, int) and b == 0:
                        pe.wait_ge(small_out, 2)
                    else:
                        pe.wait_ge(prep_act, 7 * b - 1)
                elif not (isinstance(b, int) and b == 0):
                    pe.wait_ge(prep_act, 7 * b)
                for a in range(2):
                    for c in range(KC):
                        mm = pe.transpose(turned_ctx(k)[:, a, c, 0:KP], ctx_pair[:, a, c, k * P:(k + 1) * P], ident16[0:KP, 0:KP])
                mm.then_inc(prep_mm, 1)

            def keys(b, m, part):
                if m == 0:
                    pe.wait_ge(prep_act, 7 * b + 1 + part)
                if part == 0:
                    if isinstance(b, int) and b == 0 and m == 0:
                        pe.wait_ge(w_lo, 1)
                for j, (w, a) in enumerate(PASSES):
                    mm = pe.matmul(bank(PR[m], P, S2), wpair[:, 1, w, part, m * P:(m + 1) * P], ctxT[:, a, part],
                                   start=(part == 0 and j == 0), stop=(part == 1 and j == 2))
                if part == 1:
                    mm.then_inc(prep_mm, 1)

            def turn_gp(b, p, n):
                pe.wait_ge(in_gp[p], 16 * n)
                pe.wait_ge(prep_act, 7 * b + 5)
                for c in range(KC):
                    mm = pe.transpose(ps[0:KP, PR[1], c * S:(c + 1) * S], gp_in[:, p, c * KP:(c + 1) * KP], ident[0:S, 0:S])
                mm.then_inc(prep_mm, 1)

            def vals(b, c, part):
                if c == 0 and part == 0:
                    pe.wait_ge(prep_lo, 2 * b + 2)
                    if isinstance(b, int) and b == 0:
                        pe.wait_ge(w_lo, 5)
                        pe.wait_ge(consts, 4)
                to = ps[0:KP, PR[0] if c == 2 else PR[1], c % 2 * D:c % 2 * D + D]
                if part == 0:
                    for a in range(2):
                        pe.matmul(to, ones16[0:1, 0:KP], bv_pair[0:1, a], start=(a == 0), stop=False)
                for j, (a, w) in enumerate(PASSES):
                    mm = pe.matmul(to, ctxT[:, a, part, c * KP:(c + 1) * KP], wpair[:, 2, w, part], start=False, stop=(part == 1 and j == 2))
                if part == 1 and c > 0:
                    mm.then_inc(prep_mm, 1)

            def prep_slot(b, n, p, loads):
                if n < 2:
                    turn_ctx(b, n)
                elif 3 <= n < 7:
                    keys(b, (n - 3) // 2, (n - 3) % 2)
                elif 9 <= n < 15:
                    vals(b, (n - 9) // 2, (n - 9) % 2)
                elif n == 15:
                    turn_gp(b, p, loads)

            def turn_sums(t, p):
                pe.wait_ge(rr_made, t + 1 + O_FREE)
                for c in range(ND):
                    mm = pe.transpose(turned_sums(p)[:, c], rrow[:, c * H // ND:(c + 1) * H // ND].rearrange("q h d -> q (h d)"),
                                      ident[0:S, 0:S])
                mm.then_inc(rT_mm, 1)

            def scores(t, n, p, loaded=None):
                h = ORDER[n]
                if n % (H // ND) == 0:
                    pe.wait_ge(k_in[p][n // (H // ND)], loaded)
                    pe.wait_ge(qb_made, 2 * t + 1 + n // (H // ND))
                pe.wait_ge(sc_read, 16 * t + n + 1)
                rows = slice(h % 2 * SLOT, h % 2 * SLOT + STACK)
                pe.matmul(bank(SC[n % 2], S, S2), qb[rows, p, h // 2], kst[rows, p, h // 2], start=True, stop=True).then_inc(sc_made, 1)

            def turn_probs(t, n):
                if n in POOL_HEADS:
                    pe.wait_ge(gp_times, NPOOL * t + by_pool(n))
                else:
                    pe.wait_ge(exp_made, 16 * t + n + 1)
                if n - 2 in POOL_HEADS:
                    pe.wait_ge(pt_copied, NPOOL * t + by_pool(n - 2))
                else:
                    pe.wait_ge(pt_read, NDVE * t + by_dve(n - 2) + PT_FREE)
                for c in range(KC):
                    mm = pe.transpose(ps[0:KP, PT[n % 2], c * S:(c + 1) * S], probs[:, n % PROBS, c * KP:(c + 1) * KP], ident[0:S, 0:S])
                mm.then_inc(pt_made, 1)

            def values(t, n, p):
                if n == 0:
                    pe.wait_ge(o_read, t + 1)
                    pe.wait_ge(prep_act, 7 * t + 7)
                pe.wait_ge(pt_read, NDVE * t + by_dve(n + 1) + PT_FREE)
                if n in POOL_HEADS or n + 1 in POOL_HEADS:
                    pe.wait_ge(pt_copied, NPOOL * t + by_pool(n + 1))
                for c in range(KC):
                    for k in (n, n + 1):
                        h = ORDER[k]
                        half, row = h // (H // ND), h % (H // ND) // 2 * PAD
                        first = h * PAD + (DH if h % 2 == 0 else 0)
                        mm = pe.matmul(ps[row:row + PAD, OB[p], half * S:(half + 1) * S], values_pad[p][:, c, first:first + PAD],
                                       probsT[:, k % 4, c], start=(h % 2 == 0 and c == 0), stop=(h % 2 == 1 and c == KC - 1))
                mm.then_inc(av_made, 1)

            pe.sem_inc(pt_made, PROBS_FREE)
            pe.sem_inc(av_made, AT_FREE)
            for n in range(7):
                prep_slot(0, n, 0, 1)
            turn_x(Q_TILES[0])
            for c in range(QC):
                if c + 1 < QC:
                    turn_x(Q_TILES[c + 1])
                queries(c)
            for n in range(7, H):
                prep_slot(0, n, 0, 1)
            pe.wait_ge(in_small, 16 * SMALLS)
            pe.wait_ge(xn_lo, NT)
            for f in range(NF):
                mm = pe.transpose(ps[:, PT[0], f * (E + 1):(f + 1) * (E + 1)], b1_in[:, f * P:(f + 1) * P], ident[0:E + 1, 0:E + 1])
            mm.then_inc(small_T, 1)
            for c in range(ND):
                mm = pe.transpose(ps[:, PT[1], c * E:(c + 1) * E], r_in[:, c * P:(c + 1) * P], ident[0:E, 0:E])
            mm.then_inc(small_T, 1)
            for n in range(2):
                prep_slot(1, n, 1, 1)
            for n in range(LEAD + 1):
                scores(0, n, 0, 32)

            def step(t, p, loads, loaded, loaded_next, first=False, t_next=True, t_after=True):
                for n in range(H):
                    turn_probs(t, n)
                    ahead = n + LEAD + 1
                    if ahead < H:
                        scores(t, ahead, p, loaded)
                    elif t_next:
                        scores(t + 1, ahead - H, 1 - p, loaded_next)
                    if n % 2 == 0:
                        if n > 0:
                            values(t, n - 2, p)
                        elif not first:
                            values(t - 1, H - 2, 1 - p)
                    if n == 3 and not first:
                        turn_sums(t - 1, 1 - p)
                    if first and n == 0:
                        for m in range(2, PREP):
                            prep_slot(t + 1, m, 1 - p, loads)
                    if n + PREP < H and t_next:
                        prep_slot(t + 1, n + PREP, 1 - p, loads)
                    if n + PREP >= H and t_after:
                        prep_slot(t + 2, n + PREP - H, p, None)

            pe.wait_ge(small_out, 4)
            pe.wait_ge(w_lo, 6)
            step(0, 0, 1, 32, 32, first=True)
            with pe.Fori(0, B // 2 - 2) as i:
                step(2 * i + 1, 1, i + 2, i * 32 + 32, i * 32 + 64)
                step(2 * i + 2, 0, i + 2, i * 32 + 64, i * 32 + 64)
            step(B - 3, 1, B // 2, 32 * B // 2 - 32, 32 * B // 2)
            step(B - 2, 0, B // 2, 32 * B // 2, 32 * B // 2, t_after=False)
            step(B - 1, 1, None, 32 * B // 2, None, t_next=False, t_after=False)
            values(B - 1, H - 2, 1)
            turn_sums(B - 1, 1)

            pe.wait_ge(oT_hi, B)
            pe.wait_ge(oT_lo, B)
            for i in range(NT):
                if i >= 2:
                    pe.wait_ge(x2_made, i - 1)
                parts = [(a, w, k) for k in range(ND) for a, w in PASSES]
                for j, (a, w, k) in enumerate(parts):
                    mm = pe.matmul(bank(OB[i % 2], P, D), oT[:, a, k, i * P:(i + 1) * P], wpair[:, 3, w, k],
                                   start=(j == 0), stop=(j == len(parts) - 1))
                mm.then_inc(pj_mm, 1)

            def route(i):
                pe.wait_ge(n2_Ts, i + 1)
                parts = [(a, w, k) for k in range(ND) for a in range(2) for w in range(2)]
                for j, (a, w, k) in enumerate(parts):
                    mm = pe.matmul(ps[:, PR[1], P + i * E:P + (i + 1) * E], x2T[:, a, k, i * P:(i + 1) * P], routerT[:, w, k],
                                   start=(j == 0), stop=(j == len(parts) - 1))
                mm.then_inc(rl_mm, 1)

            for i in range(NT):
                pe.wait_ge(n2_hi, i + 1)
                pe.wait_ge(n2_lo, i + 1)
                if i >= 4:
                    pe.wait_ge(n2_Ts, i - 3)
                for c in range(2 * ND):
                    mm = pe.transpose(ps[:, i % 4, 0:D].bitcast(F16)[:, c * P:(c + 1) * P], xpair[:, i, c * P:(c + 1) * P], ident16[:, :])
                mm.then_inc(n2_T, 1)
                if i >= 3:
                    route(i - 3)
            for i in range(NT - 3, NT):
                route(i)

            def turn_tile(r):
                pe.wait_ge(x_in, 16 * r + 16)
                for a in range(TILE // P):
                    for c in range(2 * ND):
                        mm = pe.transpose(ps[:, 6, 0:2 * TILE].bitcast(F16)[:, c * TILE + a * P:c * TILE + (a + 1) * P],
                                          xin[:, a, c * P:(c + 1) * P], ident16[:, :])
                mm.then_inc(xT_mm, 1)

            def hidden(p, rows):
                for f in range(NF):
                    parts = [(w, a, k) for k in range(ND) for w, a in PASSES]
                    for j, (w, a, k) in enumerate(parts):
                        mm = pe.matmul(ps[:, f // 2 % 4, f % 2 * TILE:(f % 2 + 1) * TILE], w1[:, p, w, k, f * P:(f + 1) * P],
                                       rows(a, k), start=(j == 0), stop=(j == len(parts) - 1))
                    mm.then_inc(h_mm, 1)

            def results(i, p):
                for a in range(TILE // P):
                    pe.wait_ge(y_made, 2 * i + a + 1)
                    for f in range(NF):
                        if a == 0 and f % 2 == 0:
                            pe.wait_ge(h_split, (NF // 2) * i + f // 2 + 1)
                        for j, (u, w) in enumerate(PASSES):
                            mm = pe.matmul(ps[:, 4 + a, 0:D], hid[:, u, f, a * P:(a + 1) * P], w2[:, p, w, f],
                                           start=(f == 0 and j == 0), stop=(f == NF - 1 and j == 2))
                    mm.then_inc(y_mm, 1)

            def shared_tile(i):
                hidden(0, lambda a, k: x2T[:, a, k, bass.ds(i * TILE, TILE)])
                if isinstance(i, int) and i == 0:
                    rank_pairs()
                if isinstance(i, int) and i == ST - 1:
                    turn_tile(0)
                results(i, 0)

            def rank_pairs():
                pe.wait_ge(consts, 6)
                pe.wait_ge(cnt_made, 1)
                rk = bank(PR[1], P, NT * E)
                pe.matmul(rk, tri[:, :], count16[:, 0].rearrange("p i e -> p (i e)"), start=True, stop=False)
                pe.matmul(rk, ones16[:, :], count16[:, 1].rearrange("p i e -> p (i e)"), start=False, stop=True).then_inc(rank_mm, 1)
                pe.matmul(ps[:, PR[1], NT * E:(NT + 1) * E], ones16[:, :], count16[:, 2, 0], start=True, stop=True).then_inc(rank_mm, 1)

            pe.wait_ge(w1_lo, 1)
            pe.wait_ge(w2_lo, 1)
            shared_tile(0)
            with pe.Fori(1, ST - 1) as i:
                shared_tile(i)
            shared_tile(ST - 1)
            pe.wait_ge(tiles_made, 1)
            for e in range(E):
                first = pe.value_load(tile_of[0:1, e:e + 1], min_val=e, max_val=RT)
                end = pe.value_load(tile_of[0:1, e + 1:e + 2], min_val=e + 1, max_val=RT)
                p = (e + 1) % 2
                pe.wait_ge(w1_lo, e + 2)
                pe.wait_ge(w2_lo, e + 2)
                with pe.Fori(first, end) as r:
                    pe.wait_ge(xT_made, r + 1)
                    hidden(p, lambda a, k: xT[:, a * ND + k])
                    turn_tile(r + 1)
                    results(r + ST, p)

        @block.vector
        def _(dve):
            steps = [0]

            def then(ins):
                steps[0] += 1
                ins.then_inc(dve_step, 1)
                dve.wait_ge(dve_step, steps[0])

            def inverse_root(gave):
                dve.wait_ge(act_gave, gave)
                then(dve.reciprocal(nrm[:, 3], nrm[:, 1]))
                then(dve.tensor_tensor(nrm[:, 3], nrm[:, 3], nrm[:, 0], ALU.mult))
                then(dve.tensor_tensor(nrm[:, 3], nrm[:, 3], nrm[:, 1], ALU.add))
                then(dve.tensor_scalar(nrm[:, 3], nrm[:, 3], 0.5, None, ALU.mult))
                then(dve.reciprocal(nrm[:, 2], nrm[:, 3]))

            for i in range(NT):
                if i % (NT // 2) == 0:
                    dve.wait_ge(in_x[i // (NT // 2)], 16)
                last = dve.bn_stats(stats[:, i], x_sb[:, i])
            then(last)
            for i in range(NT):
                last = dve.bn_aggr(mv[:, i], stats[:, i])
            then(last)
            dve.tensor_scalar(nrm[:, 0], mv[:, :, 1], LN_EPS, None, ALU.add).then_inc(dve_ask, 1)

            def weights_low(n):
                dve.wait_ge(w_hi, W_ORDER.index(n) + 1)
                if n == 0:
                    dve.scalar_tensor_tensor(wpair[:, 0, LO], wstage[:, 0], 0.25, wpair[:, 0, HI], ALU.mult, ALU.subtract).then_inc(w_lo, 1)
                else:
                    dve.tensor_tensor(wpair[:, n, LO], wstage[:, n], wpair[:, n, HI], ALU.subtract).then_inc(w_lo, 1)

            def norm_x(tiles):
                for i in tiles:
                    if i >= NX:
                        dve.wait_ge(xn_T, i - NX + 1)
                    dve.tensor_scalar(xn[:, i % NX], x_sb[:, i], mv[:, i, 0:1], nrm[:, 2, i:i + 1], ALU.subtract, ALU.mult).then_inc(xn_made, 1)

            def turned_low(tiles):
                for i in tiles:
                    dve.wait_ge(xn_hi, i + 1)
                    cols = slice(i * P, (i + 1) * P)
                    dve.tensor_tensor(xnT[:, LO, :, cols], bank(i % 4, P, D).rearrange("p (c t) -> p c t", c=ND),
                                      xnT[:, HI, :, cols], ALU.subtract).then_inc(xn_lo, 1)

            def queries_low(c):
                for m in range(ND):
                    dve.wait_ge(q_hi, ND * c + m + 1)
                    cols = slice(c * QB * S, (c + 1) * QB * S)
                    dve.scalar_tensor_tensor(qT[:, LO, m, cols], bank(OB[m], P, QB * S), bcol[:, m:m + 1], qT[:, HI, m, cols],
                                             ALU.add, ALU.subtract).then_inc(q_lo, 1)

            def keys_low(b, m):
                dve.wait_ge(prep_act, 7 * b + 3 + m)
                dve.scalar_tensor_tensor(kT[:, LO, m], bank(PR[m], P, S2), bcol[:, 2 + m:3 + m], kT[:, HI, m],
                                         ALU.add, ALU.subtract).then_inc(prep_lo, 1)

            weights_low(W_ORDER[0])
            weights_low(W_ORDER[1])
            inverse_root(1)
            norm_x(Q_TILES[0])
            for m in range(ND):
                keys_low(0, m)
            norm_x(Q_TILES[1])
            turned_low(Q_TILES[0])
            norm_x(Q_TILES[2])
            turned_low(Q_TILES[1])
            queries_low(0)
            weights_low(W_ORDER[2])
            weights_low(W_ORDER[3])
            dve.wait_ge(w_hi, 5)
            dve.tensor_tensor(bv_pair[:, LO], bv_in[:, :], bv_pair[:, HI], ALU.subtract).then_inc(w_lo, 1)
            for c in range(1, QC):
                if c + 2 < QC:
                    norm_x(Q_TILES[c + 2])
                if c + 1 < QC:
                    turned_low(Q_TILES[c + 1])
                queries_low(c)
            dve.wait_ge(small_out, 4)
            dve.tensor_tensor(routerT[:, LO], bank(PT[1], P, ND * E).rearrange("p (c e) -> p c e", c=ND), routerT[:, HI], ALU.subtract).then_inc(w_lo, 1)
            dve.wait_ge(act_gave, 2)
            dve.tensor_scalar(bo_bc[:, :], bo_bc[:, :], gates[:, 0:1], None, ALU.mult).then_inc(bo_made, 1)

            dve.sem_inc(sc_read, SC_FREE)
            dve.sem_inc(pt_read, PT_FREE)
            dve.sem_inc(o_read, O_FREE)
            dve.sem_inc(rr_made, O_FREE)

            def mask_scores(t, n, p):
                if n == 0:
                    dve.wait_ge(neg_made, t + 1)
                head = dve.compute_val(16 * t + n + 1)
                dve.wait_ge(neg_made, 1)
                dve.wait_ge(sc_made, head)
                dve.wait_ge(pt_made, head)
                dve.tensor_tensor_reduce(probs[:, n % PROBS], bank(SC[n % 2], S, S2), neg[:, p], -1.0, BIG, ALU.add, ALU.min,
                                         negmax[:, p, n:n + 1]).then_inc(sc_read, 1)

            def weigh(t, n, p):
                dve.wait_ge(pt_made, 16 * t + n + 1 + PROBS_FREE)
                dve.wait_ge(av_made, 8 * t + n // 2 - 1 + AT_FREE)
                dve.tensor_tensor(probsT[:, n % 4], bank(PT[n % 2], KP, KC * S).rearrange("p (c q) -> p c q", c=KC),
                                  gpT[:, p], ALU.mult).then_inc(pt_read, 1)

            def invert_sums(t, p):
                dve.wait_ge(exp_made, 16 * t + 16)
                if not (isinstance(t, int) and t == 0):
                    dve.wait_ge(rT_mm, t)
                dve.reciprocal(rinv[:, :], rowsum[:, p]).then_inc(ri_made, 1)
                dve.wait_ge(ri_made, t + 1)
                dve.tensor_copy(rrow[:, :, :], rinv[:, :].unsqueeze(2).to_broadcast([S, H, DH])).then_inc(rr_made, 1)

            def divide(t, p):
                dve.wait_ge(av_made, 8 * t + 8 + AT_FREE)
                dve.wait_ge(rT_made, t + 1)
                dve.tensor_tensor(o32[:, :, :], bank(OB[p], P, ND * S).rearrange("p (c q) -> p c q", c=ND), rT[:, :, :],
                                  ALU.mult).then_inc(o_read, 1)

            def split_out(t):
                dve.wait_ge(oT_hi, t + 1)
                cols = bass.ds(t * S, S)
                dve.tensor_tensor(oT[:, LO, :, cols], o32[:, :, :], oT[:, HI, :, cols], ALU.subtract).then_inc(oT_lo, 1)

            for n in range(LEAD):
                mask_scores(0, n, 0)

            def step(t, p, first=False, prep=True):
                for n in range(H):
                    if n + LEAD < H:
                        mask_scores(t, n + LEAD, p)
                    elif prep:
                        mask_scores(t + 1, n + LEAD - H, 1 - p)
                    if n not in POOL_HEADS:
                        weigh(t, n, p)
                    if prep and n in (1, 3):
                        keys_low(t + 1, n // 3)
                    if n == 2 and not first:
                        invert_sums(t - 1, 1 - p)
                    if n == 6 and not first:
                        divide(t - 1, 1 - p)
                    if n == 9 and not first:
                        split_out(t - 1)

            step(0, 0, first=True)
            with dve.Fori(0, B // 2 - 1) as i:
                step(2 * i + 1, 1)
                step(2 * i + 2, 0)
            step(B - 1, 1, prep=False)
            invert_sums(B - 1, 1)
            divide(B - 1, 1)
            split_out(B - 1)

            for i in range(NT):
                dve.wait_ge(pj_mm, i + 1)
                if i == 0:
                    dve.wait_ge(resid, -(-NT // BIAS_TILES))
                dve.scalar_tensor_tensor(x_sb[:, i], bank(OB[i % 2], P, D), gates[:, 0:1], x_sb[:, i], ALU.mult, ALU.add).then_inc(x2_made, 1)
                if i >= 1:
                    dve.wait_ge(x2_made, i)
                    dve.bn_stats(stats[:, i - 1], x_sb[:, i - 1])
            dve.wait_ge(x2_made, NT)
            then(dve.bn_stats(stats[:, NT - 1], x_sb[:, NT - 1]))
            for i in range(NT):
                last = dve.bn_aggr(mv[:, i], stats[:, i])
            then(last)
            then(dve.tensor_scalar(nrm[:, 4], mv[:, :, 1], LN_EPS, RMS_EPS, ALU.add, ALU.mult))
            dve.tensor_tensor(nrm[:, 0], nrm[:, 4], mv[:, :, 1], ALU.add).then_inc(dve_ask, 1)

            def center(tiles):
                for i in tiles:
                    dve.scalar_tensor_tensor(xn2[:, i], x_sb[:, i], mv[:, i, 0:1], nw_bc[:, :], ALU.subtract, ALU.mult).then_inc(n2_made, 1)

            center(range(2))
            inverse_root(3)
            dve.sem_inc(root_made, 1)
            center(range(2, NT))
            for i in range(NT):
                dve.wait_ge(n2_hi, i + 1)
                dve.scalar_tensor_tensor(xpair[:, i, D:2 * D], xn2[:, i], nrm[:, 2, i:i + 1], xpair[:, i, 0:D],
                                         ALU.mult, ALU.subtract).then_inc(n2_lo, 1)

            dve.wait_ge(rl_mm, NT)
            dve.wait_ge(sum_zero, E + 3)
            logit = ps[:, PR[1], P:P + NT * E].rearrange("p (i e) -> p i e", e=E)

            def spread(col):
                return col.unsqueeze(2).to_broadcast([P, NT, E])

            def choose(src, n):
                then(dve.tensor_reduce(top[:, n], src, AX.X, ALU.max))
                then(dve.tensor_tensor(rt[:, 3], src, spread(top[:, n]), ALU.is_equal))
                then(dve.tensor_tensor(rt[:, 3], rt[:, 3], order[:, :].unsqueeze(1).to_broadcast([P, NT, E]), ALU.mult))
                then(dve.tensor_reduce(top[:, 2 + n], rt[:, 3], AX.X, ALU.max))
                then(dve.tensor_tensor(rt[:, n], rt[:, 3], spread(top[:, 2 + n]), ALU.is_equal))

            def running(buf, n, pad, steps):
                for k in range(steps):
                    src, to = buf(k % 2), buf((k + 1) % 2)
                    then(dve.tensor_tensor(to[:, pad:pad + n], src[:, pad:pad + n], src[:, pad - 2 ** k:pad - 2 ** k + n], ALU.add))

            choose(logit, 0)
            then(dve.scalar_tensor_tensor(rt[:, 2], rt[:, 0], -BIG, logit, ALU.mult, ALU.add))
            choose(rt[:, 2], 1)
            then(dve.tensor_tensor(before[:, 0, NTP:NTP + NT], rt[:, 0], rt[:, 1], ALU.add))
            then(dve.tensor_copy(count16[:, 0], before[:, 0, NTP:NTP + NT]))
            running(lambda k: before[:, k], NT, NTP, 4)
            then(dve.tensor_copy(count16[:, 1], before[:, 0, NTP - 1:NTP - 1 + NT]))
            dve.tensor_copy(count16[:, 2, 0], before[:, 0, NTP + NT - 1]).then_inc(cnt_made, 1)
            dve.tensor_copy(xwords[:, :, 1], top[:, 2]).then_inc(word_made, 1)

            def place_pairs():
                dve.wait_ge(rank_mm, 2)
                then(dve.tensor_scalar(est_i[:, 0, :], ps[:, PR[1], NT * E:(NT + 1) * E], 1.0, float(TILE - 1), ALU.max, ALU.add))
                then(dve.tensor_scalar(est_i[:, 1, :], est_i[:, 0, :], TILE.bit_length() - 1, None, ALU.arith_shift_right))
                then(dve.tensor_copy(est[:, 0, E:2 * E], est_i[:, 1, :]))
                running(lambda k: est[:, k], E, E, 3)
                dve.tensor_copy(tile_of[:, 0:E + 1], est[:, 1, E - 1:2 * E]).then_inc(tiles_made, 1)
                then(dve.tensor_scalar(est[:, 4, 0:E], est[:, 1, E - 1:2 * E - 1], float(TILE), None, ALU.mult))
                then(dve.tensor_tensor(rt[:, 4], bank(PR[1], P, NT * E).rearrange("p (i e) -> p i e", e=E),
                                       est[:, 4, 0:E].unsqueeze(1).to_broadcast([P, NT, E]), ALU.add))
                then(dve.tensor_tensor(rt[:, 2:4], rt[:, 0:2], rt[:, 4].unsqueeze(1).to_broadcast([P, 2, NT, E]), ALU.mult))
                then(dve.tensor_reduce(top[:, 4:6], rt[:, 2:4], AX.X, ALU.add))
                dve.tensor_copy(slots[:, :, :], top[:, 4:6]).then_inc(slot_made, 1)
                dve.tensor_copy(top[:, 6:8], top[:, 0:2]).then_inc(dve_ask, 1)

            dve.sem_inc(y_made, 2)
            dve.sem_inc(y_free, Y_FREE)

            def split_hidden(i):
                for g in range(NF // 2):
                    two = slice(2 * g, 2 * g + 2)
                    dve.wait_ge(h_relu, NF * i + 2 * g + 2)
                    dve.tensor_copy(hid[:, HI, two], hid32[:, two]).then_inc(h_hi, 1)
                    dve.wait_ge(h_hi, (NF // 2) * i + g + 1)
                    dve.tensor_tensor(hid[:, LO, two], hid32[:, two], hid[:, HI, two], ALU.subtract).then_inc(h_split, 1)

            def split_high(n, p):
                dve.wait_ge(in_w2, 16 * n + 16)
                dve.tensor_copy(w2[:, p, HI], w2s[:, :, :]).then_inc(w2_hi, 1)

            def shared_tile(i):
                split_hidden(i)
                for a in range(TILE // P):
                    dve.wait_ge(y_mm, 2 * i + a + 1)
                    row = bass.ds(2 * i + a, 1)
                    dve.scalar_tensor_tensor(x_sb[:, row].rearrange("p a d -> p (a d)"), ps[:, 4 + a, 0:D], gates[:, 1:2],
                                             x_sb[:, row].rearrange("p a d -> p (a d)"), ALU.mult, ALU.add).then_inc(y_made, 1)

            then(dve.tensor_scalar(sb2_bc[:, :], sb2_bc[:, :], gates[:, 1:2], None, ALU.mult))
            shared_tile(0)
            place_pairs()
            shared_tile(1)
            split_high(1, 1)
            shared_tile(2)
            dve.wait_ge(y_made, 2 * 3 + 2)
            then(dve.tensor_tensor(x_sb[:, :, :], x_sb[:, :, :], sb2_bc[:, :].unsqueeze(1).to_broadcast([P, NT, D]), ALU.add))
            with dve.Fori(3, ST) as i:
                shared_tile(i)
            dve.wait_ge(act_gave, 4)
            then(dve.tensor_scalar(top[:, 6:8], top[:, 6:8], 1.0, None, ALU.add))
            then(dve.reciprocal(top[:, 6:8], top[:, 6:8]))
            then(dve.tensor_tensor(top[:, 8], top[:, 6], top[:, 7], ALU.add))
            then(dve.tensor_scalar(top[:, 8], top[:, 8], 1e-6, None, ALU.add))
            then(dve.reciprocal(top[:, 9], top[:, 8]))
            then(dve.tensor_scalar(top[:, 9], top[:, 9], gates[:, 1:2], None, ALU.mult))
            then(dve.tensor_tensor(top[:, 6:8], top[:, 6:8], top[:, 9].unsqueeze(1).to_broadcast([P, 2, NT]), ALU.mult))

            dve.wait_ge(z_done, 16 * ZEROS)
            dve.wait_ge(in_b2, 16)

            def take_words(r):
                dve.wait_ge(x_in, 16 * r + 16)
                dve.tensor_copy(words[:, :, :], xin[:, :, 2 * D:RW].bitcast(F32)).then_inc(words_taken, 1)

            take_words(0)
            dve.wait_ge(tiles_made, 1)
            for e in range(E):
                first = dve.value_load(tile_of[0:1, e:e + 1], min_val=e, max_val=RT)
                end = dve.value_load(tile_of[0:1, e + 1:e + 2], min_val=e + 1, max_val=RT)
                if e + 1 < E:
                    split_high(e + 2, e % 2)
                with dve.Fori(first, end) as r:
                    split_hidden(r + ST)
                    dve.wait_ge(words_taken, r + 1)
                    dve.wait_ge(y_free, r + Y_FREE)
                    dve.scalar_tensor_tensor(dest[:, :], words[:, :, 1], float(E - e), words[:, :, 0], ALU.not_equal, ALU.add).then_inc(dest_cmp, 1)
                    dve.wait_ge(dest_cmp, 2 * r + 1)
                    dve.tensor_scalar(dest[:, 1:2], dest[:, 1:2], 2.0, None, ALU.max).then_inc(dest_cmp, 1)
                    take_words(r + 1)
                    for a in range(TILE // P):
                        dve.wait_ge(y_mm, 2 * r + 2 * ST + a + 1)
                        dve.tensor_tensor(y_sb[:, a], ps[:, 4 + a, 0:D], b2_bc[:, e], ALU.add).then_inc(y_made, 1)

            for i in range(NT):
                if i % BACK == 0:
                    dve.wait_ge(back_in[i // BACK], 16)
                then(dve.scalar_tensor_tensor(x_sb[:, i], back[:, i, 0], top[:, 6, i:i + 1], x_sb[:, i], ALU.mult, ALU.add))
                dve.scalar_tensor_tensor(x_sb[:, i], back[:, i, 1], top[:, 7, i:i + 1], x_sb[:, i], ALU.mult, ALU.add).then_inc(mixed, 1)


_INS = ['x', 'ctx_1024', 'fside_BxSxS2_0', 'mask_BxSxS2_ik1', 'g_xattn', 'g_ffn', 'L0_xattn_wq_k', 'L0_xattn_wq_b',
        'L0_xattn_wk_k', 'L0_xattn_wk_b', 'L0_xattn_wv_k', 'L0_xattn_wv_b', 'L0_xattn_wo_k', 'L0_xattn_wo_b',
        'L0_ffn_norm_weight', 'L0_ffn_router_w', 'L0_ffn_sw1', 'L0_ffn_sb1', 'L0_ffn_sw2', 'L0_ffn_sb2',
        'L0_ffn_ew1', 'L0_ffn_eb1', 'L0_ffn_ew2', 'L0_ffn_eb2']
_OUTS = [((B, S, D), 'float32')]


def kernel(**inputs):
    import numpy as _np
    import concourse.bacc as _bacc
    from concourse import mybir as _mybir
    from concourse.bass_utils import run_bass_kernel_spmd as _run

    nc = _bacc.Bacc("TRN2", target_bir_lowering=False, num_devices=1)
    arrays, args = {}, []
    for name in _INS:
        a = _np.ascontiguousarray(inputs[name])
        arrays[f"in_{name}_dram"] = a
        args.append(nc.dram_tensor(f"in_{name}_dram", a.shape, _mybir.dt.from_np(a.dtype), kind="ExternalInput").ap())
    for i, (shape, dtype) in enumerate(_OUTS):
        dt = _mybir.dt.from_np(_np.dtype(dtype))
        args.append(nc.dram_tensor(f"out_{i}_dram", shape, dt, kind="ExternalOutput").ap())
    flamingo_block(nc, *args)
    r = _run(nc, [arrays], core_ids=[0])
    got = tuple(r.results[0][f"out_{i}_dram"] for i in range(len(_OUTS)))
    return got[0]
```
